# Optimizing a Trainium2 kernel written in Bass

```python
import numpy as np
import jax
import jax.numpy as jnp

def _softmax(x, axis=-1):
    return jax.nn.softmax(x, axis=axis)

def _gelu(x):
    return jax.nn.gelu(x, approximate=True)

def _silu(x):
    return jax.nn.silu(x)

def _sigmoid(x):
    return jax.nn.sigmoid(x)

def _layernorm(x, axis=-1, eps=1e-05):
    m = jnp.mean(x, axis=axis, keepdims=True)
    v = jnp.var(x, axis=axis, keepdims=True)
    return (x - m) / jnp.sqrt(v + eps)

def _scatter_add(tgt, idx, src, axis=0):
    return tgt.at[idx].add(src)

def _segment_sum(src, seg, n):
    return jax.ops.segment_sum(src, seg, n)
kernel_name = 'mk_gnn_ffn_d1_gnn_r8_e54905'

def setup_inputs(seed: int=0):
    np.random.seed(seed)
    _w = jnp.asarray

    def _rec_inputs():
        import jax
        import jax.numpy as jnp
        _gk = jax.random.key(seed)
        x = -0.0003019 + 1 * jax.random.normal(jax.random.fold_in(_gk, 1), (1250, 1024), jnp.float32)
        src = jax.random.randint(jax.random.fold_in(_gk, 2), (40000,), 0, 1250, jnp.int32)
        dst = jax.random.randint(jax.random.fold_in(_gk, 3), (40000,), 0, 1250, jnp.int32)
        _o = jnp.argsort(dst, stable=True)
        src = src[_o]
        dst = dst[_o]
        return (x, src, dst)
    x, src, dst = _rec_inputs()

    def _L0_gnn_setup():
        import jax, jax.numpy as jnp
        import numpy as np
        N = 2500
        E = 40000
        D_IN = 1024
        D_OUT = 1024
        key = jax.random.key(seed)
        k1, k2, k3, k4 = jax.random.split(key, 4)
        x = jax.random.normal(k1, (N, D_IN), dtype=jnp.float32)
        edge_index = jax.random.randint(k2, (2, E), 0, N, dtype=jnp.int64)
        W = jax.random.normal(k3, (D_OUT, D_IN), dtype=jnp.float32) * (1.0 / np.sqrt(D_IN))
        b = jax.random.normal(k4, (D_OUT,), dtype=jnp.float32) * 0.01
        return {'x': x, 'edge_index': edge_index, 'W': W, 'b': b}
    _L0_gnn_all = _L0_gnn_setup()
    _L0_gnn_in = {k: v for k, v in _L0_gnn_all.items() if k in ('W', 'b')}
    del _L0_gnn_all

    def _L0_ffn_setup():
        import jax, jax.numpy as jnp
        import numpy as np
        D, H, P, E, K, F = (1024, 16, 64, 8, 2, 512)
        B, S = (2, 256)
        NROT = 32
        BASE = 10000.0
        EPS = 1e-05

        def _ln(x, g, b):
            m = jnp.mean(x, -1, keepdims=True)
            v = jnp.mean(jnp.square(x - m), -1, keepdims=True)
            return (x - m) * jax.lax.rsqrt(v + EPS) * g + b

        def _rope(x):
            xr, xp = (x[..., :NROT], x[..., NROT:])
            half = NROT // 2
            inv = BASE ** (-jnp.arange(half, dtype=jnp.float32) / half)
            ang = jnp.arange(x.shape[2], dtype=jnp.float32)[:, None] * inv[None, :]
            cos, sin = (jnp.cos(ang), jnp.sin(ang))
            x1, x2 = (xr[..., :half], xr[..., half:])
            xr = jnp.concatenate([x1 * cos - x2 * sin, x1 * sin + x2 * cos], -1)
            return jnp.concatenate([xr, xp], -1)

        def _gate(x, Wsel):
            s = jax.nn.sigmoid(jnp.einsum('bsd,hed->bhse', x, Wsel))
            _, idx = jax.lax.top_k(s, K)
            mask = jax.nn.one_hot(idx, E, dtype=s.dtype).sum(-2)
            return s * mask

        def _moe_attn(x, Wq, Wk, Wv, Wo, Wsel_v, Wsel_o):
            q = _rope(jnp.einsum('bsd,hdp->bhsp', x, Wq))
            k = _rope(jnp.einsum('bsd,hdp->bhsp', x, Wk))
            gv = _gate(x, Wsel_v)
            v = jnp.einsum('bsd,bhse,hedp->bhsp', x, gv, Wv)
            att = jax.nn.softmax(jnp.einsum('bhsp,bhtp->bhst', q, k) / np.sqrt(P), axis=-1)
            o = jnp.einsum('bhst,bhtp->bhsp', att, v)
            go = _gate(x, Wsel_o)
            return jnp.einsum('bhsp,bhse,hepd->bsd', o, go, Wo)
        key = jax.random.key(seed)
        ks = jax.random.split(key, 10)
        f = lambda k, sh: jax.random.normal(k, sh, jnp.float32) * 0.02
        return dict(src=jax.random.normal(ks[0], (B, S, D), jnp.float32), Wq=f(ks[1], (H, D, P)), Wk=f(ks[2], (H, D, P)), Wv=f(ks[3], (H, E, D, P)), Wo=f(ks[4], (H, E, P, D)), Wsel_v=f(ks[5], (H, E, D)), Wsel_o=f(ks[6], (H, E, D)), ln1_g=jnp.ones(D, jnp.float32), ln1_b=jnp.zeros(D, jnp.float32), ln2_g=jnp.ones(D, jnp.float32), ln2_b=jnp.zeros(D, jnp.float32), W1=f(ks[7], (D, F)), b1=jnp.zeros(F, jnp.float32), W2=f(ks[8], (F, D)), b2=jnp.zeros(D, jnp.float32))
    _L0_ffn_all = _L0_ffn_setup()
    _L0_ffn_in = {k: v for k, v in _L0_ffn_all.items() if k in ('Wq', 'Wk', 'Wv', 'Wo', 'Wsel_v', 'Wsel_o', 'ln1_g', 'ln1_b', 'ln2_g', 'ln2_b', 'W1', 'b1', 'W2', 'b2')}
    del _L0_ffn_all
    return {'x': x, 'src': src, 'dst': dst, 'L0_gnn_W': _L0_gnn_in['W'], 'L0_gnn_b': _L0_gnn_in['b'], 'L0_ffn_Wq': _L0_ffn_in['Wq'], 'L0_ffn_Wk': _L0_ffn_in['Wk'], 'L0_ffn_Wv': _L0_ffn_in['Wv'], 'L0_ffn_Wo': _L0_ffn_in['Wo'], 'L0_ffn_Wsel_v': _L0_ffn_in['Wsel_v'], 'L0_ffn_Wsel_o': _L0_ffn_in['Wsel_o'], 'L0_ffn_ln1_g': _L0_ffn_in['ln1_g'], 'L0_ffn_ln1_b': _L0_ffn_in['ln1_b'], 'L0_ffn_ln2_g': _L0_ffn_in['ln2_g'], 'L0_ffn_ln2_b': _L0_ffn_in['ln2_b'], 'L0_ffn_W1': _L0_ffn_in['W1'], 'L0_ffn_b1': _L0_ffn_in['b1'], 'L0_ffn_W2': _L0_ffn_in['W2'], 'L0_ffn_b2': _L0_ffn_in['b2']}

def reference(x, src, dst, L0_gnn_W, L0_gnn_b, L0_ffn_Wq, L0_ffn_Wk, L0_ffn_Wv, L0_ffn_Wo, L0_ffn_Wsel_v, L0_ffn_Wsel_o, L0_ffn_ln1_g, L0_ffn_ln1_b, L0_ffn_ln2_g, L0_ffn_ln2_b, L0_ffn_W1, L0_ffn_b1, L0_ffn_W2, L0_ffn_b2):
    import jax
    import jax.numpy as jnp

    def _L0_gnn_ref(x, edge_index, W, b):
        import jax, jax.numpy as jnp
        import numpy as np
        N = 2500
        E = 40000
        D_IN = 1024
        D_OUT = 1024
        num_nodes = x.shape[0]
        self_idx = jnp.arange(num_nodes, dtype=edge_index.dtype)
        ei = jnp.concatenate([edge_index, jnp.stack([self_idx, self_idx], axis=0)], axis=1)
        row, col = (ei[0], ei[1])
        h = jnp.einsum('nd,od->no', x, W) + b
        deg = jnp.zeros((num_nodes,), dtype=h.dtype).at[row].add(1.0)
        deg_inv_sqrt = deg ** (-0.5)
        norm = deg_inv_sqrt[row] * deg_inv_sqrt[col]
        msg = norm[:, None] * h[col]
        out = jax.ops.segment_sum(msg, row, num_segments=num_nodes)
        return out

    def _L0_ffn_ref(src, Wq, Wk, Wv, Wo, Wsel_v, Wsel_o, ln1_g, ln1_b, ln2_g, ln2_b, W1, b1, W2, b2):
        import jax, jax.numpy as jnp
        import numpy as np
        D, H, P, E, K, F = (1024, 16, 64, 8, 2, 512)
        B, S = (2, 256)
        NROT = 32
        BASE = 10000.0
        EPS = 1e-05

        def _ln(x, g, b):
            m = jnp.mean(x, -1, keepdims=True)
            v = jnp.mean(jnp.square(x - m), -1, keepdims=True)
            return (x - m) * jax.lax.rsqrt(v + EPS) * g + b

        def _rope(x):
            xr, xp = (x[..., :NROT], x[..., NROT:])
            half = NROT // 2
            inv = BASE ** (-jnp.arange(half, dtype=jnp.float32) / half)
            ang = jnp.arange(x.shape[2], dtype=jnp.float32)[:, None] * inv[None, :]
            cos, sin = (jnp.cos(ang), jnp.sin(ang))
            x1, x2 = (xr[..., :half], xr[..., half:])
            xr = jnp.concatenate([x1 * cos - x2 * sin, x1 * sin + x2 * cos], -1)
            return jnp.concatenate([xr, xp], -1)

        def _gate(x, Wsel):
            s = jax.nn.sigmoid(jnp.einsum('bsd,hed->bhse', x, Wsel))
            _, idx = jax.lax.top_k(s, K)
            mask = jax.nn.one_hot(idx, E, dtype=s.dtype).sum(-2)
            return s * mask

        def _moe_attn(x, Wq, Wk, Wv, Wo, Wsel_v, Wsel_o):
            q = _rope(jnp.einsum('bsd,hdp->bhsp', x, Wq))
            k = _rope(jnp.einsum('bsd,hdp->bhsp', x, Wk))
            gv = _gate(x, Wsel_v)
            v = jnp.einsum('bsd,bhse,hedp->bhsp', x, gv, Wv)
            att = jax.nn.softmax(jnp.einsum('bhsp,bhtp->bhst', q, k) / np.sqrt(P), axis=-1)
            o = jnp.einsum('bhst,bhtp->bhsp', att, v)
            go = _gate(x, Wsel_o)
            return jnp.einsum('bhsp,bhse,hepd->bsd', o, go, Wo)
        src2 = _moe_attn(src, Wq, Wk, Wv, Wo, Wsel_v, Wsel_o)
        src = src + src2
        src = _ln(src, ln1_g, ln1_b)
        src2 = jax.nn.relu(src @ W1 + b1) @ W2 + b2
        src = src + src2
        return _ln(src, ln2_g, ln2_b)
    edge_index = jnp.stack([src, dst])
    x = x + _L0_gnn_ref(_layernorm(x, axis=-1), edge_index, L0_gnn_W, L0_gnn_b)
    x = x + _L0_ffn_ref(_layernorm(x, axis=-1)[None], L0_ffn_Wq, L0_ffn_Wk, L0_ffn_Wv, L0_ffn_Wo, L0_ffn_Wsel_v, L0_ffn_Wsel_o, L0_ffn_ln1_g, L0_ffn_ln1_b, L0_ffn_ln2_g, L0_ffn_ln2_b, L0_ffn_W1, L0_ffn_b1, L0_ffn_W2, L0_ffn_b2)[0]
    return x

_drawn_inputs = setup_inputs


def setup_inputs(seed=0):
    import zlib

    import numpy as np

    out = dict(_drawn_inputs(seed))
    spreads = {'L0_ffn_ln1_g': (1.0, 0.2),
     'L0_ffn_ln1_b': (0.0, 0.1),
     'L0_ffn_ln2_g': (1.0, 0.2),
     'L0_ffn_ln2_b': (0.0, 0.1),
     'L0_ffn_b1': (0.0, 0.537),
     'L0_ffn_b2': (0.0, 0.1)}
    factors = {'L0_gnn_b': 5.977,
     'L0_ffn_Wq': 8.0,
     'L0_ffn_Wk': 8.0,
     'L0_ffn_Wv': 7.389,
     'L0_ffn_Wo': 7.487,
     'L0_ffn_Wsel_v': 8.0,
     'L0_ffn_Wsel_o': 8.0}
    for name, (base, spread) in spreads.items():
        noise = np.random.default_rng([zlib.crc32(name.encode()), seed]).standard_normal(out[name].shape)
        drawn = base * np.exp(spread * noise) if base else spread * noise
        out[name] = jnp.asarray(drawn.astype(out[name].dtype))
    for name, factor in factors.items():
        out[name] = (out[name] * factor).astype(out[name].dtype)
    return out
```

```python
from contextlib import ExitStack

import concourse.bass as bass
from concourse import mybir

ALU = mybir.AluOpType
ACT = mybir.ActivationFunctionType
AX_X = mybir.AxisListType.X
F32 = mybir.dt.float32
F16 = mybir.dt.float16
I32 = mybir.dt.int32
ds = bass.ds

N = 1250
D = 1024
E_EDGES = 40000
H, P, EX, F = 16, 64, 8, 512
NROT = 32
EPS = 1e-5

T = 125
NT = N // T
PITCH = 128
KD = D // 128
NCH = E_EDGES // T
CPR = 4
SELF = NCH + 8
ECOLS = SELF + NT
HALF = D // 2
GROUPS = ((0, 4), (4, 4), (8, 2))

SX = 64.0
SW = 256.0

SQ = 16.0
SP_ = 1024.0
SM = 512.0
WQKV = (2 + EX) * P
PAIRS = EX // 2
CH = 2
NCK = NT // CH
KU = NT // 2
SPLIT = 3
CHN = CH * T

Q_LO, Q_HI, MAXC, K_LO, K_HI, K_HI2, TOKW = 0, 64, 128, 132, 196, 260, 328

C_ID = 0
C_REV = 128
C_LNP = C_REV + EX
C_KEPT = C_LNP + 1
C_IOTA = 0
C_CHUNK = C_IOTA + NT * PITCH
C_SELF = C_CHUNK + NCH
C_LOW = C_SELF + NT
C_UPPER = C_LOW + 1
C_ID10 = C_UPPER + NT
CCOLS = C_ID10 + NCH // CPR


class Chain:

    def __init__(self, engine, sem):
        self.engine, self.sem, self.base, self.n = engine, sem, 0, 0

    def done(self, instruction):
        instruction.then_inc(self.sem, 1)
        self.n += 1

    def wait(self):
        self.engine.wait_ge(self.sem, self.base + self.n)

    def step(self, instruction):
        self.done(instruction)
        self.wait()

    def enter(self, i, per_round):
        self.saved, self.per_round = (self.base, self.n), per_round
        self.base, self.n = self.base + self.n + i * per_round, 0

    def leave(self, rounds):
        assert self.n == self.per_round, (self.n, self.per_round)
        base, n = self.saved
        self.base, self.n = base, n + rounds * self.per_round


def build(nc, x, src, dst, dst_rows, wg, bg, wsel, wqkv, wo, w1, b1, w2, rowvecs, ctab, gtab, rtab, out):
    ctx = ExitStack()

    def sb(name, shape, dt, where=None):
        return (where or ctx).enter_context(nc.sbuf_tensor(name, shape, dt))

    def sem(name):
        return ctx.enter_context(nc.semaphore(name))

    with ctx:
        ps = ctx.enter_context(nc.psum_tensor("ps", [128, 8, 512], F32))
        goT_dram = nc.dram_tensor("goT_dram", [H * EX, N], F32, kind="Internal").ap()
        x1_dram = nc.dram_tensor("x1_dram", [N, D], F32, kind="Internal").ap()

        consts = sb("consts", [128, C_KEPT], F32)
        xT_hi = sb("xT_hi", [128, KD, NT, PITCH], F16)
        xT_lo = sb("xT_lo", [128, KD, NT, PITCH], F16)
        arena = sb("arena", [128, NT * D], F32)
        stats = sb("stats", [T, 2, 2, 6], F32)
        mv = sb("mv", [T, 2, 2], F32)
        var = sb("var", [T, 2], F32)
        std = sb("std", [T, 2], F32)
        rstd = sb("rstd", [T, 2], F32)
        ident = consts[:, C_ID:C_ID + 128]
        ident16 = sb("ident16", [128, 128], F16)
        acc = arena[0:T, :].rearrange("p (t d) -> p t d", t=NT)
        wg_hi = arena[:, 0:KD * D // 2].bitcast(F16).rearrange("p (k d) -> p k d", k=KD)
        wg_lo = arena[:, KD * D // 2:KD * D].bitcast(F16).rearrange("p (k d) -> p k d", k=KD)
        w_stage = arena[:, KD * D:NT * D].rearrange("p (s d) -> p s d", s=2)

        gnn = ExitStack()
        gconst = sb("gconst", [128, CCOLS], F32, gnn)
        aT_hi = sb("aT_hi", [T, NT, NT, PITCH], F16, gnn)
        aT_lo = sb("aT_lo", [T, NT, NT, PITCH], F16, gnn)
        h_hi = sb("h_hi", [T, NT, D], F16, gnn)
        h_lo = sb("h_lo", [T, NT, D], F16, gnn)
        xb = sb("xb", [T, 2, D], F32, gnn)
        xn = sb("xn", [T, 2, D], F32, gnn)
        bias_g = sb("bias_g", [T, D], F32, gnn)
        edges_i = xn[:, 0, 0:2 * NCH].bitcast(I32).rearrange("p (a c) -> p a c", a=2)
        near = xn[0:NT, 0, 0:2 * NCH].rearrange("p (a c) -> p a c", a=2)
        rows_i = xn[0:NCH // CPR, 1, 0:CPR * T].bitcast(I32).rearrange("p (a c) -> p a c", a=CPR)
        rows = xn[0:NCH // CPR, 1, HALF:HALF + CPR * T].rearrange("p (a c) -> p a c", a=CPR)
        edges = sb("edges", [T, 2, ECOLS], F32, gnn)
        spans = sb("spans", [NCH // CPR, 2, CPR], F32, gnn)
        walk = sb("walk", [NT, 8], F32, gnn)
        walk_i = sb("walk_i", [NT, 1], I32, gnn)
        plan = sb("plan", [1, 3 * NT], I32, gnn)
        deg = sb("deg", [T, NT], F32, gnn)
        dis = sb("dis", [T, 3, NT], F32, gnn)
        iota16 = h_hi[:, 0:2, :].rearrange("p a b -> p (a b)")[:, 0:NT * PITCH]
        hot_src = [h_hi[:, 2 + 2 * s:4 + 2 * s, :].rearrange("p a b -> p (a b)")[:, 0:N] for s in range(4)]
        hot_dst = [h_lo[:, s, 0:PITCH] for s in range(4)]
        ones16 = sb("ones16", [T, 2], F16, gnn)
        gnn.close()

        gv = sb("gv", [T, NT, H * EX], F32)
        rope = sb("rope", [T, NT, 2 * NROT], F32)

        gates = ExitStack()
        wsel_hi = sb("wsel_hi", [128, KD, 2 * H * EX], F16, gates)
        wsel_lo = sb("wsel_lo", [128, KD, 2 * H * EX], F16, gates)
        sig = sb("sig", [T, NT, 2 * H * EX], F32, gates)
        pick_a = sb("pick_a", [T, NT, 2 * H * EX], F32, gates)
        pick_b = sb("pick_b", [T, NT, 2 * H * EX], F32, gates)
        best = sb("best", [T, 2, NT * 2 * H], F32, gates)
        goT = sb("goT", [128, NT, T], F32, gates)
        sel_stage = sb("sel_stage", [128, 2, 2 * H * EX], F32, gates)
        gates.close()

        att = ExitStack()
        wqkv_hi = sb("wqkv_hi", [128, KD, WQKV], F16, att)
        wqkv_lo = sb("wqkv_lo", [128, KD, WQKV], F16, att)
        wo_hi = sb("wo_hi", [128, PAIRS, D], F16, att)
        wo_lo = sb("wo_lo", [128, PAIRS, D], F16, att)
        stage = sb("stage", [128, 2, D], F32, att)
        tok = sb("tok", [T, NT, TOKW], F16, att)
        vt = sb("vt", [T, NT, 2 * P + 2], F16, att)
        qk32 = sb("qk32", [T, 2, 2, P], F32, att)
        rot = sb("rot", [T, 2, 2, NROT], F32, att)
        vprod = sb("vprod", [T, EX, P], F32, att)
        v32 = sb("v32", [T, 2, P], F32, att)
        qkT = sb("qkT", [128, 2, NT, PITCH], F16, att)
        qb = sb("qb", [P + 1, NT, PITCH], F16, att)
        kb = sb("kb", [P + 1, NT, PITCH], F16, att)
        mx = sb("mx", [T, 2], F32, att)
        pT_hi = sb("pT_hi", [T, 2, NT, CH, PITCH], F16, att)
        pT_lo = sb("pT_lo", [T, 2, NT, CH, PITCH], F16, att)
        p32 = sb("p32", [T, 2, 2 * CHN], F32, att)
        go_b = sb("go_b", [128, 2, PAIRS, CHN], F32, att)
        og32 = sb("og32", [128, PAIRS, CHN], F32, att)
        og_hi = sb("og_hi", [128, 2, PAIRS, CH, PITCH], F16, att)
        og_lo = sb("og_lo", [128, 2, PAIRS, CH, PITCH], F16, att)
        rsum = sb("rsum", [T, CH], F32, att)
        o_part = sb("o_part", [T, CH, P], F32, att)
        o32 = sb("o32", [T, CH, 2, P], F32, att)
        att.close()

        mlp = ExitStack()
        w1_hi = sb("w1_hi", [128, KD, F], F16, mlp)
        w1_lo = sb("w1_lo", [128, KD, F], F16, mlp)
        w2_hi = sb("w2_hi", [128, F // 128, D], F16, mlp)
        w2_lo = sb("w2_lo", [128, F // 128, D], F16, mlp)
        mlp_stage = sb("mlp_stage", [128, 2, D], F32, mlp)
        vecs = sb("vecs", [T, 5, D], F32, mlp)
        hT_hi = sb("hT_hi", [128, F // 128, NT, PITCH], F16, mlp)
        hT_lo = sb("hT_lo", [128, F // 128, NT, PITCH], F16, mlp)
        h32 = sb("h32", [128, 2, 4 * T], F32, mlp)
        b1c = sb("b1c", [128, F // 128], F32, mlp)
        fin = sb("fin", [T, 2, D], F32, mlp)
        x1b = sb("x1b", [T, 2, D], F32, mlp)
        mlp.close()

        const_in = sem("const_in")
        edges_in = sem("edges_in")
        bias_in = sem("bias_in")
        x_in = [sem("x_in0"), sem("x_in1")]
        wg_in = [sem("wg_in0"), sem("wg_in1")]
        wg_split = sem("wg_split")
        pool_chain = sem("pool_chain")
        dve_chain = sem("dve_chain")
        pads_ready = sem("pads_ready")
        spans_ready = sem("spans_ready")
        spans_spread = sem("spans_spread")
        walk_ready = sem("walk_ready")
        walk_turned = sem("walk_turned")
        plan_ready = sem("plan_ready")
        var_ready = sem("var_ready")
        std_ready = sem("std_ready")
        xn_ready = sem("xn_ready")
        turned = sem("turned")
        hi_ready = sem("hi_ready")
        lo_ready = sem("lo_ready")
        hot_ready = sem("hot_ready")
        hot_used = [sem(f"hot_used{s}") for s in range(4)]
        a_hi_ready = sem("a_hi_ready")
        a_lo_ready = sem("a_lo_ready")
        deg_ready = sem("deg_ready")
        deg_root = sem("deg_root")
        dis_ready = sem("dis_ready")
        h_ready = sem("h_ready")
        hb_ready = sem("hb_ready")
        h_hi_ready = sem("h_hi_ready")
        h_lo_ready = sem("h_lo_ready")
        agg_ready = sem("agg_ready")
        x1_ready = sem("x1_ready")
        acc_ready = sem("acc_ready")
        x1_out = [sem("x1_out0"), sem("x1_out1")]

        sel_in0 = sem("sel_in0")
        sel_in1 = sem("sel_in1")
        sel_split = sem("sel_split")
        rope_in = sem("rope_in")
        logits_ready = sem("logits_ready")
        exp_ready = sem("exp_ready")
        gates_ready = sem("gates_ready")
        go_turned = sem("go_turned")
        goT_ready = sem("goT_ready")
        goT_out = sem("goT_out")
        w_in0 = sem("w_in0")
        w_in1 = sem("w_in1")
        w_split = sem("w_split")
        split_gate = sem("split_gate")
        att_pads = sem("att_pads")
        proj_ready = sem("proj_ready")
        qk_pass = sem("qk_pass")
        rope_ready = sem("rope_ready")
        v32_ready = sem("v32_ready")
        tok_hi = sem("tok_hi")
        vt_hi = sem("vt_hi")
        tok_ready = sem("tok_ready")
        vt_ready = sem("vt_ready")
        tr_ready = sem("tr_ready")
        qkT_ready = sem("qkT_ready")
        kb_ready = sem("kb_ready")
        smax_ready = sem("smax_ready")
        max_ready = sem("max_ready")
        qm_turned = sem("qm_turned")
        qb_ready = sem("qb_ready")
        st_ready = sem("st_ready")
        exp_done = sem("exp_done")
        plo_ready = sem("plo_ready")
        av_ready = sem("av_ready")
        rs_ready = sem("rs_ready")
        opart_ready = sem("opart_ready")
        o32_ready = sem("o32_ready")
        ot_ready = sem("ot_ready")
        og_ready = sem("og_ready")
        og_hi_ready = sem("og_hi_ready")
        og_pair_ready = sem("og_pair_ready")
        go_in0 = sem("go_in0")
        go_in1 = sem("go_in1")
        o_ready = sem("o_ready")
        acc_added = sem("acc_added")
        mlp_in0 = sem("mlp_in0")
        mlp_in1 = sem("mlp_in1")
        mlp_split = sem("mlp_split")
        vecs_in = sem("vecs_in")
        b1_in = sem("b1_in")
        b1_ready = sem("b1_ready")
        y_ready = sem("y_ready")
        hs_ready = sem("hs_ready")
        h_hi2_ready = sem("h_hi2_ready")
        h_lo2_ready = sem("h_lo2_ready")
        z_ready = sem("z_ready")
        x1_in0 = sem("x1_in0")
        x1_in1 = sem("x1_in1")
        fin_ready = sem("fin_ready")
        fin_out0 = sem("fin_out0")
        fin_out1 = sem("fin_out1")
        w_in, go_in = (w_in0, w_in1), (go_in0, go_in1)
        sel_in, mlp_in, x1_in, fin_out = (sel_in0, sel_in1), (mlp_in0, mlp_in1), (x1_in0, x1_in1), (fin_out0, fin_out1)

        ps16 = ps[:, :, :].rearrange("p a b -> p (a b)").bitcast(F16).rearrange("p (a b) -> p a b", a=8)
        AV, OT = 5, CH * (2 * P + 1)
        QM = 512

        def head_of(w, h):
            return w[ds(h, 1)].rearrange("o p k n -> (o p) k n") if not isinstance(h, int) else w[h]

        def columns(row, a, b, n):
            step = b - a
            return row[:, a:a + 2 * step].rearrange("p (x c) -> p x c", x=2)[:, :, 0:n]

        def p_block(j, u):
            return p32[:, (KU * j + u) % 2, :].rearrange("p (t s c) -> p t s c", t=2, s=CH)

        def hidden():
            return [(first, tiles, f) for first, tiles in GROUPS for f in range(F // 128)]

        def flat(ap):
            return ap.rearrange("p a b -> p (a b)")

        block = ctx.enter_context(nc.Block())

        def tile_rows(dram, t):
            return dram[ds(t * T, T), :]

        def turned_view(par, bank=0):
            both = ps[:, bank + 2 * par:bank + 2 * par + 2, :].rearrange("p a (b c) -> p a b c", b=4)
            return both[:, :, :, 0:T].rearrange("p a b (o c) -> p (a b) o c", o=1)

        @block.sync
        def _(sp):
            sp.dma_start(gconst[:, :], gtab).then_inc(const_in, 16)
            sp.dma_start(consts[:, :], ctab).then_inc(const_in, 16)
            sp.dma_start(rows_i[:, :, :], dst_rows).then_inc(edges_in, 16)
            sp.dma_start(edges_i[:, 0, :], src).then_inc(edges_in, 16)
            sp.dma_start(edges_i[:, 1, :], dst).then_inc(edges_in, 16)
            for t in range(2):
                sp.dma_start(xb[:, t, :], tile_rows(x, t)).then_inc(x_in[t], 16)
            sp.dma_start(bias_g[:, :], bg.partition_broadcast(T)).then_inc(bias_in, 16)
            with sp.Fori(1, NT // 2) as g:
                for par in range(2):
                    sp.wait_ge(turned, 2 * g + par - 1)
                    sp.dma_start(xb[:, par, :], tile_rows(x, 2 * g + par)).then_inc(x_in[par], 16)
            with sp.Fori(0, NT // 2) as g:
                for par in range(2):
                    sp.wait_ge(h_lo_ready, NT)
                    sp.wait_ge(x1_out[par], g * 16)
                    sp.wait_ge(xn_ready, NT + 2 * g)
                    sp.dma_start(xb[:, par, :], tile_rows(x, 2 * g + par)).then_inc(x_in[par], 16)
                for par in range(2):
                    sp.wait_ge(x1_ready, 2 * g + par + 1)
                    sp.dma_start(tile_rows(x1_dram, 2 * g + par), xb[:, par, :]).then_inc(x1_out[par], 16)
            for par in range(2):
                sp.wait_ge(x1_out[par], 16 * (NT // 2))
            n_chunks = KD + PAIRS

            def load_chunk(h, c):
                if c < KD:
                    sp.dma_start(stage[:, c % 2, 0:WQKV], head_of(wqkv, h)[:, c, :]).then_inc(w_in[c % 2], 16)
                else:
                    sp.dma_start(stage[:, c % 2, :], head_of(wo, h)[:, c - KD, :]).then_inc(w_in[c % 2], 16)

            sp.wait_ge(goT_out, 16)
            sp.dma_start(rope[:, :, :], rtab).then_inc(rope_in, 16)
            load_chunk(0, 0)
            load_chunk(0, 1)
            with sp.Fori(0, H - 1) as h:
                for c in range(n_chunks):
                    sp.wait_ge(w_split, SPLIT * n_chunks * h + SPLIT * (c + 1))
                    load_chunk(h + (c + 2) // n_chunks, (c + 2) % n_chunks)
            for c in range(n_chunks - 2):
                sp.wait_ge(w_split, SPLIT * n_chunks * (H - 1) + SPLIT * (c + 1))
                load_chunk(H - 1, c + 2)


            sp.wait_ge(acc_added, 20 * H)
            chunks = [(w1, k, F) for k in range(KD)] + [(w2, k, D) for k in range(F // 128)]
            for c, (w, k, width) in enumerate(chunks):
                if c >= 2:
                    sp.wait_ge(mlp_split, SPLIT * (c - 1))
                sp.dma_start(mlp_stage[:, c % 2, 0:width], w[:, k, :]).then_inc(mlp_in[c % 2], 16)
                if c == 1:
                    sp.dma_start(vecs[:, :, :], rowvecs.partition_broadcast(T)).then_inc(vecs_in, 16)
                    sp.dma_start(b1c[:, :], b1).then_inc(b1_in, 16)
            for t in range(NT):
                if t >= 2:
                    sp.wait_ge(fin_ready, t - 1)
                sp.dma_start(x1b[:, t % 2, :], x1_dram[t * T:(t + 1) * T, :]).then_inc(x1_in[t % 2], 16)
                if t >= 1:
                    sp.wait_ge(fin_ready, t)
                    sp.dma_start(out[(t - 1) * T:t * T, :], fin[:, (t - 1) % 2, :]).then_inc(fin_out[(t - 1) % 2], 16)
            sp.wait_ge(fin_ready, NT)
            sp.dma_start(out[(NT - 1) * T:NT * T, :], fin[:, (NT - 1) % 2, :]).then_inc(fin_out[(NT - 1) % 2], 16)
            for par in range(2):
                sp.wait_ge(fin_out[par], 16 * (NT // 2))

        @block.gpsimd
        def _(pool):
            def split(hi, lo, staged, steps_done, n, gate=None):
                if gate is not None:
                    pool.sem_inc(gate, 1)
                pool.tensor_scalar(staged, staged, SW, 0.0, ALU.mult, ALU.add).then_inc(steps_done, 1)
                pool.wait_ge(steps_done, n + 1)
                if gate is not None:
                    pool.sem_inc(gate, 1)
                pool.tensor_copy(hi, staged).then_inc(steps_done, 1)
                pool.wait_ge(steps_done, n + 2)
                pool.tensor_tensor(lo, staged, hi, ALU.subtract).then_inc(steps_done, 1)

            for buf in (xT_hi, xT_lo):
                pool.memset(buf[:, :, :, T:PITCH], 0.0).then_inc(pads_ready, 1)
            for buf in (aT_hi, aT_lo):
                pool.memset(buf[:, :, :, T:PITCH], 0.0).then_inc(pads_ready, 1)
            pool.memset(ones16[:, :], 1.0).then_inc(pads_ready, 1)
            for k in range(2):
                pool.dma_start(w_stage[:, k, :], wg[:, k, :]).then_inc(wg_in[k], 16)
            for k in range(KD):
                pool.wait_ge(wg_in[k % 2], 16 * (k // 2 + 1))
                split(wg_hi[:, k, :], wg_lo[:, k, :], w_stage[:, k % 2, :], pool_chain, SPLIT * k)
                if k + 2 < KD:
                    pool.wait_ge(pool_chain, SPLIT * (k + 1))
                    pool.dma_start(w_stage[:, k % 2, :], wg[:, k + 2, :]).then_inc(wg_in[k % 2], 16)
            pool.wait_ge(pool_chain, SPLIT * KD)
            pool.sem_inc(wg_split, 1)
            with pool.Fori(0, NT // 2) as g:
                for par in range(2):
                    pool.wait_ge(xn_ready, NT + 2 * g + par + 1)
                    pool.tensor_copy(acc[:, ds(2 * g + par, 1), :].rearrange("p a b -> p (a b)"), xn[:, par, :])\
                        .then_inc(acc_ready, 1)

            pool.wait_ge(lo_ready, 2 * NT)
            for par in range(2):
                pool.wait_ge(x1_out[par], 16 * (NT // 2))
            for k in range(KD):
                if k >= 2:
                    pool.wait_ge(sel_split, SPLIT * (k - 1))
                pool.dma_start(sel_stage[:, k % 2, :], wsel[:, k, :]).then_inc(sel_in[k % 2], 16)
                if k >= 1:
                    pool.wait_ge(sel_in[(k - 1) % 2], 16 * ((k - 1) // 2 + 1))
                    split(wsel_hi[:, k - 1, :], wsel_lo[:, k - 1, :], sel_stage[:, (k - 1) % 2, :], sel_split, SPLIT * (k - 1))
            pool.wait_ge(sel_in[(KD - 1) % 2], 16 * (KD // 2))
            split(wsel_hi[:, KD - 1, :], wsel_lo[:, KD - 1, :], sel_stage[:, (KD - 1) % 2, :], sel_split, SPLIT * (KD - 1))

            pool.wait_ge(goT_out, 16)
            for buf in (qkT[:, :, :, T:PITCH], qb[:, :, T:PITCH], kb[:, :, T:PITCH], og_hi[:, :, :, :, T:PITCH],
                        og_lo[:, :, :, :, T:PITCH], pT_hi[:, :, :, :, T:PITCH], pT_lo[:, :, :, :, T:PITCH]):
                pool.memset(buf, 0.0).then_inc(att_pads, 1)
            pool.wait_ge(att_pads, 7)
            pool.memset(kb[P:P + 1, :, 0:T], SM).then_inc(att_pads, 1)
            pool.wait_ge(att_pads, 8)
            pool.memset(vt[:, :, 2 * P:2 * P + 2], 1.0).then_inc(att_pads, 1)
            pool.memset(tok[:, :, MAXC + 1:K_LO], 0.0).then_inc(att_pads, 1)

            n_chunks = KD + PAIRS
            with pool.Fori(0, H) as h:
                for c in range(n_chunks):
                    if c == 0:
                        pool.wait_ge(proj_ready, NT * h)
                    if c == KD:
                        pool.wait_ge(o_ready, 2 * NT * h)
                    pool.wait_ge(w_in[c % 2], 16 * (n_chunks // 2 * h + c // 2 + 1))
                    if c < KD:
                        split(wqkv_hi[:, c, :], wqkv_lo[:, c, :], stage[:, c % 2, 0:WQKV], w_split, SPLIT * n_chunks * h + SPLIT * c, split_gate)
                    else:
                        split(wo_hi[:, c - KD, :], wo_lo[:, c - KD, :], stage[:, c % 2, :], w_split, SPLIT * n_chunks * h + SPLIT * c, split_gate)

            pool.wait_ge(acc_added, 2 * NT * H)
            for buf in (hT_hi, hT_lo):
                pool.memset(buf[:, :, :, T:PITCH], 0.0).then_inc(att_pads, 1)
            for c in range(KD + F // 128):
                pool.wait_ge(mlp_in[c % 2], 16 * (c // 2 + 1))
                if c < KD:
                    split(w1_hi[:, c, :], w1_lo[:, c, :], mlp_stage[:, c % 2, 0:F], mlp_split, SPLIT * c)
                else:
                    split(w2_hi[:, c - KD, :], w2_lo[:, c - KD, :], mlp_stage[:, c % 2, :], mlp_split, SPLIT * c)

        def stats_of(dve, chain, par, tile, sems):
            for j in range(2):
                chain.done(dve.bn_stats(stats[:, par, j, :], tile[:, j * HALF:(j + 1) * HALF]))
            chain.wait()
            chain.step(dve.bn_aggr(mv[:, par, :], stats[:, par, :, :]))
            dve.tensor_scalar(var[:, par:par + 1], mv[:, par, 1:2], EPS, None, ALU.add).then_inc(sems, 1)

        @block.vector
        def _(dve):
            chain = Chain(dve, dve_chain)
            dve.wait_ge(const_in, 32)
            dve.wait_ge(edges_in, 48)
            dve.tensor_copy(ident16[:, :], ident)
            dve.tensor_copy(iota16, gconst[0:T, C_IOTA:C_IOTA + NT * PITCH])
            dve.memset(edges[:, :, NCH:SELF], -1.0)
            for a in range(2):
                dve.tensor_copy(edges[:, a, 0:NCH], edges_i[:, a, :])
                dve.tensor_copy(edges[:, a, SELF:ECOLS], gconst[0:T, C_SELF:C_SELF + NT])
            chain.step(dve.tensor_copy(rows[:, :, :], rows_i[:, :, :]))
            dve.tensor_reduce(spans[:, 0, :], rows[:, :, :], AX_X, ALU.min)
            dve.tensor_reduce(spans[:, 1, :], rows[:, :, :], AX_X, ALU.max).then_inc(spans_ready, 1)
            dve.wait_ge(spans_spread, 1)
            least = ps[0:NT, 6, 0:NCH]
            greatest = ps[0:NT, 7, 0:NCH]
            low = gconst[0:NT, C_LOW:C_LOW + 1]
            chain.step(dve.tensor_scalar(walk[:, 0:1], low, float(T - 1), None, ALU.add))
            chain.step(dve.tensor_scalar(near[:, 0, :], least, walk[:, 0:1], None, ALU.is_le))
            chain.step(dve.scalar_tensor_tensor(near[:, 0, :], greatest, low, near[:, 0, :], ALU.is_ge, ALU.mult))
            number = gconst[0:NT, C_CHUNK:C_CHUNK + NCH]
            chain.step(dve.scalar_tensor_tensor(near[:, 1, :], near[:, 0, :], -1000.0, number, ALU.mult, ALU.add))
            chain.step(dve.tensor_reduce(walk[:, 1:2], near[:, 1, :], AX_X, ALU.min))
            chain.step(dve.tensor_scalar(walk[:, 2:3], walk[:, 1:2], 1000.0, float(NCH - 1), ALU.add, ALU.min))
            chain.step(dve.scalar_tensor_tensor(near[:, 1, :], number, 1.0, near[:, 0, :], ALU.add, ALU.mult))
            chain.step(dve.tensor_reduce(walk[:, 3:4], near[:, 1, :], AX_X, ALU.max))
            chain.step(dve.scalar_tensor_tensor(walk[:, 4:5], walk[:, 3:4], 4.0, walk[:, 2:3], ALU.add, ALU.subtract))
            chain.step(dve.tensor_scalar(walk[:, 5:6], walk[:, 4:5], 8.0, None, ALU.max))
            chain.step(dve.tensor_copy(walk_i[:, :], walk[:, 5:6]))
            chain.step(dve.tensor_scalar(walk_i[:, :], walk_i[:, :], 2, None, ALU.logical_shift_right))
            dve.tensor_copy(walk[:, 6:7], walk_i[:, :]).then_inc(walk_ready, 1)
            dve.wait_ge(walk_turned, 1)
            dve.tensor_copy(plan[:, :], ps[0:1, 5, 0:3 * NT]).then_inc(plan_ready, 1)

            for g in range(NT // 2):
                for par in range(2):
                    dve.wait_ge(x_in[par], 16 * g + 16)
                    stats_of(dve, chain, par, xb[:, par, :], var_ready)
                for par in range(2):
                    dve.wait_ge(std_ready, 2 * g + par + 1)
                    chain.step(dve.reciprocal(rstd[:, par:par + 1], std[:, par:par + 1]))
                    dve.tensor_scalar(xb[:, par, :], xb[:, par, :], mv[:, par, 0:1], rstd[:, par:par + 1],
                                      ALU.subtract, ALU.mult).then_inc(xn_ready, 1)
                for par in range(2):
                    t = 2 * g + par
                    dve.wait_ge(hi_ready, t + 1)
                    dve.scalar_tensor_tensor(xT_lo[:, :, ds(t, 1), 0:T], turned_view(par), SX,
                                             xT_hi[:, :, ds(t, 1), 0:T], ALU.mult, ALU.subtract)\
                        .then_inc(lo_ready, 1)

            dve.wait_ge(plan_ready, 1)

            def one_hot(s, column, b):
                dve.tensor_scalar(hot_src[s], iota16[:, 0:N], edges[:, 0, ds(column, 1)], None, ALU.is_equal)
                dve.tensor_scalar(hot_dst[s], iota16[:, ds(b * T, PITCH)], edges[:, 1, ds(column, 1)], None,
                                  ALU.is_equal).then_inc(hot_ready, 1)

            def a_low(b, par):
                dve.wait_ge(a_hi_ready, b + 1)
                for first, n in GROUPS:
                    into = aT_lo[:, ds(b, 1), first:first + n, 0:T]
                    sums = ps[0:T, 3 * par + first // 4, 0:n * T].rearrange("p (a b c) -> p a b c", a=1, b=n)
                    last = dve.tensor_tensor(into, sums, aT_hi[:, ds(b, 1), first:first + n, 0:T], ALU.subtract)
                last.then_inc(a_lo_ready, 1)

            with dve.Fori(0, NT // 2) as g:
                for par in range(2):
                    b = 2 * g + par
                    first = dve.value_load(plan[0:1, ds(b, 1)], min_val=0, max_val=NCH - 1)
                    rounds = dve.value_load(plan[0:1, ds(NT + b, 1)], min_val=2, max_val=NCH // 4 + 1)
                    before = dve.value_load(plan[0:1, ds(2 * NT + b, 1)], min_val=0, max_val=NT * (NCH // 4 + 1))
                    for s in range(4):
                        dve.wait_ge(hot_used[s], before)
                        one_hot(s, first + (s - 1) if s else b + SELF, b)
                    with dve.Fori(1, rounds) as i:
                        for s in range(4):
                            column = nc.s_assert_within(
                                first + 4 * i + (s - 1), 0, SELF - 1,
                                skip_runtime_bounds_check_because="rounds ends at most 3 chunks after the last")
                            dve.wait_ge(hot_used[s], before + i)
                            one_hot(s, column, b)
                    a_low(b, par)

            dve.wait_ge(deg_root, 1)
            chain.step(dve.reciprocal(dis[:, 0, :], deg[:, :]))
            dve.tensor_scalar(dis[:, 1, :], dis[:, 0, :], SX, None, ALU.mult)
            chain.step(dve.tensor_scalar(dis[:, 2, :], dis[:, 0, :], 1.0 / SX, None, ALU.mult))
            dve.sem_inc(dis_ready, 1)

            dve.wait_ge(bias_in, 16)
            with dve.Fori(0, NT // 2) as g:
                for par in range(2):
                    t = 2 * g + par
                    dve.wait_ge(h_ready, t + 1)
                    dve.wait_ge(h_lo_ready, 2 * g)
                    dve.scalar_tensor_tensor(xb[:, par, :], ps[0:T, 2 * par:2 * par + 2, :].rearrange("p a b -> p (a b)"),
                                             1.0 / (SX * SW), bias_g[:, :], ALU.mult, ALU.add).then_inc(hb_ready, 1)
                for par in range(2):
                    t = 2 * g + par
                    dve.wait_ge(h_hi_ready, t + 1)
                    dve.scalar_tensor_tensor(h_lo[:, ds(t, 1), :].rearrange("p a b -> p (a b)"), xb[:, par, :],
                                             dis[:, 1, ds(t, 1)], h_hi[:, ds(t, 1), :].rearrange("p a b -> p (a b)"),
                                             ALU.mult, ALU.subtract).then_inc(h_lo_ready, 1)

            for g in range(NT // 2):
                for par in range(2):
                    t = 2 * g + par
                    dve.wait_ge(x_in[par], 16 * (NT // 2) + 16 * g + 16)
                    dve.wait_ge(agg_ready, t + 1)
                    dve.scalar_tensor_tensor(
                        xb[:, par, :], ps[0:T, 2 * par:2 * par + 2, :].rearrange("p a b -> p (a b)"),
                        dis[:, 2, ds(t, 1)], xb[:, par, :], ALU.mult, ALU.add).then_inc(x1_ready, 1)
                    dve.wait_ge(x1_ready, t + 1)
                    stats_of(dve, chain, par, xb[:, par, :], var_ready)
                for par in range(2):
                    t = 2 * g + par
                    dve.wait_ge(std_ready, NT + t + 1)
                    chain.step(dve.reciprocal(rstd[:, par:par + 1], std[:, par:par + 1]))
                    dve.wait_ge(turned, NT + 2 * g)
                    dve.wait_ge(acc_ready, 2 * g)
                    dve.tensor_scalar(xn[:, par, :], xb[:, par, :], mv[:, par, 0:1], rstd[:, par:par + 1],
                                      ALU.subtract, ALU.mult).then_inc(xn_ready, 1)
                for par in range(2):
                    t = 2 * g + par
                    dve.wait_ge(hi_ready, NT + t + 1)
                    dve.scalar_tensor_tensor(xT_lo[:, :, ds(t, 1), 0:T], turned_view(par, 4), SX,
                                             xT_hi[:, :, ds(t, 1), 0:T], ALU.mult, ALU.subtract)\
                        .then_inc(lo_ready, 1)

            groups = NT * 2 * H
            sig8, a8, b8 = (buf[:, :, :].rearrange("p t (g e) -> p (t g) e", e=EX) for buf in (sig, pick_a, pick_b))
            rev8 = consts[0:T, C_REV:C_REV + EX].unsqueeze(1).to_broadcast([T, groups, EX])

            def spread(j):
                return best[:, j, :].unsqueeze(2).to_broadcast([T, groups, EX])

            dve.wait_ge(exp_ready, NT)
            chain.step(dve.tensor_scalar(sig[:, :, :], sig[:, :, :], 1.0, None, ALU.add))
            chain.step(dve.reciprocal(sig[:, :, :], sig[:, :, :]))

            def choose(values, into, other):
                chain.step(dve.tensor_reduce(best[:, 0, :], values, AX_X, ALU.max))
                chain.step(dve.tensor_tensor(other, values, spread(0), ALU.is_equal))
                chain.step(dve.tensor_tensor(other, other, rev8, ALU.mult))
                chain.step(dve.tensor_reduce(best[:, 1, :], other, AX_X, ALU.max))
                chain.step(dve.tensor_tensor(into, other, spread(1), ALU.is_equal))

            choose(sig8, a8, b8)
            chain.step(dve.scalar_tensor_tensor(b8, a8, -4.0, sig8, ALU.mult, ALU.add))
            chain.step(dve.tensor_reduce(best[:, 0, :], b8, AX_X, ALU.max))
            chain.step(dve.tensor_tensor(b8, b8, spread(0), ALU.is_equal))
            chain.step(dve.tensor_tensor(b8, b8, rev8, ALU.mult))
            chain.step(dve.tensor_reduce(best[:, 1, :], b8, AX_X, ALU.max))
            chain.step(dve.tensor_tensor(b8, b8, spread(1), ALU.is_equal))
            chain.step(dve.tensor_tensor(a8, a8, b8, ALU.add))
            chain.step(dve.tensor_tensor(sig8, sig8, a8, ALU.mult))
            dve.tensor_copy(gv[:, :, :], sig[:, :, 0:H * EX]).then_inc(gates_ready, 1)
            for first, n in GROUPS:
                dve.wait_ge(go_turned, NT)
                last = dve.tensor_copy(goT[:, first:first + n, :],
                                       ps[:, 4 + first // 4, 0:n * T].rearrange("p (a b) -> p a b", a=n))
            last.then_inc(goT_ready, 1)

            for par in range(2):
                dve.wait_ge(x1_out[par], 16 * (NT // 2))
            dve.wait_ge(rope_in, 16)
            dve.wait_ge(goT_out, 16)
            with dve.Fori(0, H) as h:
                def first_half(i):
                    par = i % 2
                    qk = qk32[:, par, :, :]
                    half = NROT // 2

                    def table(first, n):
                        return rope[:, i:i + 1, first:first + n].to_broadcast([T, 2, n])

                    dve.wait_ge(qk_pass, NT * h + i + 1)
                    if i:
                        dve.wait_ge(rope_ready, NT * h + i)
                    dve.tensor_tensor(rot[:, 0, :, :], qk[:, :, 0:NROT], table(0, NROT), ALU.mult)
                    dve.tensor_tensor(rot[:, 1, :, 0:half], qk[:, :, half:NROT], table(NROT, half), ALU.mult)
                    chain.step(dve.tensor_tensor(rot[:, 1, :, half:NROT], qk[:, :, 0:half], table(NROT + half, half),
                                                 ALU.mult))
                    dve.tensor_tensor(qk32[:, par, :, 0:NROT], rot[:, 0, :, :], rot[:, 1, :, :], ALU.add)\
                        .then_inc(rope_ready, 1)
                    gate = gv[:, i:i + 1, ds(EX * h, EX)].rearrange("p o e -> p (o e)").unsqueeze(2)
                    chain.step(dve.tensor_tensor(vprod[:, :, :], ps[0:T, par, :].rearrange("p (e c) -> p e c", e=EX),
                                                 gate.to_broadcast([T, EX, P]), ALU.mult))
                    dve.tensor_reduce(v32[:, par, :], vprod[:, :, :].rearrange("p e c -> p c e"), AX_X, ALU.add)\
                        .then_inc(v32_ready, 1)

                def second_half(i):
                    par = i % 2
                    dve.wait_ge(tok_hi, NT * h + i + 1)
                    dve.tensor_tensor(columns(tok[:, i, :], Q_LO, K_LO, P), qk32[:, par, :, :],
                                      columns(tok[:, i, :], Q_HI, K_HI, P), ALU.subtract).then_inc(tok_ready, 1)
                    dve.wait_ge(vt_hi, NT * h + i + 1)
                    dve.scalar_tensor_tensor(vt[:, i, P:2 * P], v32[:, par, :], SQ / (SX * SW), vt[:, i, 0:P],
                                             ALU.mult, ALU.subtract).then_inc(vt_ready, 1)

                def take_kb(i):
                    dve.wait_ge(qkT_ready, NT * h + i + 1)
                    dve.tensor_copy(kb[0:P, i, 0:T], ps16[0:P, 4 + i % 2, 2 * PITCH:2 * PITCH + T]).then_inc(kb_ready, 1)

                def row_max(i):
                    dve.wait_ge(smax_ready, NT * h + i + 1)
                    chain.done(dve.tensor_reduce(mx[:, 0:1], ps[0:T, 0:2, 0:4 * T], mybir.AxisListType.XY, ALU.max))
                    chain.step(dve.tensor_reduce(mx[:, 1:2], ps[0:T, 2, 0:2 * T], AX_X, ALU.max))
                    dve.tensor_scalar(tok[:, i, MAXC:MAXC + 1], mx[:, 0:1], mx[:, 1:2], -1.0 / SM, ALU.max, ALU.mult)\
                        .then_inc(max_ready, 1)

                def p_low(j, u):
                    dve.wait_ge(exp_done, KU * NCK * h + KU * j + u + 1)
                    dve.tensor_tensor(pT_lo[:, j % 2, 2 * u:2 * u + 2, :, 0:T], p_block(j, u),
                                      pT_hi[:, j % 2, 2 * u:2 * u + 2, :, 0:T], ALU.subtract).then_inc(plo_ready, 1)

                def sums(j):
                    values = ps[0:T, AV, 0:OT].rearrange("p (s c) -> p s c", s=CH)
                    dve.wait_ge(av_ready, NCK * h + j + 1)
                    dve.reciprocal(rsum[:, :], values[:, :, 2 * P:2 * P + 1].rearrange("p s o -> p (s o)"))\
                        .then_inc(rs_ready, 1)
                    dve.wait_ge(opart_ready, NCK * h + j + 1)
                    for a in range(CH):
                        chain.done(dve.scalar_tensor_tensor(o32[:, a, 0, :], values[:, a, P:2 * P], rsum[:, a:a + 1],
                                                            o_part[:, a, :], ALU.mult, ALU.add))
                    chain.wait()
                    dve.tensor_copy(o32[:, :, 1, :], o32[:, :, 0, :]).then_inc(o32_ready, 1)

                def gated(j):
                    dve.wait_ge(ot_ready, NCK * h + j + 1)
                    dve.wait_ge(go_in[j % 2], 32 * (((NCK + 1 - j % 2) // 2) * h + j // 2 + 1))
                    oT = ps[:, AV, OT:OT + CHN].unsqueeze(1).to_broadcast([128, PAIRS, CHN])
                    dve.tensor_tensor(og32[:, :, :], go_b[:, j % 2, :, :], oT, ALU.mult).then_inc(og_ready, 1)
                    dve.wait_ge(og_hi_ready, NCK * h + j + 1)
                    dve.tensor_tensor(og_lo[:, j % 2, :, :, 0:T], og32[:, :, :].rearrange("p a (s c) -> p a s c", s=CH),
                                      og_hi[:, j % 2, :, :, 0:T], ALU.subtract).then_inc(og_pair_ready, 1)

                def add_out(j, a, half):
                    n = 4 * j + 2 * a + half
                    dve.wait_ge(o_ready, 2 * NT * h + n + 1)
                    into = acc[:, CH * j + a, half * HALF:(half + 1) * HALF]
                    dve.scalar_tensor_tensor(into, ps[0:T, 6 + half, :], 1.0 / (SQ * SW), into, ALU.mult, ALU.add)\
                        .then_inc(acc_added, 1)

                chain.enter(h, NT * 2 + NT * 2 + NCK * 2)
                for i in range(NT + 2):
                    if i < NT:
                        first_half(i)
                    if 1 <= i <= NT:
                        second_half(i - 1)
                    if i >= 2:
                        take_kb(i - 2)
                for a in range(CH):
                    row_max(a)
                for j in range(NCK + 2):
                    if j < NCK:
                        for u in range(KU):
                            p_low(j, u)
                    if j + 1 < NCK:
                        row_max(CH * (j + 1))
                    if 1 <= j <= NCK:
                        sums(j - 1)
                    if j + 1 < NCK:
                        row_max(CH * (j + 1) + 1)
                    if j >= 2:
                        add_out(j - 2, 0, 0)
                        add_out(j - 2, 0, 1)
                    if 1 <= j <= NCK:
                        gated(j - 1)
                    if j >= 2:
                        add_out(j - 2, 1, 0)
                        add_out(j - 2, 1, 1)
            chain.leave(H)

            def normed(t, tile, count, gain, shift):
                par = t % 2
                dve.wait_ge(std_ready, count + t + 1)
                chain.step(dve.reciprocal(rstd[:, par:par + 1], std[:, par:par + 1]))
                chain.step(dve.tensor_scalar(tile, tile, mv[:, par, 0:1], rstd[:, par:par + 1], ALU.subtract, ALU.mult))
                chain.step(dve.tensor_tensor(tile, tile, vecs[:, gain, :], ALU.mult))
                return dve.tensor_tensor(tile, tile, vecs[:, shift, :], ALU.add)

            dve.wait_ge(acc_added, 2 * NT * H)
            dve.wait_ge(vecs_in, 16)
            dve.wait_ge(b1_in, 16)
            dve.tensor_scalar(b1c[:, :], b1c[:, :], SQ, None, ALU.mult).then_inc(b1_ready, 1)
            for g in range(NT // 2):
                for par in range(2):
                    stats_of(dve, chain, par, acc[:, 2 * g + par, :], var_ready)
                for par in range(2):
                    t = 2 * g + par
                    normed(t, acc[:, t, :], 2 * NT, 0, 1).then_inc(y_ready, 1)
                for par in range(2):
                    t = 2 * g + par
                    dve.wait_ge(hi_ready, 2 * NT + t + 1)
                    dve.scalar_tensor_tensor(xT_lo[:, :, t:t + 1, 0:T], turned_view(par), SX,
                                             xT_hi[:, :, t:t + 1, 0:T], ALU.mult, ALU.subtract).then_inc(lo_ready, 1)
            for n, (first, tiles, f) in enumerate(hidden()):
                dve.wait_ge(h_hi2_ready, n + 1)
                dve.tensor_tensor(hT_lo[:, f, first:first + tiles, 0:T],
                                  h32[:, n % 2, 0:tiles * T].rearrange("p (a b) -> p a b", a=tiles),
                                  hT_hi[:, f, first:first + tiles, 0:T], ALU.subtract).then_inc(h_lo2_ready, 1)
            for g in range(NT // 2):
                for par in range(2):
                    t = 2 * g + par
                    dve.wait_ge(z_ready, t + 1)
                    if g:
                        dve.wait_ge(fin_out[par], 16 * g)
                    chain.step(dve.scalar_tensor_tensor(fin[:, par, :], flat(ps[0:T, 4 + 2 * par:6 + 2 * par, :]),
                                                        1.0 / (SQ * SW), acc[:, t, :], ALU.mult, ALU.add))
                    chain.step(dve.tensor_tensor(fin[:, par, :], fin[:, par, :], vecs[:, 2, :], ALU.add))
                    stats_of(dve, chain, par, fin[:, par, :], var_ready)
                for par in range(2):
                    t = 2 * g + par
                    chain.step(normed(t, fin[:, par, :], 3 * NT, 3, 4))
                    dve.wait_ge(x1_in[par], 16 * (g + 1))
                    dve.tensor_tensor(fin[:, par, :], fin[:, par, :], x1b[:, par, :], ALU.add).then_inc(fin_ready, 1)

        @block.scalar
        def _(act):
            with act.Fori(0, NT // 2) as g:
                for par in range(2):
                    act.wait_ge(var_ready, 2 * g + par + 1)
                    act.activation(std[:, par:par + 1], var[:, par:par + 1], ACT.Sqrt).then_inc(std_ready, 1)
                for par in range(2):
                    t = 2 * g + par
                    act.wait_ge(turned, t + 1)
                    act.activation(xT_hi[:, :, ds(t, 1), 0:T], turned_view(par), ACT.Copy, scale=SX)\
                        .then_inc(hi_ready, 1)
            act.wait_ge(plan_ready, 1)
            with act.Fori(0, NT // 2) as g:
                for par in range(2):
                    b = 2 * g + par
                    rounds = act.value_load(plan[0:1, ds(NT + b, 1)], min_val=2, max_val=NCH // 4 + 1)
                    before = act.value_load(plan[0:1, ds(2 * NT + b, 1)], min_val=0, max_val=NT * (NCH // 4 + 1))
                    act.wait_ge(hot_used[3], before + rounds)
                    for first, n in GROUPS:
                        sums = ps[0:T, 3 * par + first // 4, 0:n * T].rearrange("p (a b c) -> p a b c", a=1, b=n)
                        last = act.activation(aT_hi[:, ds(b, 1), first:first + n, 0:T], sums, ACT.Copy)
                    last.then_inc(a_hi_ready, 1)
            act.wait_ge(deg_ready, 1)
            act.activation(deg[:, :], ps[0:T, 6, 0:NT], ACT.Sqrt).then_inc(deg_root, 1)
            act.wait_ge(dis_ready, 1)
            with act.Fori(0, NT // 2) as g:
                for par in range(2):
                    t = 2 * g + par
                    act.wait_ge(hb_ready, t + 1)
                    act.activation(h_hi[:, ds(t, 1), :].rearrange("p a b -> p (a b)"), xb[:, par, :], ACT.Copy,
                                   scale=dis[:, 1, ds(t, 1)]).then_inc(h_hi_ready, 1)
            with act.Fori(0, NT // 2) as g:
                for par in range(2):
                    act.wait_ge(var_ready, NT + 2 * g + par + 1)
                    act.activation(std[:, par:par + 1], var[:, par:par + 1], ACT.Sqrt).then_inc(std_ready, 1)
                for par in range(2):
                    t = 2 * g + par
                    act.wait_ge(turned, NT + t + 1)
                    act.activation(xT_hi[:, :, ds(t, 1), 0:T], turned_view(par, 4), ACT.Copy, scale=SX)\
                        .then_inc(hi_ready, 1)

            with act.Fori(0, NT // 2) as g:
                for par in range(2):
                    t = 2 * g + par
                    act.wait_ge(logits_ready, t + 1)
                    act.activation(flat(sig[:, ds(t, 1), :]), ps[0:T, par, 0:2 * H * EX], ACT.Exp, scale=-1.0 / (SX * SW))\
                        .then_inc(exp_ready, 1)
            act.wait_ge(goT_ready, 1)
            for par in range(2):
                act.wait_ge(x1_out[par], 16 * (NT // 2))
            act.dma_start(goT_dram, flat(goT[:, :, :])).then_inc(goT_out, 16)
            act.wait_ge(goT_out, 16)

            with act.Fori(0, H) as h:
                def load_gates(j):
                    for e in range(2):
                        rows = goT_dram[ds(EX * h, EX), CHN * j:CHN * (j + 1)].rearrange("(k e) n -> e k n", e=2)[e]
                        act.dma_start(go_b[P * e:P * (e + 1), j % 2, :, :], rows.partition_broadcast(P))\
                            .then_inc(go_in[j % 2], 16)

                act.wait_ge(og_ready, NCK * h)
                load_gates(0)
                load_gates(1)

                def take_qk(i):
                    par = i % 2
                    qk = ps[0:T, 2 + par, 0:2 * P].rearrange("p (a c) -> p a c", a=2)
                    act.wait_ge(proj_ready, NT * h + i + 1)
                    act.wait_ge(tok_ready, NT * h + max(i - 1, 0))
                    act.activation(qk32[:, par, :, :], qk, ACT.Copy, scale=SQ / (SX * SW))\
                        .then_inc(qk_pass, 1)

                def high_halves(i):
                    par = i % 2
                    act.wait_ge(rope_ready, NT * h + i + 1)
                    act.wait_ge(qm_turned, NCK * h)
                    act.activation(columns(tok[:, i, :], Q_HI, K_HI, P), qk32[:, par, :, :], ACT.Copy)
                    act.activation(tok[:, i, K_HI2:K_HI2 + P], qk32[:, par, 1, :], ACT.Copy).then_inc(tok_hi, 1)
                    act.wait_ge(v32_ready, NT * h + i + 1)
                    act.wait_ge(av_ready, NCK * h)
                    act.activation(vt[:, i, 0:P], v32[:, par, :], ACT.Copy, scale=SQ / (SX * SW)).then_inc(vt_hi, 1)

                def take_qkT(i):
                    act.wait_ge(tr_ready, NT * h + i + 1)
                    act.activation(qkT[:, :, i, 0:T], ps16[:, 4 + i % 2, 0:2 * PITCH]
                                   .rearrange("p (a c) -> p a c", a=2)[:, :, 0:T], ACT.Copy).then_inc(qkT_ready, 1)

                def exps(j, u):
                    n = KU * j + u
                    act.wait_ge(st_ready, KU * NCK * h + n + 1)
                    act.wait_ge(plo_ready, KU * NCK * h + max(n - 1, 0))
                    if u == 0:
                        act.wait_ge(av_ready, NCK * h + max(j - 1, 0))
                    scores = ps[0:T, 3 + n % 2, 0:2 * CHN]
                    act.activation(p32[:, n % 2, :], scores, ACT.Exp, bias=consts[0:T, C_LNP:C_LNP + 1],
                                   scale=1.0 / (SQ * SQ * P ** 0.5))
                    act.activation(pT_hi[:, j % 2, 2 * u:2 * u + 2, :, 0:T],
                                   scores.rearrange("p (t s c) -> p t s c", t=2, s=CH), ACT.Exp,
                                   bias=consts[0:T, C_LNP:C_LNP + 1], scale=1.0 / (SQ * SQ * P ** 0.5))\
                        .then_inc(exp_done, 1)

                for i in range(NT + 2):
                    if i < NT:
                        take_qk(i)
                    if 1 <= i <= NT:
                        high_halves(i - 1)
                    if i >= 2:
                        take_qkT(i - 2)
                for j in range(NCK + 1):
                    if j < NCK:
                        act.wait_ge(qm_turned, NCK * h + j + 1)
                        act.activation(qb[:, CH * j:CH * (j + 1), 0:T], ps16[0:P + 1, 2, QM:QM + CH * PITCH]
                                       .rearrange("p (a c) -> p a c", a=CH)[:, :, 0:T], ACT.Copy).then_inc(qb_ready, 1)
                        for u in range(KU):
                            exps(j, u)
                    if j >= 1:
                        values = ps[0:T, AV, 0:OT].rearrange("p (s c) -> p s c", s=CH)
                        act.wait_ge(rs_ready, NCK * h + j)
                        for a in range(CH):
                            last = act.activation(o_part[:, a, :], values[:, a, 0:P], ACT.Copy, scale=rsum[:, a:a + 1])
                        last.then_inc(opart_ready, 1)
                        act.wait_ge(og_ready, NCK * h + j)
                        act.wait_ge(o_ready, 2 * NT * h + 4 * max(j - 2, 0))
                        act.activation(og_hi[:, (j - 1) % 2, :, :, 0:T], og32[:, :, :]
                                       .rearrange("p a (s c) -> p a s c", s=CH), ACT.Copy).then_inc(og_hi_ready, 1)
                        if j + 1 < NCK:
                            load_gates(j + 1)

            for g in range(NT // 2):
                for par in range(2):
                    act.wait_ge(var_ready, 2 * NT + 2 * g + par + 1)
                    act.activation(std[:, par:par + 1], var[:, par:par + 1], ACT.Sqrt).then_inc(std_ready, 1)
                for par in range(2):
                    t = 2 * g + par
                    act.wait_ge(turned, 2 * NT + t + 1)
                    act.activation(xT_hi[:, :, t:t + 1, 0:T], turned_view(par), ACT.Copy, scale=SX).then_inc(hi_ready, 1)
            act.wait_ge(b1_ready, 1)
            for n, (first, tiles, f) in enumerate(hidden()):
                act.wait_ge(hs_ready, n + 1)
                if n >= 2:
                    act.wait_ge(h_lo2_ready, n - 1)
                product = ps[:, 4 + n % 4, 0:tiles * T]
                act.activation(h32[:, n % 2, 0:tiles * T], product, ACT.Relu, bias=b1c[:, f:f + 1],
                               scale=SQ / (SX * SW))
                act.activation(hT_hi[:, f, first:first + tiles, 0:T], product.rearrange("p (a b) -> p a b", a=tiles),
                               ACT.Relu, bias=b1c[:, f:f + 1], scale=SQ / (SX * SW)).then_inc(h_hi2_ready, 1)
            for t in range(NT):
                act.wait_ge(var_ready, 3 * NT + t + 1)
                act.activation(std[:, t % 2:t % 2 + 1], var[:, t % 2:t % 2 + 1], ACT.Sqrt).then_inc(std_ready, 1)

        @block.tensor
        def _(pe):
            pe.wait_ge(const_in, 32)
            pe.wait_ge(spans_ready, 1)
            n_rows = NCH // CPR
            for a in range(2):
                for j in range(CPR):
                    last = pe.matmul(ps[0:NT, 6 + a, j * n_rows:(j + 1) * n_rows],
                                     spans[:, a, j:j + 1].to_broadcast([n_rows, NT]),
                                     gconst[0:n_rows, C_ID10:C_ID10 + n_rows], start=True, stop=True)
            last.then_inc(spans_spread, 1)
            pe.wait_ge(walk_ready, 1)
            pe.matmul(ps[0:1, 5, 0:NT], walk[:, 2:3], gconst[0:NT, C_ID10:C_ID10 + NT], start=True, stop=True)
            pe.matmul(ps[0:1, 5, NT:2 * NT], walk[:, 6:7], gconst[0:NT, C_ID10:C_ID10 + NT], start=True, stop=True)
            pe.matmul(ps[0:1, 5, 2 * NT:3 * NT], walk[:, 6:7], gconst[0:NT, C_UPPER:C_UPPER + NT],
                      start=True, stop=True).then_inc(walk_turned, 1)

            with pe.Fori(0, NT // 2) as g:
                for par in range(2):
                    t = 2 * g + par
                    pe.wait_ge(xn_ready, t + 1)
                    pe.wait_ge(lo_ready, 2 * g)
                    for k in range(KD):
                        last = pe.transpose(ps[:, 2 * par + k // 4, (k % 4) * PITCH:(k % 4) * PITCH + T],
                                            xb[:, par, k * 128:(k + 1) * 128], ident[0:T, 0:T])
                    last.then_inc(turned, 1)

            pe.wait_ge(lo_ready, NT)
            pe.wait_ge(plan_ready, 1)

            def count(s, par, start, stop):
                for first, n in GROUPS:
                    last = pe.matmul(ps[:, 3 * par + first // 4, 0:n * T], hot_dst[s],
                                     hot_src[s][:, first * T:(first + n) * T], start=start, stop=stop,
                                     skip_group_check=True)
                last.then_inc(hot_used[s], 1)
                return last

            with pe.Fori(0, NT // 2) as g:
                for par in range(2):
                    b = 2 * g + par
                    rounds = pe.value_load(plan[0:1, ds(NT + b, 1)], min_val=2, max_val=NCH // 4 + 1)
                    before = pe.value_load(plan[0:1, ds(2 * NT + b, 1)], min_val=0, max_val=NT * (NCH // 4 + 1))
                    pe.wait_ge(a_lo_ready, 2 * g)
                    for s in range(4):
                        pe.wait_ge(hot_ready, 4 * before + s + 1)
                        count(s, par, s == 0, False)
                    with pe.Fori(1, rounds) as i:
                        for s in range(4):
                            pe.wait_ge(hot_ready, 4 * before + 4 * i + s + 1)
                            count(s, par, False, s == 3)

            pe.wait_ge(a_lo_ready, NT)
            pe.wait_ge(pads_ready, 5)
            for t in range(NT):
                for b in range(NT):
                    pe.matmul(ps[:, 6, t:t + 1], aT_hi[:, b, t, :], ones16[:, 0:1], start=(b == 0), stop=False)
                    last = pe.matmul(ps[:, 6, t:t + 1], aT_lo[:, b, t, :], ones16[:, 0:1], start=False,
                                     stop=(b == NT - 1))
            last.then_inc(deg_ready, 1)

            pe.wait_ge(wg_split, 1)
            with pe.Fori(0, NT // 2) as g:
                for par in range(2):
                    t = 2 * g + par
                    pe.wait_ge(hb_ready, 2 * g)
                    for k in range(KD):
                        for x_part, w_parts in ((xT_hi, (wg_hi, wg_lo)), (xT_lo, (wg_hi,))):
                            for w_part in w_parts:
                                for j in range(2):
                                    last = pe.matmul(ps[:, 2 * par + j, :], x_part[:, k, ds(t, 1), :].rearrange("p a b -> p (a b)"),
                                                     w_part[:, k, j * HALF:(j + 1) * HALF],
                                                     start=(k == 0 and x_part is xT_hi and w_part is wg_hi),
                                                     stop=(k == KD - 1 and x_part is xT_lo))
                    last.then_inc(h_ready, 1)

            pe.wait_ge(h_lo_ready, NT)
            with pe.Fori(0, NT // 2) as g:
                for par in range(2):
                    t = 2 * g + par
                    pe.wait_ge(x1_ready, 2 * g)
                    for b in range(NT):
                        for a_part, h_parts in ((aT_hi, (h_hi, h_lo)), (aT_lo, (h_hi,))):
                            for h_part in h_parts:
                                for j in range(2):
                                    last = pe.matmul(ps[:, 2 * par + j, :],
                                                     a_part[:, b, ds(t, 1), :].rearrange("p a b -> p (a b)"),
                                                     h_part[:, b, j * HALF:(j + 1) * HALF],
                                                     start=(b == 0 and a_part is aT_hi and h_part is h_hi),
                                                     stop=(b == NT - 1 and a_part is aT_lo))
                    last.then_inc(agg_ready, 1)
                for par in range(2):
                    t = 2 * g + par
                    pe.wait_ge(xn_ready, NT + t + 1)
                    pe.wait_ge(lo_ready, NT + 2 * g)
                    for k in range(KD):
                        last = pe.transpose(ps[:, 4 + 2 * par + k // 4, (k % 4) * PITCH:(k % 4) * PITCH + T],
                                            xn[:, par, k * 128:(k + 1) * 128], ident[0:T, 0:T])
                    last.then_inc(turned, 1)


            pe.wait_ge(sel_split, SPLIT * KD)
            pe.wait_ge(lo_ready, 2 * NT)
            with pe.Fori(0, NT // 2) as g:
                for par in range(2):
                    t = 2 * g + par
                    pe.wait_ge(exp_ready, 2 * g)
                    for k in range(KD):
                        for x_part, w_parts in ((xT_hi, (wsel_hi, wsel_lo)), (xT_lo, (wsel_hi,))):
                            for w_part in w_parts:
                                last = pe.matmul(ps[:, par, 0:2 * H * EX], flat(x_part[:, k, ds(t, 1), :]), w_part[:, k, :],
                                                 start=(k == 0 and x_part is xT_hi and w_part is wsel_hi),
                                                 stop=(k == KD - 1 and x_part is xT_lo))
                    last.then_inc(logits_ready, 1)
            pe.wait_ge(gates_ready, 1)
            for t in range(NT):
                pe.transpose(ps[:, 4 + t // 4, (t % 4) * T:(t % 4 + 1) * T], sig[:, t, H * EX:2 * H * EX], ident[0:T, 0:T])\
                    .then_inc(go_turned, 1)

            n_chunks = KD + PAIRS
            pe.wait_ge(att_pads, 10)
            pe.wait_ge(goT_ready, 1)
            with pe.Fori(0, H) as h:
                def project(i):
                    par = i % 2
                    for k in range(KD):
                        for x_part, w_parts in ((xT_hi, (wqkv_hi, wqkv_lo)), (xT_lo, (wqkv_hi,))):
                            for w_part in w_parts:
                                start = k == 0 and x_part is xT_hi and w_part is wqkv_hi
                                stop = k == KD - 1 and x_part is xT_lo
                                pe.matmul(ps[:, 2 + par, 0:2 * P], x_part[:, k, i, :], w_part[:, k, 0:2 * P],
                                          start=start, stop=stop)
                                last = pe.matmul(ps[:, par, :], x_part[:, k, i, :], w_part[:, k, 2 * P:WQKV],
                                                 start=start, stop=stop)
                    last.then_inc(proj_ready, 1)

                def turn(i):
                    bank = 4 + i % 2
                    pe.wait_ge(tok_ready, NT * h + i + 1)
                    if i >= 2:
                        pe.wait_ge(qkT_ready, NT * h + i - 1)
                        pe.wait_ge(kb_ready, NT * h + i - 1)
                    pe.transpose(ps16[:, bank, 0:T], tok[:, i, Q_LO:Q_LO + 2 * P], ident16[0:T, 0:T])
                    pe.transpose(ps16[:, bank, PITCH:PITCH + T], tok[:, i, K_HI:K_HI + 2 * P], ident16[0:T, 0:T])
                    pe.transpose(ps16[0:P, bank, 2 * PITCH:2 * PITCH + T], tok[:, i, K_LO:K_LO + P], ident16[0:T, 0:T])\
                        .then_inc(tr_ready, 1)

                def rough_scores(i):
                    pe.wait_ge(max_ready, NT * h + i)
                    for first, n in GROUPS:
                        last = pe.matmul(ps[:, first // 4, 0:n * T], qkT[:, 0, i, :], qkT[:, 1, first:first + n, 0:T],
                                         start=True, stop=True)
                    last.then_inc(smax_ready, 1)

                def turn_maxima(j):
                    pe.wait_ge(max_ready, NT * h + CH * (j + 1))
                    pe.wait_ge(qb_ready, NCK * h + j)
                    for a in range(CH):
                        last = pe.transpose(ps16[0:P + 1, 2, QM + PITCH * a:QM + PITCH * a + T],
                                            tok[:, CH * j + a, Q_HI:MAXC + 1], ident16[0:T, 0:T])
                    last.then_inc(qm_turned, 1)

                def scores(j, u):
                    n = KU * j + u
                    pe.wait_ge(qb_ready, NCK * h + j + 1)
                    pe.wait_ge(exp_done, KU * NCK * h + max(n - 1, 0))
                    for a in range(2):
                        into = ps[:, 3 + n % 2, a * CHN:(a + 1) * CHN]
                        pe.matmul(into, qkT[:, 1, 2 * u + a, :], qkT[:, 0, CH * j:CH * (j + 1), 0:T], start=True, stop=False)
                        last = pe.matmul(into, kb[:, 2 * u + a, :], qb[:, CH * j:CH * (j + 1), 0:T], start=False, stop=True)
                    last.then_inc(st_ready, 1)

                def weigh(j):
                    pe.wait_ge(plo_ready, KU * NCK * h + KU * (j + 1))
                    pe.wait_ge(og_ready, NCK * h + j)
                    if j == 0:
                        pe.wait_ge(vt_ready, NT * (h + 1))
                    for a in range(CH):
                        for t in range(NT):
                            for part in (pT_hi, pT_lo):
                                last = pe.matmul(ps[:, AV, a * (2 * P + 1):(a + 1) * (2 * P + 1)], part[:, j % 2, t, a, :],
                                                 vt[:, t, 0:2 * P + 1], start=(t == 0 and part is pT_hi),
                                                 stop=(t == NT - 1 and part is pT_lo))
                    last.then_inc(av_ready, 1)

                def turn_outputs(j):
                    pe.wait_ge(o32_ready, NCK * h + j + 1)
                    for a in range(CH):
                        last = pe.transpose(ps[:, AV, OT + a * T:OT + (a + 1) * T], flat(o32[:, a, :, :]), ident[0:T, 0:T])
                    last.then_inc(ot_ready, 1)

                def outputs(j, a):
                    for half in range(2):
                        n = 4 * j + 2 * a + half
                        pe.wait_ge(og_pair_ready, NCK * h + j + 1)
                        pe.wait_ge(acc_added, 2 * NT * h + max(n - 1, 0))
                        for k in range(PAIRS):
                            for o_part_, w_parts in ((og_hi, (wo_hi, wo_lo)), (og_lo, (wo_hi,))):
                                for w_part in w_parts:
                                    last = pe.matmul(ps[:, 6 + half, :], o_part_[:, j % 2, k, a, :],
                                                     w_part[:, k, half * HALF:(half + 1) * HALF],
                                                     start=(k == 0 and o_part_ is og_hi and w_part is wo_hi),
                                                     stop=(k == PAIRS - 1 and o_part_ is og_lo))
                        last.then_inc(o_ready, 1)

                pe.wait_ge(w_split, SPLIT * n_chunks * h + SPLIT * KD)
                for i in range(NT + 2):
                    if i < NT:
                        if i >= 2:
                            pe.wait_ge(v32_ready, NT * h + i - 1)
                            pe.wait_ge(qk_pass, NT * h + i - 1)
                        project(i)
                    if i >= 2:
                        turn(i - 2)
                pe.wait_ge(v32_ready, NT * (h + 1))
                pe.wait_ge(qk_pass, NT * (h + 1))
                pe.wait_ge(qkT_ready, NT * (h + 1))
                pe.wait_ge(kb_ready, NT * (h + 1))
                for a in range(CH):
                    rough_scores(a)
                for j in range(NCK + 2):
                    if j < NCK:
                        turn_maxima(j)
                        for u in range(KU):
                            scores(j, u)
                    if j + 1 < NCK:
                        rough_scores(CH * (j + 1))
                    if 1 <= j <= NCK:
                        weigh(j - 1)
                    if j + 1 < NCK:
                        rough_scores(CH * (j + 1) + 1)
                    if j == 2:
                        pe.wait_ge(w_split, SPLIT * n_chunks * (h + 1))
                    if j >= 2:
                        outputs(j - 2, 0)
                    if 1 <= j <= NCK:
                        turn_outputs(j - 1)
                    if j >= 2:
                        outputs(j - 2, 1)

            for g in range(NT // 2):
                for par in range(2):
                    t = 2 * g + par
                    pe.wait_ge(y_ready, t + 1)
                    if g:
                        pe.wait_ge(lo_ready, 2 * NT + 2 * g)
                    for k in range(KD):
                        last = pe.transpose(ps[:, 2 * par + k // 4, (k % 4) * PITCH:(k % 4) * PITCH + T],
                                            acc[:, t, k * 128:(k + 1) * 128], ident[0:T, 0:T])
                    last.then_inc(turned, 1)
            pe.wait_ge(mlp_split, SPLIT * KD)
            for n, (first, tiles, f) in enumerate(hidden()):
                pe.wait_ge(lo_ready, 2 * NT + first + tiles)
                if n >= 4:
                    pe.wait_ge(h_hi2_ready, n - 3)
                for k in range(KD):
                    for w_part, x_parts in ((w1_hi, (xT_hi, xT_lo)), (w1_lo, (xT_hi,))):
                        for x_part in x_parts:
                            last = pe.matmul(ps[:, 4 + n % 4, 0:tiles * T], w_part[:, k, f * 128:(f + 1) * 128],
                                             x_part[:, k, first:first + tiles, 0:T],
                                             start=(k == 0 and w_part is w1_hi and x_part is xT_hi),
                                             stop=(k == KD - 1 and w_part is w1_lo))
                last.then_inc(hs_ready, 1)
            pe.wait_ge(att_pads, 12)
            pe.wait_ge(mlp_split, SPLIT * (KD + F // 128))
            pe.wait_ge(h_lo2_ready, len(hidden()))
            for t in range(NT):
                if t >= 2:
                    pe.wait_ge(var_ready, 3 * NT + t - 1)
                for k in range(F // 128):
                    for h_part, w_parts in ((hT_hi, (w2_hi, w2_lo)), (hT_lo, (w2_hi,))):
                        for w_part in w_parts:
                            for half in range(2):
                                last = pe.matmul(ps[:, 4 + 2 * (t % 2) + half, :], h_part[:, k, t, :],
                                                 w_part[:, k, half * HALF:(half + 1) * HALF],
                                                 start=(k == 0 and h_part is hT_hi and w_part is w2_hi),
                                                 stop=(k == F // 128 - 1 and h_part is hT_lo))
                last.then_inc(z_ready, 1)


def constants():
    import numpy as np

    kept = np.zeros((128, C_KEPT), np.float32)
    kept[:, C_ID:C_ID + 128] = np.eye(128)
    kept[:, C_REV:C_REV + EX] = np.arange(EX, 0, -1)
    kept[:, C_LNP] = np.log(SP_)
    c = np.zeros((128, CCOLS), np.float32)
    c[:, C_IOTA:C_IOTA + NT * PITCH] = np.arange(NT * PITCH)
    c[:, C_CHUNK:C_CHUNK + NCH] = np.arange(NCH).reshape(NCH // CPR, CPR).T.reshape(-1)
    c[:, C_SELF:C_SELF + NT] = np.arange(128)[:, None] + T * np.arange(NT)
    c[:, C_LOW] = T * np.arange(128)
    c[:, C_UPPER:C_UPPER + NT] = np.arange(128)[:, None] < np.arange(NT)
    c[:, C_ID10:] = np.eye(128)[:, 0:NCH // CPR]
    half = NROT // 2
    inv = np.float32(10000.0) ** (-np.arange(half, dtype=np.float32) / np.float32(half))
    angle = np.arange(N, dtype=np.float32)[:, None] * inv[None, :].astype(np.float32)
    cos, sin = np.cos(angle), np.sin(angle)
    rope = np.concatenate([cos, cos, -sin, sin], -1).astype(np.float32)
    return kept, c, rope.reshape(NT, T, 2 * NROT).transpose(1, 0, 2)


def kernel(**inputs):
    import numpy as np
    import concourse.bacc as bacc
    from concourse.bass_utils import run_bass_kernel_spmd

    def slabs(w):
        return np.ascontiguousarray(w.reshape(-1, 128, w.shape[-1]).transpose(1, 0, 2))

    nc = bacc.Bacc("TRN2", target_bir_lowering=False, num_devices=1)
    arrays, args = {}, []

    def give(name, a):
        a = np.ascontiguousarray(a)
        arrays[name] = a
        args.append(nc.dram_tensor(name, a.shape, mybir.dt.from_np(a.dtype), kind="ExternalInput").ap())

    give("x", inputs["x"])
    give("src", inputs["src"].reshape(NCH, T).T)
    give("dst", inputs["dst"].reshape(NCH, T).T)
    give("dst_rows", inputs["dst"].reshape(NCH // CPR, CPR, T))
    give("wg", slabs(inputs["L0_gnn_W"].T))
    give("bg", inputs["L0_gnn_b"])
    sel = np.concatenate([inputs["L0_ffn_Wsel_v"].reshape(H * EX, D), inputs["L0_ffn_Wsel_o"].reshape(H * EX, D)])
    give("wsel", slabs(sel.T))
    wv = inputs["L0_ffn_Wv"].transpose(0, 2, 1, 3).reshape(H, D, EX * P)
    qkv = np.concatenate([inputs["L0_ffn_Wq"], inputs["L0_ffn_Wk"], wv], -1)
    give("wqkv", qkv.reshape(H, KD, 128, WQKV).transpose(0, 2, 1, 3))
    give("wo", inputs["L0_ffn_Wo"].reshape(H, PAIRS, 128, D).transpose(0, 2, 1, 3))
    give("w1", slabs(inputs["L0_ffn_W1"]))
    give("b1", inputs["L0_ffn_b1"].reshape(F // 128, 128).T)
    give("w2", slabs(inputs["L0_ffn_W2"]))
    give("rowvecs", np.stack([inputs["L0_ffn_ln1_g"], inputs["L0_ffn_ln1_b"], inputs["L0_ffn_b2"],
                              inputs["L0_ffn_ln2_g"], inputs["L0_ffn_ln2_b"]]))
    kept, graph, rope = constants()
    give("ctab", kept)
    give("gtab", graph)
    give("rtab", rope)
    args.append(nc.dram_tensor("out", [N, D], F32, kind="ExternalOutput").ap())
    build(nc, *args)
    r = run_bass_kernel_spmd(nc, [arrays], core_ids=[0])
    return r.results[0]["out"]
```

```python
from contextlib import ExitStack

import concourse.bass as bass
from concourse import mybir

ALU = mybir.AluOpType
ACT = mybir.ActivationFunctionType
AX_X = mybir.AxisListType.X
F32 = mybir.dt.float32
F16 = mybir.dt.float16
I32 = mybir.dt.int32
ds = bass.ds

N = 1250
D = 1024
E_EDGES = 40000
H, P, EX, F = 16, 64, 8, 512
NROT = 32
EPS = 1e-5

T = 125
NT = N // T
PITCH = 128
KD = D // 128
NCH = E_EDGES // T
CPR = 4
SELF = NCH + 8
ECOLS = SELF + NT
HALF = D // 2
GROUPS = ((0, 4), (4, 4), (8, 2))

SX = 64.0
SW = 256.0

SQ = 16.0
SP_ = 1024.0
SM = 512.0
WQKV = (2 + EX) * P
PAIRS = EX // 2
CH = 2
NCK = NT // CH
KU = NT // 2
SPLIT = 3
CHN = CH * T

Q_LO, Q_HI, MAXC, K_LO, K_HI, K_HI2, TOKW = 0, 64, 128, 132, 196, 260, 328

C_ID = 0
C_REV = 128
C_LNP = C_REV + EX
C_KEPT = C_LNP + 1
C_IOTA = 0
C_CHUNK = C_IOTA + NT * PITCH
C_SELF = C_CHUNK + NCH
C_LOW = C_SELF + NT
C_UPPER = C_LOW + 1
C_ID10 = C_UPPER + NT
CCOLS = C_ID10 + NCH // CPR


class Chain:

    def __init__(self, engine, sem):
        self.engine, self.sem, self.base, self.n = engine, sem, 0, 0

    def done(self, instruction):
        instruction.then_inc(self.sem, 1)
        self.n += 1

    def wait(self):
        self.engine.wait_ge(self.sem, self.base + self.n)

    def step(self, instruction):
        self.done(instruction)
        self.wait()

    def enter(self, i, per_round):
        self.saved, self.per_round = (self.base, self.n), per_round
        self.base, self.n = self.base + self.n + i * per_round, 0

    def leave(self, rounds):
        assert self.n == self.per_round, (self.n, self.per_round)
        base, n = self.saved
        self.base, self.n = base, n + rounds * self.per_round


def build(nc, x, src, dst, dst_rows, wg, bg, wsel, wqkv, wo, w1, b1, w2, rowvecs, ctab, gtab, rtab, out):
    ctx = ExitStack()

    def sb(name, shape, dt, where=None):
        return (where or ctx).enter_context(nc.sbuf_tensor(name, shape, dt))

    def sem(name):
        return ctx.enter_context(nc.semaphore(name))

    with ctx:
        ps = ctx.enter_context(nc.psum_tensor("ps", [128, 8, 512], F32))
        goT_dram = nc.dram_tensor("goT_dram", [H * EX, N], F32, kind="Internal").ap()
        x1_dram = nc.dram_tensor("x1_dram", [N, D], F32, kind="Internal").ap()

        consts = sb("consts", [128, C_KEPT], F32)
        xT_hi = sb("xT_hi", [128, KD, NT, PITCH], F16)
        xT_lo = sb("xT_lo", [128, KD, NT, PITCH], F16)
        arena = sb("arena", [128, NT * D], F32)
        stats = sb("stats", [T, 2, 2, 6], F32)
        mv = sb("mv", [T, 2, 2], F32)
        var = sb("var", [T, 2], F32)
        std = sb("std", [T, 2], F32)
        rstd = sb("rstd", [T, 2], F32)
        ident = consts[:, C_ID:C_ID + 128]
        ident16 = sb("ident16", [128, 128], F16)
        acc = arena[0:T, :].rearrange("p (t d) -> p t d", t=NT)
        wg_hi = arena[:, 0:KD * D // 2].bitcast(F16).rearrange("p (k d) -> p k d", k=KD)
        wg_lo = arena[:, KD * D // 2:KD * D].bitcast(F16).rearrange("p (k d) -> p k d", k=KD)
        w_stage = arena[:, KD * D:NT * D].rearrange("p (s d) -> p s d", s=2)

        gnn = ExitStack()
        gconst = sb("gconst", [128, CCOLS], F32, gnn)
        aT_hi = sb("aT_hi", [T, NT, NT, PITCH], F16, gnn)
        aT_lo = sb("aT_lo", [T, NT, NT, PITCH], F16, gnn)
        h_hi = sb("h_hi", [T, NT, D], F16, gnn)
        h_lo = sb("h_lo", [T, NT, D], F16, gnn)
        xb = sb("xb", [T, 2, D], F32, gnn)
        xn = sb("xn", [T, 2, D], F32, gnn)
        bias_g = sb("bias_g", [T, D], F32, gnn)
        edges_i = xn[:, 0, 0:2 * NCH].bitcast(I32).rearrange("p (a c) -> p a c", a=2)
        near = xn[0:NT, 0, 0:2 * NCH].rearrange("p (a c) -> p a c", a=2)
        rows_i = xn[0:NCH // CPR, 1, 0:CPR * T].bitcast(I32).rearrange("p (a c) -> p a c", a=CPR)
        rows = xn[0:NCH // CPR, 1, HALF:HALF + CPR * T].rearrange("p (a c) -> p a c", a=CPR)
        edges = sb("edges", [T, 2, ECOLS], F32, gnn)
        spans = sb("spans", [NCH // CPR, 2, CPR], F32, gnn)
        walk = sb("walk", [NT, 8], F32, gnn)
        walk_i = sb("walk_i", [NT, 1], I32, gnn)
        plan = sb("plan", [1, 3 * NT], I32, gnn)
        deg = sb("deg", [T, NT], F32, gnn)
        dis = sb("dis", [T, 3, NT], F32, gnn)
        iota16 = h_hi[:, 0:2, :].rearrange("p a b -> p (a b)")[:, 0:NT * PITCH]
        hot_src = [h_hi[:, 2 + 2 * s:4 + 2 * s, :].rearrange("p a b -> p (a b)")[:, 0:N] for s in range(4)]
        hot_dst = [h_lo[:, s, 0:PITCH] for s in range(4)]
        ones16 = sb("ones16", [T, 2], F16, gnn)
        gnn.close()

        gv = sb("gv", [T, NT, H * EX], F32)
        rope = sb("rope", [T, NT, 2 * NROT], F32)

        gates = ExitStack()
        wsel_hi = sb("wsel_hi", [128, KD, 2 * H * EX], F16, gates)
        wsel_lo = sb("wsel_lo", [128, KD, 2 * H * EX], F16, gates)
        sig = sb("sig", [T, NT, 2 * H * EX], F32, gates)
        pick_a = sb("pick_a", [T, NT, 2 * H * EX], F32, gates)
        pick_b = sb("pick_b", [T, NT, 2 * H * EX], F32, gates)
        best = sb("best", [T, 2, NT * 2 * H], F32, gates)
        goT = sb("goT", [128, NT, T], F32, gates)
        sel_stage = sb("sel_stage", [128, 2, 2 * H * EX], F32, gates)
        gates.close()

        att = ExitStack()
        wqkv_hi = sb("wqkv_hi", [128, KD, WQKV], F16, att)
        wqkv_lo = sb("wqkv_lo", [128, KD, WQKV], F16, att)
        wo_hi = sb("wo_hi", [128, PAIRS, D], F16, att)
        wo_lo = sb("wo_lo", [128, PAIRS, D], F16, att)
        stage = sb("stage", [128, 2, D], F32, att)
        tok = sb("tok", [T, NT, TOKW], F16, att)
        vt = sb("vt", [T, NT, 2 * P + 2], F16, att)
        qk32 = sb("qk32", [T, 2, 2, P], F32, att)
        rot = sb("rot", [T, 2, 2, NROT], F32, att)
        vprod = sb("vprod", [T, EX, P], F32, att)
        v32 = sb("v32", [T, 2, P], F32, att)
        qkT = sb("qkT", [128, 2, NT, PITCH], F16, att)
        qb = sb("qb", [P + 1, NT, PITCH], F16, att)
        kb = sb("kb", [P + 1, NT, PITCH], F16, att)
        mx = sb("mx", [T, 2], F32, att)
        pT_hi = sb("pT_hi", [T, 2, NT, CH, PITCH], F16, att)
        pT_lo = sb("pT_lo", [T, 2, NT, CH, PITCH], F16, att)
        p32 = sb("p32", [T, 2, 2 * CHN], F32, att)
        go_b = sb("go_b", [128, 2, PAIRS, CHN], F32, att)
        og32 = sb("og32", [128, PAIRS, CHN], F32, att)
        og_hi = sb("og_hi", [128, 2, PAIRS, CH, PITCH], F16, att)
        og_lo = sb("og_lo", [128, 2, PAIRS, CH, PITCH], F16, att)
        rsum = sb("rsum", [T, CH], F32, att)
        o_part = sb("o_part", [T, CH, P], F32, att)
        o32 = sb("o32", [T, CH, 2, P], F32, att)
        att.close()

        mlp = ExitStack()
        w1_hi = sb("w1_hi", [128, KD, F], F16, mlp)
        w1_lo = sb("w1_lo", [128, KD, F], F16, mlp)
        w2_hi = sb("w2_hi", [128, F // 128, D], F16, mlp)
        w2_lo = sb("w2_lo", [128, F // 128, D], F16, mlp)
        mlp_stage = sb("mlp_stage", [128, 2, D], F32, mlp)
        vecs = sb("vecs", [T, 5, D], F32, mlp)
        hT_hi = sb("hT_hi", [128, F // 128, NT, PITCH], F16, mlp)
        hT_lo = sb("hT_lo", [128, F // 128, NT, PITCH], F16, mlp)
        h32 = sb("h32", [128, 2, 4 * T], F32, mlp)
        b1c = sb("b1c", [128, F // 128], F32, mlp)
        fin = sb("fin", [T, 2, D], F32, mlp)
        x1b = sb("x1b", [T, 2, D], F32, mlp)
        mlp.close()

        const_in = sem("const_in")
        edges_in = sem("edges_in")
        bias_in = sem("bias_in")
        x_in = [sem("x_in0"), sem("x_in1")]
        wg_in = [sem("wg_in0"), sem("wg_in1")]
        wg_split = sem("wg_split")
        pool_chain = sem("pool_chain")
        dve_chain = sem("dve_chain")
        pads_ready = sem("pads_ready")
        spans_ready = sem("spans_ready")
        spans_spread = sem("spans_spread")
        walk_ready = sem("walk_ready")
        walk_turned = sem("walk_turned")
        plan_ready = sem("plan_ready")
        var_ready = sem("var_ready")
        std_ready = sem("std_ready")
        xn_ready = sem("xn_ready")
        turned = sem("turned")
        hi_ready = sem("hi_ready")
        lo_ready = sem("lo_ready")
        hot_ready = sem("hot_ready")
        hot_used = [sem(f"hot_used{s}") for s in range(4)]
        a_hi_ready = sem("a_hi_ready")
        a_lo_ready = sem("a_lo_ready")
        deg_ready = sem("deg_ready")
        deg_root = sem("deg_root")
        dis_ready = sem("dis_ready")
        h_ready = sem("h_ready")
        hb_ready = sem("hb_ready")
        h_hi_ready = sem("h_hi_ready")
        h_lo_ready = sem("h_lo_ready")
        agg_ready = sem("agg_ready")
        x1_ready = sem("x1_ready")
        acc_ready = sem("acc_ready")
        x1_out = [sem("x1_out0"), sem("x1_out1")]

        sel_in0 = sem("sel_in0")
        sel_in1 = sem("sel_in1")
        sel_split = sem("sel_split")
        rope_in = sem("rope_in")
        logits_ready = sem("logits_ready")
        exp_ready = sem("exp_ready")
        gates_ready = sem("gates_ready")
        go_turned = sem("go_turned")
        goT_ready = sem("goT_ready")
        goT_out = sem("goT_out")
        w_in0 = sem("w_in0")
        w_in1 = sem("w_in1")
        w_split = sem("w_split")
        split_gate = sem("split_gate")
        att_pads = sem("att_pads")
        proj_ready = sem("proj_ready")
        values_ready = sem("values_ready")
        qk_pass = sem("qk_pass")
        rope_ready = sem("rope_ready")
        v32_ready = sem("v32_ready")
        tok_hi = sem("tok_hi")
        vt_hi = sem("vt_hi")
        tok_ready = sem("tok_ready")
        vt_ready = sem("vt_ready")
        tr_ready = sem("tr_ready")
        qkT_ready = sem("qkT_ready")
        kb_ready = sem("kb_ready")
        smax_ready = sem("smax_ready")
        max_ready = sem("max_ready")
        qm_turned = sem("qm_turned")
        qb_ready = sem("qb_ready")
        st_ready = sem("st_ready")
        exp_done = sem("exp_done")
        plo_ready = sem("plo_ready")
        av_ready = sem("av_ready")
        rs_ready = sem("rs_ready")
        opart_ready = sem("opart_ready")
        o32_ready = sem("o32_ready")
        ot_ready = sem("ot_ready")
        og_ready = sem("og_ready")
        og_hi_ready = sem("og_hi_ready")
        og_pair_ready = sem("og_pair_ready")
        go_in0 = sem("go_in0")
        go_in1 = sem("go_in1")
        o_ready = sem("o_ready")
        acc_added = sem("acc_added")
        mlp_in0 = sem("mlp_in0")
        mlp_in1 = sem("mlp_in1")
        mlp_split = sem("mlp_split")
        vecs_in = sem("vecs_in")
        b1_in = sem("b1_in")
        b1_ready = sem("b1_ready")
        y_ready = sem("y_ready")
        hs_ready = sem("hs_ready")
        h_hi2_ready = sem("h_hi2_ready")
        h_lo2_ready = sem("h_lo2_ready")
        z_ready = sem("z_ready")
        x1_in0 = sem("x1_in0")
        x1_in1 = sem("x1_in1")
        fin_ready = sem("fin_ready")
        fin_out0 = sem("fin_out0")
        fin_out1 = sem("fin_out1")
        w_in, go_in = (w_in0, w_in1), (go_in0, go_in1)
        sel_in, mlp_in, x1_in, fin_out = (sel_in0, sel_in1), (mlp_in0, mlp_in1), (x1_in0, x1_in1), (fin_out0, fin_out1)

        ps16 = ps[:, :, :].rearrange("p a b -> p (a b)").bitcast(F16).rearrange("p (a b) -> p a b", a=8)
        PER_HEAD = 2 * NT
        LATE = 2 * 2 * CH
        LATE_VALUES = 6
        AV, OT = 5, CH * (2 * P + 1)
        QM = 512

        def head_of(w, h):
            return w[ds(h, 1)].rearrange("o p k n -> (o p) k n") if not isinstance(h, int) else w[h]

        def columns(row, a, b, n):
            step = b - a
            return row[:, a:a + 2 * step].rearrange("p (x c) -> p x c", x=2)[:, :, 0:n]

        def p_block(j, u):
            return p32[:, (KU * j + u) % 2, :].rearrange("p (t s c) -> p t s c", t=2, s=CH)

        def head_order():
            def sc(j, *pairs):
                return [(what, j, u) for u in pairs for what in ("scores", "weights")]

            def out_(j, *numbers):
                return [("output", j, n) for n in numbers]

            def values(*tiles):
                return [("values", 0, t) for t in tiles]

            def rough(t):
                return [("rough", 0, t)]

            def weigh(j):
                return [("weigh", j, a) for a in range(CH)] + [("normalise", j, 0)]

            def max_(j):
                return [("turn maxima", j, 0)]

            def turn_out(j):
                return [("turn outputs", j, 0)]

            order = []
            for t in range(NT + 1):
                order.append(("project", 0, t))
                if t % 2 == 0 and t < NT:
                    order += values(t // 2)
                if 2 <= t < NT:
                    order.append(("turn", 0, t - 2))
            order += values(5) + [("turn", 0, NT - 2)] + out_(3, 0) + [("turn", 0, NT - 1)] + out_(3, 1)
            order += rough(0) + out_(3, 2) + rough(1) + out_(3, 3) + max_(0) + out_(4, 0)
            order += sc(0, 0, 1) + rough(2) + out_(4, 1) + sc(0, 2, 3) + out_(4, 2) + rough(3) + sc(0, 4) + out_(4, 3)
            order += max_(1) + values(6)
            order += sc(1, 0, 1) + rough(4) + values(7) + sc(1, 2, 3) + rough(5) + values(8) + max_(2) + sc(1, 4)
            order += values(9) + [("scores", 2, 0), ("scores", 2, 1)] + weigh(0) + rough(6)
            order += [("weights", 2, 0)]
            order += turn_out(0) + [("weights", 2, 1)] + rough(7) + sc(2, 2) + weigh(1) + sc(2, 3) + out_(0, 0) + sc(2, 4)
            order += out_(0, 1) + max_(3) + turn_out(1) + out_(0, 2) + out_(0, 3)
            order += sc(3, 0, 1) + out_(1, 0) + rough(8) + sc(3, 2, 3) + weigh(2) + out_(1, 1) + rough(9) + sc(3, 4)
            order += out_(1, 2) + max_(4) + turn_out(2) + out_(1, 3)
            order += sc(4, 0, 1) + out_(2, 0) + sc(4, 2, 3) + weigh(3) + sc(4, 4) + out_(2, 1) + turn_out(3) + out_(2, 2)
            order += weigh(4) + out_(2, 3) + turn_out(4)
            return order

        def output_count(h, j, n):
            return PER_HEAD * h + 2 * CH * ((j + 2) % NCK) + n

        def hidden():
            return [(first, tiles, f) for first, tiles in GROUPS for f in range(F // 128)]

        def values_bank(i):
            return i % 2 if i < LATE_VALUES else 6 + i % 2

        def flat(ap):
            return ap.rearrange("p a b -> p (a b)")

        block = ctx.enter_context(nc.Block())

        def tile_rows(dram, t):
            return dram[ds(t * T, T), :]

        def turned_view(par, bank=0):
            both = ps[:, bank + 2 * par:bank + 2 * par + 2, :].rearrange("p a (b c) -> p a b c", b=4)
            return both[:, :, :, 0:T].rearrange("p a b (o c) -> p (a b) o c", o=1)

        @block.sync
        def _(sp):
            sp.dma_start(gconst[:, :], gtab).then_inc(const_in, 16)
            sp.dma_start(consts[:, :], ctab).then_inc(const_in, 16)
            sp.dma_start(rows_i[:, :, :], dst_rows).then_inc(edges_in, 16)
            sp.dma_start(edges_i[:, 0, :], src).then_inc(edges_in, 16)
            sp.dma_start(edges_i[:, 1, :], dst).then_inc(edges_in, 16)
            for t in range(2):
                sp.dma_start(xb[:, t, :], tile_rows(x, t)).then_inc(x_in[t], 16)
            sp.dma_start(bias_g[:, :], bg.partition_broadcast(T)).then_inc(bias_in, 16)
            with sp.Fori(1, NT // 2) as g:
                for par in range(2):
                    sp.wait_ge(turned, 2 * g + par - 1)
                    sp.dma_start(xb[:, par, :], tile_rows(x, 2 * g + par)).then_inc(x_in[par], 16)
            with sp.Fori(0, NT // 2) as g:
                for par in range(2):
                    sp.wait_ge(h_lo_ready, NT)
                    sp.wait_ge(x1_out[par], g * 16)
                    sp.wait_ge(xn_ready, NT + 2 * g)
                    sp.dma_start(xb[:, par, :], tile_rows(x, 2 * g + par)).then_inc(x_in[par], 16)
                for par in range(2):
                    sp.wait_ge(x1_ready, 2 * g + par + 1)
                    sp.dma_start(tile_rows(x1_dram, 2 * g + par), xb[:, par, :]).then_inc(x1_out[par], 16)
            for par in range(2):
                sp.wait_ge(x1_out[par], 16 * (NT // 2))
            n_chunks = KD + PAIRS

            def load_chunk(h, c):
                if c < KD:
                    sp.dma_start(stage[:, c % 2, 0:WQKV], head_of(wqkv, h)[:, c, :]).then_inc(w_in[c % 2], 16)
                else:
                    sp.dma_start(stage[:, c % 2, :], head_of(wo, h)[:, c - KD, :]).then_inc(w_in[c % 2], 16)

            sp.wait_ge(goT_out, 16)
            sp.dma_start(rope[:, :, :], rtab).then_inc(rope_in, 16)
            load_chunk(0, 0)
            load_chunk(0, 1)
            with sp.Fori(0, H - 1) as h:
                for c in range(n_chunks):
                    sp.wait_ge(w_split, SPLIT * n_chunks * h + SPLIT * (c + 1))
                    load_chunk(h + (c + 2) // n_chunks, (c + 2) % n_chunks)
            for c in range(n_chunks - 2):
                sp.wait_ge(w_split, SPLIT * n_chunks * (H - 1) + SPLIT * (c + 1))
                load_chunk(H - 1, c + 2)


            sp.wait_ge(acc_added, PER_HEAD * H + LATE)
            chunks = [(w1, k, F) for k in range(KD)] + [(w2, k, D) for k in range(F // 128)]
            for c, (w, k, width) in enumerate(chunks):
                if c >= 2:
                    sp.wait_ge(mlp_split, SPLIT * (c - 1))
                sp.dma_start(mlp_stage[:, c % 2, 0:width], w[:, k, :]).then_inc(mlp_in[c % 2], 16)
                if c == 1:
                    sp.dma_start(vecs[:, :, :], rowvecs.partition_broadcast(T)).then_inc(vecs_in, 16)
                    sp.dma_start(b1c[:, :], b1).then_inc(b1_in, 16)
            for t in range(NT):
                if t >= 2:
                    sp.wait_ge(fin_ready, t - 1)
                sp.dma_start(x1b[:, t % 2, :], x1_dram[t * T:(t + 1) * T, :]).then_inc(x1_in[t % 2], 16)
                if t >= 1:
                    sp.wait_ge(fin_ready, t)
                    sp.dma_start(out[(t - 1) * T:t * T, :], fin[:, (t - 1) % 2, :]).then_inc(fin_out[(t - 1) % 2], 16)
            sp.wait_ge(fin_ready, NT)
            sp.dma_start(out[(NT - 1) * T:NT * T, :], fin[:, (NT - 1) % 2, :]).then_inc(fin_out[(NT - 1) % 2], 16)
            for par in range(2):
                sp.wait_ge(fin_out[par], 16 * (NT // 2))

        @block.gpsimd
        def _(pool):
            def split(hi, lo, staged, steps_done, n, gate=None):
                if gate is not None:
                    pool.sem_inc(gate, 1)
                pool.tensor_scalar(hi, staged, SW, 0.0, ALU.mult, ALU.add).then_inc(steps_done, 1)
                pool.wait_ge(steps_done, n + 1)
                if gate is not None:
                    pool.sem_inc(gate, 1)
                pool.tensor_scalar(staged, staged, SW, 0.0, ALU.mult, ALU.add).then_inc(steps_done, 1)
                pool.wait_ge(steps_done, n + 2)
                pool.tensor_tensor(lo, staged, hi, ALU.subtract).then_inc(steps_done, 1)

            for buf in (xT_hi, xT_lo):
                pool.memset(buf[:, :, :, T:PITCH], 0.0).then_inc(pads_ready, 1)
            for buf in (aT_hi, aT_lo):
                pool.memset(buf[:, :, :, T:PITCH], 0.0).then_inc(pads_ready, 1)
            pool.memset(ones16[:, :], 1.0).then_inc(pads_ready, 1)
            for k in range(2):
                pool.dma_start(w_stage[:, k, :], wg[:, k, :]).then_inc(wg_in[k], 16)
            for k in range(KD):
                pool.wait_ge(wg_in[k % 2], 16 * (k // 2 + 1))
                split(wg_hi[:, k, :], wg_lo[:, k, :], w_stage[:, k % 2, :], pool_chain, SPLIT * k)
                if k + 2 < KD:
                    pool.wait_ge(pool_chain, SPLIT * (k + 1))
                    pool.dma_start(w_stage[:, k % 2, :], wg[:, k + 2, :]).then_inc(wg_in[k % 2], 16)
            pool.wait_ge(pool_chain, SPLIT * KD)
            pool.sem_inc(wg_split, 1)
            with pool.Fori(0, NT // 2) as g:
                for par in range(2):
                    pool.wait_ge(xn_ready, NT + 2 * g + par + 1)
                    pool.tensor_copy(acc[:, ds(2 * g + par, 1), :].rearrange("p a b -> p (a b)"), xn[:, par, :])\
                        .then_inc(acc_ready, 1)

            pool.wait_ge(lo_ready, 2 * NT)
            for par in range(2):
                pool.wait_ge(x1_out[par], 16 * (NT // 2))
            for k in range(KD):
                if k >= 2:
                    pool.wait_ge(sel_split, SPLIT * (k - 1))
                pool.dma_start(sel_stage[:, k % 2, :], wsel[:, k, :]).then_inc(sel_in[k % 2], 16)
                if k >= 1:
                    pool.wait_ge(sel_in[(k - 1) % 2], 16 * ((k - 1) // 2 + 1))
                    split(wsel_hi[:, k - 1, :], wsel_lo[:, k - 1, :], sel_stage[:, (k - 1) % 2, :], sel_split, SPLIT * (k - 1))
            pool.wait_ge(sel_in[(KD - 1) % 2], 16 * (KD // 2))
            split(wsel_hi[:, KD - 1, :], wsel_lo[:, KD - 1, :], sel_stage[:, (KD - 1) % 2, :], sel_split, SPLIT * (KD - 1))

            pool.wait_ge(goT_out, 16)
            for buf in (wo_hi[:, :, :], wo_lo[:, :, :], og_hi[:, :, :, :, :], og_lo[:, :, :, :, :],
                        qkT[:, :, :, T:PITCH], qb[:, :, T:PITCH], kb[:, :, T:PITCH], pT_hi[:, :, :, :, T:PITCH], pT_lo[:, :, :, :, T:PITCH]):
                pool.memset(buf, 0.0).then_inc(att_pads, 1)
            pool.wait_ge(att_pads, 9)
            pool.memset(kb[P:P + 1, :, 0:T], SM).then_inc(att_pads, 1)
            pool.wait_ge(att_pads, 10)
            pool.memset(vt[:, :, 2 * P:2 * P + 2], 1.0).then_inc(att_pads, 1)
            pool.memset(tok[:, :, MAXC + 1:K_LO], 0.0).then_inc(att_pads, 1)

            n_chunks = KD + PAIRS
            with pool.Fori(0, H) as h:
                for c in range(n_chunks):
                    if c == 0:
                        pool.wait_ge(values_ready, NT * h)
                    if c == KD:
                        pool.wait_ge(o_ready, PER_HEAD * h + LATE)
                    pool.wait_ge(w_in[c % 2], 16 * (n_chunks // 2 * h + c // 2 + 1))
                    if c < KD:
                        split(wqkv_hi[:, c, :], wqkv_lo[:, c, :], stage[:, c % 2, 0:WQKV], w_split, SPLIT * n_chunks * h + SPLIT * c, split_gate)
                    else:
                        split(wo_hi[:, c - KD, :], wo_lo[:, c - KD, :], stage[:, c % 2, :], w_split, SPLIT * n_chunks * h + SPLIT * c, split_gate)

            pool.wait_ge(acc_added, PER_HEAD * H + LATE)
            for buf in (hT_hi, hT_lo):
                pool.memset(buf[:, :, :, T:PITCH], 0.0).then_inc(att_pads, 1)
            for c in range(KD + F // 128):
                pool.wait_ge(mlp_in[c % 2], 16 * (c // 2 + 1))
                if c < KD:
                    split(w1_hi[:, c, :], w1_lo[:, c, :], mlp_stage[:, c % 2, 0:F], mlp_split, SPLIT * c)
                else:
                    split(w2_hi[:, c - KD, :], w2_lo[:, c - KD, :], mlp_stage[:, c % 2, :], mlp_split, SPLIT * c)

        def stats_of(dve, chain, par, tile, sems):
            for j in range(2):
                chain.done(dve.bn_stats(stats[:, par, j, :], tile[:, j * HALF:(j + 1) * HALF]))
            chain.wait()
            chain.step(dve.bn_aggr(mv[:, par, :], stats[:, par, :, :]))
            dve.tensor_scalar(var[:, par:par + 1], mv[:, par, 1:2], EPS, None, ALU.add).then_inc(sems, 1)

        @block.vector
        def _(dve):
            chain = Chain(dve, dve_chain)
            dve.wait_ge(const_in, 32)
            dve.wait_ge(edges_in, 48)
            dve.tensor_copy(ident16[:, :], ident)
            dve.tensor_copy(iota16, gconst[0:T, C_IOTA:C_IOTA + NT * PITCH])
            dve.memset(edges[:, :, NCH:SELF], -1.0)
            for a in range(2):
                dve.tensor_copy(edges[:, a, 0:NCH], edges_i[:, a, :])
                dve.tensor_copy(edges[:, a, SELF:ECOLS], gconst[0:T, C_SELF:C_SELF + NT])
            chain.step(dve.tensor_copy(rows[:, :, :], rows_i[:, :, :]))
            dve.tensor_reduce(spans[:, 0, :], rows[:, :, :], AX_X, ALU.min)
            dve.tensor_reduce(spans[:, 1, :], rows[:, :, :], AX_X, ALU.max).then_inc(spans_ready, 1)
            dve.wait_ge(spans_spread, 1)
            least = ps[0:NT, 6, 0:NCH]
            greatest = ps[0:NT, 7, 0:NCH]
            low = gconst[0:NT, C_LOW:C_LOW + 1]
            chain.step(dve.tensor_scalar(walk[:, 0:1], low, float(T - 1), None, ALU.add))
            chain.step(dve.tensor_scalar(near[:, 0, :], least, walk[:, 0:1], None, ALU.is_le))
            chain.step(dve.scalar_tensor_tensor(near[:, 0, :], greatest, low, near[:, 0, :], ALU.is_ge, ALU.mult))
            number = gconst[0:NT, C_CHUNK:C_CHUNK + NCH]
            chain.step(dve.scalar_tensor_tensor(near[:, 1, :], near[:, 0, :], -1000.0, number, ALU.mult, ALU.add))
            chain.step(dve.tensor_reduce(walk[:, 1:2], near[:, 1, :], AX_X, ALU.min))
            chain.step(dve.tensor_scalar(walk[:, 2:3], walk[:, 1:2], 1000.0, float(NCH - 1), ALU.add, ALU.min))
            chain.step(dve.scalar_tensor_tensor(near[:, 1, :], number, 1.0, near[:, 0, :], ALU.add, ALU.mult))
            chain.step(dve.tensor_reduce(walk[:, 3:4], near[:, 1, :], AX_X, ALU.max))
            chain.step(dve.scalar_tensor_tensor(walk[:, 4:5], walk[:, 3:4], 4.0, walk[:, 2:3], ALU.add, ALU.subtract))
            chain.step(dve.tensor_scalar(walk[:, 5:6], walk[:, 4:5], 8.0, None, ALU.max))
            chain.step(dve.tensor_copy(walk_i[:, :], walk[:, 5:6]))
            chain.step(dve.tensor_scalar(walk_i[:, :], walk_i[:, :], 2, None, ALU.logical_shift_right))
            dve.tensor_copy(walk[:, 6:7], walk_i[:, :]).then_inc(walk_ready, 1)
            dve.wait_ge(walk_turned, 1)
            dve.tensor_copy(plan[:, :], ps[0:1, 5, 0:3 * NT]).then_inc(plan_ready, 1)

            for g in range(NT // 2):
                for par in range(2):
                    dve.wait_ge(x_in[par], 16 * g + 16)
                    stats_of(dve, chain, par, xb[:, par, :], var_ready)
                for par in range(2):
                    dve.wait_ge(std_ready, 2 * g + par + 1)
                    chain.step(dve.reciprocal(rstd[:, par:par + 1], std[:, par:par + 1]))
                    dve.tensor_scalar(xb[:, par, :], xb[:, par, :], mv[:, par, 0:1], rstd[:, par:par + 1],
                                      ALU.subtract, ALU.mult).then_inc(xn_ready, 1)
                for par in range(2):
                    t = 2 * g + par
                    dve.wait_ge(hi_ready, t + 1)
                    dve.scalar_tensor_tensor(xT_lo[:, :, ds(t, 1), 0:T], turned_view(par), SX,
                                             xT_hi[:, :, ds(t, 1), 0:T], ALU.mult, ALU.subtract)\
                        .then_inc(lo_ready, 1)

            dve.wait_ge(plan_ready, 1)

            def one_hot(s, column, b):
                dve.tensor_scalar(hot_src[s], iota16[:, 0:N], edges[:, 0, ds(column, 1)], None, ALU.is_equal)
                dve.tensor_scalar(hot_dst[s], iota16[:, ds(b * T, PITCH)], edges[:, 1, ds(column, 1)], None,
                                  ALU.is_equal).then_inc(hot_ready, 1)

            def a_low(b, par):
                dve.wait_ge(a_hi_ready, b + 1)
                for first, n in GROUPS:
                    into = aT_lo[:, ds(b, 1), first:first + n, 0:T]
                    sums = ps[0:T, 3 * par + first // 4, 0:n * T].rearrange("p (a b c) -> p a b c", a=1, b=n)
                    last = dve.tensor_tensor(into, sums, aT_hi[:, ds(b, 1), first:first + n, 0:T], ALU.subtract)
                last.then_inc(a_lo_ready, 1)

            with dve.Fori(0, NT // 2) as g:
                for par in range(2):
                    b = 2 * g + par
                    first = dve.value_load(plan[0:1, ds(b, 1)], min_val=0, max_val=NCH - 1)
                    rounds = dve.value_load(plan[0:1, ds(NT + b, 1)], min_val=2, max_val=NCH // 4 + 1)
                    before = dve.value_load(plan[0:1, ds(2 * NT + b, 1)], min_val=0, max_val=NT * (NCH // 4 + 1))
                    for s in range(4):
                        dve.wait_ge(hot_used[s], before)
                        one_hot(s, first + (s - 1) if s else b + SELF, b)
                    with dve.Fori(1, rounds) as i:
                        for s in range(4):
                            column = nc.s_assert_within(
                                first + 4 * i + (s - 1), 0, SELF - 1,
                                skip_runtime_bounds_check_because="rounds ends at most 3 chunks after the last")
                            dve.wait_ge(hot_used[s], before + i)
                            one_hot(s, column, b)
                    a_low(b, par)

            dve.wait_ge(deg_root, 1)
            chain.step(dve.reciprocal(dis[:, 0, :], deg[:, :]))
            dve.tensor_scalar(dis[:, 1, :], dis[:, 0, :], SX, None, ALU.mult)
            chain.step(dve.tensor_scalar(dis[:, 2, :], dis[:, 0, :], 1.0 / SX, None, ALU.mult))
            dve.sem_inc(dis_ready, 1)

            dve.wait_ge(bias_in, 16)
            with dve.Fori(0, NT // 2) as g:
                for par in range(2):
                    t = 2 * g + par
                    dve.wait_ge(h_ready, t + 1)
                    dve.wait_ge(h_lo_ready, 2 * g)
                    dve.scalar_tensor_tensor(xb[:, par, :], ps[0:T, 2 * par:2 * par + 2, :].rearrange("p a b -> p (a b)"),
                                             1.0 / (SX * SW), bias_g[:, :], ALU.mult, ALU.add).then_inc(hb_ready, 1)
                for par in range(2):
                    t = 2 * g + par
                    dve.wait_ge(h_hi_ready, t + 1)
                    dve.scalar_tensor_tensor(h_lo[:, ds(t, 1), :].rearrange("p a b -> p (a b)"), xb[:, par, :],
                                             dis[:, 1, ds(t, 1)], h_hi[:, ds(t, 1), :].rearrange("p a b -> p (a b)"),
                                             ALU.mult, ALU.subtract).then_inc(h_lo_ready, 1)

            for g in range(NT // 2):
                for par in range(2):
                    t = 2 * g + par
                    dve.wait_ge(x_in[par], 16 * (NT // 2) + 16 * g + 16)
                    dve.wait_ge(agg_ready, t + 1)
                    dve.scalar_tensor_tensor(
                        xb[:, par, :], ps[0:T, 2 * par:2 * par + 2, :].rearrange("p a b -> p (a b)"),
                        dis[:, 2, ds(t, 1)], xb[:, par, :], ALU.mult, ALU.add).then_inc(x1_ready, 1)
                    dve.wait_ge(x1_ready, t + 1)
                    stats_of(dve, chain, par, xb[:, par, :], var_ready)
                for par in range(2):
                    t = 2 * g + par
                    dve.wait_ge(std_ready, NT + t + 1)
                    chain.step(dve.reciprocal(rstd[:, par:par + 1], std[:, par:par + 1]))
                    dve.wait_ge(turned, NT + 2 * g)
                    dve.wait_ge(acc_ready, 2 * g)
                    dve.tensor_scalar(xn[:, par, :], xb[:, par, :], mv[:, par, 0:1], rstd[:, par:par + 1],
                                      ALU.subtract, ALU.mult).then_inc(xn_ready, 1)
                for par in range(2):
                    t = 2 * g + par
                    dve.wait_ge(hi_ready, NT + t + 1)
                    dve.scalar_tensor_tensor(xT_lo[:, :, ds(t, 1), 0:T], turned_view(par, 4), SX,
                                             xT_hi[:, :, ds(t, 1), 0:T], ALU.mult, ALU.subtract)\
                        .then_inc(lo_ready, 1)

            groups = NT * 2 * H
            sig8, a8, b8 = (buf[:, :, :].rearrange("p t (g e) -> p (t g) e", e=EX) for buf in (sig, pick_a, pick_b))
            rev8 = consts[0:T, C_REV:C_REV + EX].unsqueeze(1).to_broadcast([T, groups, EX])

            def spread(j):
                return best[:, j, :].unsqueeze(2).to_broadcast([T, groups, EX])

            dve.wait_ge(exp_ready, NT)
            chain.step(dve.tensor_scalar(sig[:, :, :], sig[:, :, :], 1.0, None, ALU.add))
            chain.step(dve.reciprocal(sig[:, :, :], sig[:, :, :]))

            def choose(values, into, other):
                chain.step(dve.tensor_reduce(best[:, 0, :], values, AX_X, ALU.max))
                chain.step(dve.tensor_tensor(other, values, spread(0), ALU.is_equal))
                chain.step(dve.tensor_tensor(other, other, rev8, ALU.mult))
                chain.step(dve.tensor_reduce(best[:, 1, :], other, AX_X, ALU.max))
                chain.step(dve.tensor_tensor(into, other, spread(1), ALU.is_equal))

            choose(sig8, a8, b8)
            chain.step(dve.scalar_tensor_tensor(b8, a8, -4.0, sig8, ALU.mult, ALU.add))
            chain.step(dve.tensor_reduce(best[:, 0, :], b8, AX_X, ALU.max))
            chain.step(dve.tensor_tensor(b8, b8, spread(0), ALU.is_equal))
            chain.step(dve.tensor_tensor(b8, b8, rev8, ALU.mult))
            chain.step(dve.tensor_reduce(best[:, 1, :], b8, AX_X, ALU.max))
            chain.step(dve.tensor_tensor(b8, b8, spread(1), ALU.is_equal))
            chain.step(dve.tensor_tensor(a8, a8, b8, ALU.add))
            chain.step(dve.tensor_tensor(sig8, sig8, a8, ALU.mult))
            dve.tensor_copy(gv[:, :, :], sig[:, :, 0:H * EX]).then_inc(gates_ready, 1)
            for first, n in GROUPS:
                dve.wait_ge(go_turned, NT)
                last = dve.tensor_copy(goT[:, first:first + n, :],
                                       ps[:, 4 + first // 4, 0:n * T].rearrange("p (a b) -> p a b", a=n))
            last.then_inc(goT_ready, 1)

            for par in range(2):
                dve.wait_ge(x1_out[par], 16 * (NT // 2))
            dve.wait_ge(rope_in, 16)
            dve.wait_ge(goT_out, 16)
            dve.wait_ge(att_pads, 12)
            dve.sem_inc(og_pair_ready, 2)
            with dve.Fori(0, H) as h:
                def rotate(i):
                    par = i % 2
                    qk = qk32[:, par, :, :]
                    half = NROT // 2

                    def table(first, n):
                        return rope[:, i:i + 1, first:first + n].to_broadcast([T, 2, n])

                    dve.wait_ge(qk_pass, NT * h + i + 1)
                    if i:
                        dve.wait_ge(rope_ready, NT * h + i)
                    dve.tensor_tensor(rot[:, 0, :, :], qk[:, :, 0:NROT], table(0, NROT), ALU.mult)
                    dve.tensor_tensor(rot[:, 1, :, 0:half], qk[:, :, half:NROT], table(NROT, half), ALU.mult)
                    chain.step(dve.tensor_tensor(rot[:, 1, :, half:NROT], qk[:, :, 0:half], table(NROT + half, half),
                                                 ALU.mult))
                    dve.tensor_tensor(qk32[:, par, :, 0:NROT], rot[:, 0, :, :], rot[:, 1, :, :], ALU.add)\
                        .then_inc(rope_ready, 1)

                def values(i):
                    par = i % 2
                    dve.wait_ge(values_ready, NT * h + i + 1)
                    gate = gv[:, i:i + 1, ds(EX * h, EX)].rearrange("p o e -> p (o e)").unsqueeze(2)
                    chain.step(dve.tensor_tensor(vprod[:, :, :], ps[0:T, values_bank(i), :].rearrange("p (e c) -> p e c", e=EX),
                                                 gate.to_broadcast([T, EX, P]), ALU.mult))
                    dve.tensor_reduce(v32[:, par, :], vprod[:, :, :].rearrange("p e c -> p c e"), AX_X, ALU.add)\
                        .then_inc(v32_ready, 1)

                def low_qk(i):
                    par = i % 2
                    dve.wait_ge(tok_hi, NT * h + i + 1)
                    dve.tensor_tensor(columns(tok[:, i, :], Q_LO, K_LO, P), qk32[:, par, :, :],
                                      columns(tok[:, i, :], Q_HI, K_HI, P), ALU.subtract).then_inc(tok_ready, 1)

                def low_values(i):
                    dve.wait_ge(vt_hi, NT * h + i + 1)
                    dve.scalar_tensor_tensor(vt[:, i, 0:P], v32[:, i % 2, :], SQ / (SX * SW), vt[:, i, P:2 * P],
                                             ALU.mult, ALU.subtract).then_inc(vt_ready, 1)

                def take_kb(i):
                    dve.wait_ge(qkT_ready, NT * h + i + 1)
                    dve.tensor_copy(kb[0:P, i, 0:T], ps16[0:P, 4 + i % 2, 2 * PITCH:2 * PITCH + T]).then_inc(kb_ready, 1)

                def row_max(i):
                    dve.wait_ge(smax_ready, NT * h + i + 1)
                    chain.done(dve.tensor_reduce(mx[:, 0:1], ps[0:T, 0:2, 0:4 * T], mybir.AxisListType.XY, ALU.max))
                    chain.step(dve.tensor_reduce(mx[:, 1:2], ps[0:T, 2, 0:2 * T], AX_X, ALU.max))
                    dve.tensor_scalar(tok[:, i, MAXC:MAXC + 1], mx[:, 0:1], mx[:, 1:2], -1.0 / SM, ALU.max, ALU.mult)\
                        .then_inc(max_ready, 1)

                def p_low(j, u):
                    dve.wait_ge(exp_done, KU * NCK * h + KU * j + u + 1)
                    dve.tensor_tensor(pT_lo[:, j % 2, 2 * u:2 * u + 2, :, 0:T], p_block(j, u),
                                      pT_hi[:, j % 2, 2 * u:2 * u + 2, :, 0:T], ALU.subtract).then_inc(plo_ready, 1)

                def add_out(j, n):
                    dve.wait_ge(o_ready, output_count(h, j, n) + 1)
                    into = acc[:, CH * j + n // 2, (n % 2) * HALF:(n % 2 + 1) * HALF]
                    dve.scalar_tensor_tensor(into, ps[0:T, 6 + n % 2, :], 1.0 / (SQ * SW), into, ALU.mult, ALU.add)\
                        .then_inc(acc_added, 1)

                def sums(j):
                    values = ps[0:T, AV, 0:OT].rearrange("p (s c) -> p s c", s=CH)
                    dve.wait_ge(av_ready, NCK * h + j + 1)
                    dve.reciprocal(rsum[:, :], values[:, :, 2 * P:2 * P + 1].rearrange("p s o -> p (s o)"))\
                        .then_inc(rs_ready, 1)
                    dve.wait_ge(opart_ready, NCK * h + j + 1)
                    for a in range(CH):
                        chain.done(dve.scalar_tensor_tensor(o32[:, a, 0, :], values[:, a, P:2 * P], rsum[:, a:a + 1],
                                                            o_part[:, a, :], ALU.mult, ALU.add))
                    chain.wait()
                    dve.tensor_copy(o32[:, :, 1, :], o32[:, :, 0, :]).then_inc(o32_ready, 1)

                def gated(j):
                    dve.wait_ge(ot_ready, NCK * h + j + 1)
                    dve.wait_ge(go_in[j % 2], 32 * (((NCK + 1 - j % 2) // 2) * h + j // 2 + 1))
                    oT = ps[:, AV, OT:OT + CHN].unsqueeze(1).to_broadcast([128, PAIRS, CHN])
                    dve.tensor_tensor(og32[:, :, :], go_b[:, j % 2, :, :], oT, ALU.mult).then_inc(og_ready, 1)
                    dve.wait_ge(og_hi_ready, NCK * h + j + 1)
                    dve.tensor_tensor(og_lo[:, j % 2, :, :, 0:T], og32[:, :, :].rearrange("p a (s c) -> p a s c", s=CH),
                                      og_hi[:, j % 2, :, :, 0:T], ALU.subtract).then_inc(og_pair_ready, 1)

                chain.enter(h, NT * 2 + NT * 2 + NCK * 2)
                for what, j, n in head_order():
                    if what == "project":
                        if n < NT:
                            rotate(n)
                        if n >= 1:
                            low_qk(n - 1)
                    if what == "values":
                        values(n)
                        if n >= 1:
                            low_values(n - 1)
                        if n == NT - 1:
                            low_values(n)
                    if what == "turn":
                        take_kb(n)
                    if what == "rough":
                        row_max(n)
                    if what == "weights":
                        p_low(j, n)
                    if what == "normalise":
                        sums(j)
                    if what == "turn outputs":
                        gated(j)
                    if what == "output":
                        add_out(j, n)
            chain.leave(H)
            for j in (3, 4):
                for n in range(2 * CH):
                    dve.wait_ge(o_ready, output_count(H, j, n) + 1)
                    into = acc[:, CH * j + n // 2, (n % 2) * HALF:(n % 2 + 1) * HALF]
                    dve.scalar_tensor_tensor(into, ps[0:T, 6 + n % 2, :], 1.0 / (SQ * SW), into, ALU.mult, ALU.add)\
                        .then_inc(acc_added, 1)

            def normed(t, tile, count, gain, shift):
                par = t % 2
                dve.wait_ge(std_ready, count + t + 1)
                chain.step(dve.reciprocal(rstd[:, par:par + 1], std[:, par:par + 1]))
                chain.step(dve.tensor_scalar(tile, tile, mv[:, par, 0:1], rstd[:, par:par + 1], ALU.subtract, ALU.mult))
                chain.step(dve.tensor_tensor(tile, tile, vecs[:, gain, :], ALU.mult))
                return dve.tensor_tensor(tile, tile, vecs[:, shift, :], ALU.add)

            dve.wait_ge(acc_added, PER_HEAD * H + LATE)
            dve.wait_ge(vecs_in, 16)
            dve.wait_ge(b1_in, 16)
            dve.tensor_scalar(b1c[:, :], b1c[:, :], SQ, None, ALU.mult).then_inc(b1_ready, 1)
            for g in range(NT // 2):
                for par in range(2):
                    stats_of(dve, chain, par, acc[:, 2 * g + par, :], var_ready)
                for par in range(2):
                    t = 2 * g + par
                    normed(t, acc[:, t, :], 2 * NT, 0, 1).then_inc(y_ready, 1)
                for par in range(2):
                    t = 2 * g + par
                    dve.wait_ge(hi_ready, 2 * NT + t + 1)
                    dve.scalar_tensor_tensor(xT_lo[:, :, t:t + 1, 0:T], turned_view(par), SX,
                                             xT_hi[:, :, t:t + 1, 0:T], ALU.mult, ALU.subtract).then_inc(lo_ready, 1)
            for n, (first, tiles, f) in enumerate(hidden()):
                dve.wait_ge(h_hi2_ready, n + 1)
                dve.tensor_tensor(hT_lo[:, f, first:first + tiles, 0:T],
                                  h32[:, n % 2, 0:tiles * T].rearrange("p (a b) -> p a b", a=tiles),
                                  hT_hi[:, f, first:first + tiles, 0:T], ALU.subtract).then_inc(h_lo2_ready, 1)
            for g in range(NT // 2):
                for par in range(2):
                    t = 2 * g + par
                    dve.wait_ge(z_ready, t + 1)
                    if g:
                        dve.wait_ge(fin_out[par], 16 * g)
                    chain.step(dve.scalar_tensor_tensor(fin[:, par, :], flat(ps[0:T, 4 + 2 * par:6 + 2 * par, :]),
                                                        1.0 / (SQ * SW), acc[:, t, :], ALU.mult, ALU.add))
                    chain.step(dve.tensor_tensor(fin[:, par, :], fin[:, par, :], vecs[:, 2, :], ALU.add))
                    stats_of(dve, chain, par, fin[:, par, :], var_ready)
                for par in range(2):
                    t = 2 * g + par
                    chain.step(normed(t, fin[:, par, :], 3 * NT, 3, 4))
                    dve.wait_ge(x1_in[par], 16 * (g + 1))
                    dve.tensor_tensor(fin[:, par, :], fin[:, par, :], x1b[:, par, :], ALU.add).then_inc(fin_ready, 1)

        @block.scalar
        def _(act):
            with act.Fori(0, NT // 2) as g:
                for par in range(2):
                    act.wait_ge(var_ready, 2 * g + par + 1)
                    act.activation(std[:, par:par + 1], var[:, par:par + 1], ACT.Sqrt).then_inc(std_ready, 1)
                for par in range(2):
                    t = 2 * g + par
                    act.wait_ge(turned, t + 1)
                    act.activation(xT_hi[:, :, ds(t, 1), 0:T], turned_view(par), ACT.Copy, scale=SX)\
                        .then_inc(hi_ready, 1)
            act.wait_ge(plan_ready, 1)
            with act.Fori(0, NT // 2) as g:
                for par in range(2):
                    b = 2 * g + par
                    rounds = act.value_load(plan[0:1, ds(NT + b, 1)], min_val=2, max_val=NCH // 4 + 1)
                    before = act.value_load(plan[0:1, ds(2 * NT + b, 1)], min_val=0, max_val=NT * (NCH // 4 + 1))
                    act.wait_ge(hot_used[3], before + rounds)
                    for first, n in GROUPS:
                        sums = ps[0:T, 3 * par + first // 4, 0:n * T].rearrange("p (a b c) -> p a b c", a=1, b=n)
                        last = act.activation(aT_hi[:, ds(b, 1), first:first + n, 0:T], sums, ACT.Copy)
                    last.then_inc(a_hi_ready, 1)
            act.wait_ge(deg_ready, 1)
            act.activation(deg[:, :], ps[0:T, 6, 0:NT], ACT.Sqrt).then_inc(deg_root, 1)
            act.wait_ge(dis_ready, 1)
            with act.Fori(0, NT // 2) as g:
                for par in range(2):
                    t = 2 * g + par
                    act.wait_ge(hb_ready, t + 1)
                    act.activation(h_hi[:, ds(t, 1), :].rearrange("p a b -> p (a b)"), xb[:, par, :], ACT.Copy,
                                   scale=dis[:, 1, ds(t, 1)]).then_inc(h_hi_ready, 1)
            with act.Fori(0, NT // 2) as g:
                for par in range(2):
                    act.wait_ge(var_ready, NT + 2 * g + par + 1)
                    act.activation(std[:, par:par + 1], var[:, par:par + 1], ACT.Sqrt).then_inc(std_ready, 1)
                for par in range(2):
                    t = 2 * g + par
                    act.wait_ge(turned, NT + t + 1)
                    act.activation(xT_hi[:, :, ds(t, 1), 0:T], turned_view(par, 4), ACT.Copy, scale=SX)\
                        .then_inc(hi_ready, 1)

            with act.Fori(0, NT // 2) as g:
                for par in range(2):
                    t = 2 * g + par
                    act.wait_ge(logits_ready, t + 1)
                    act.activation(flat(sig[:, ds(t, 1), :]), ps[0:T, par, 0:2 * H * EX], ACT.Exp, scale=-1.0 / (SX * SW))\
                        .then_inc(exp_ready, 1)
            act.wait_ge(goT_ready, 1)
            for par in range(2):
                act.wait_ge(x1_out[par], 16 * (NT // 2))
            act.dma_start(goT_dram, flat(goT[:, :, :])).then_inc(goT_out, 16)
            act.wait_ge(goT_out, 16)

            with act.Fori(0, H) as h:
                def load_gates(j):
                    for e in range(2):
                        rows = goT_dram[ds(EX * h, EX), CHN * j:CHN * (j + 1)].rearrange("(k e) n -> e k n", e=2)[e]
                        act.dma_start(go_b[P * e:P * (e + 1), j % 2, :, :], rows.partition_broadcast(P))\
                            .then_inc(go_in[j % 2], 16)

                act.wait_ge(og_ready, NCK * h)
                load_gates(0)
                load_gates(1)

                def take_qk(i):
                    par = i % 2
                    qk = ps[0:T, 2 + par, 0:2 * P].rearrange("p (a c) -> p a c", a=2)
                    act.wait_ge(proj_ready, NT * h + i + 1)
                    act.wait_ge(tok_ready, NT * h + max(i - 1, 0))
                    act.activation(qk32[:, par, :, :], qk, ACT.Copy, scale=SQ / (SX * SW))\
                        .then_inc(qk_pass, 1)

                def high_halves(i):
                    par = i % 2
                    act.wait_ge(rope_ready, NT * h + i + 1)
                    act.wait_ge(qm_turned, NCK * h)
                    act.activation(columns(tok[:, i, :], Q_HI, K_HI, P), qk32[:, par, :, :], ACT.Copy)
                    act.activation(tok[:, i, K_HI2:K_HI2 + P], qk32[:, par, 1, :], ACT.Copy).then_inc(tok_hi, 1)

                def high_values(i):
                    act.wait_ge(v32_ready, NT * h + i + 1)
                    act.wait_ge(av_ready, NCK * h)
                    act.activation(vt[:, i, P:2 * P], v32[:, i % 2, :], ACT.Copy, scale=SQ / (SX * SW)).then_inc(vt_hi, 1)

                def take_qkT(i):
                    act.wait_ge(tr_ready, NT * h + i + 1)
                    act.activation(qkT[:, :, i, 0:T], ps16[:, 4 + i % 2, 0:2 * PITCH]
                                   .rearrange("p (a c) -> p a c", a=2)[:, :, 0:T], ACT.Copy).then_inc(qkT_ready, 1)

                def exps(j, u):
                    n = KU * j + u
                    act.wait_ge(st_ready, KU * NCK * h + n + 1)
                    act.wait_ge(plo_ready, KU * NCK * h + max(n - 1, 0))
                    if u == 0:
                        act.wait_ge(av_ready, NCK * h + max(j - 1, 0))
                    scores = ps[0:T, 3 + n % 2, 0:2 * CHN]
                    act.activation(p32[:, n % 2, :], scores, ACT.Exp, bias=consts[0:T, C_LNP:C_LNP + 1],
                                   scale=1.0 / (SQ * SQ * P ** 0.5))
                    act.activation(pT_hi[:, j % 2, 2 * u:2 * u + 2, :, 0:T],
                                   scores.rearrange("p (t s c) -> p t s c", t=2, s=CH), ACT.Exp,
                                   bias=consts[0:T, C_LNP:C_LNP + 1], scale=1.0 / (SQ * SQ * P ** 0.5))\
                        .then_inc(exp_done, 1)

                def take_maxima(j):
                    act.wait_ge(qm_turned, NCK * h + j + 1)
                    act.activation(qb[:, CH * j:CH * (j + 1), 0:T], ps16[0:P + 1, 2, QM:QM + CH * PITCH]
                                   .rearrange("p (a c) -> p a c", a=CH)[:, :, 0:T], ACT.Copy).then_inc(qb_ready, 1)

                def part_of_sums(j):
                    values = ps[0:T, AV, 0:OT].rearrange("p (s c) -> p s c", s=CH)
                    act.wait_ge(rs_ready, NCK * h + j + 1)
                    for a in range(CH):
                        last = act.activation(o_part[:, a, :], values[:, a, 0:P], ACT.Copy, scale=rsum[:, a:a + 1])
                    last.then_inc(opart_ready, 1)

                def gated(j):
                    act.wait_ge(og_ready, NCK * h + j + 1)
                    act.wait_ge(o_ready, output_count(h, j - 2, 0) + 2 * CH if j >= 2 else PER_HEAD * h + LATE)
                    act.activation(og_hi[:, j % 2, :, :, 0:T], og32[:, :, :].rearrange("p a (s c) -> p a s c", s=CH),
                                   ACT.Copy).then_inc(og_hi_ready, 1)
                    if j + 2 < NCK:
                        load_gates(j + 2)

                for what, j, n in head_order():
                    if what == "project":
                        if n < NT:
                            take_qk(n)
                        if n >= 1:
                            high_halves(n - 1)
                    if what == "values":
                        high_values(n)
                    if what == "turn":
                        take_qkT(n)
                    if what == "turn maxima":
                        take_maxima(j)
                    if what == "weights":
                        exps(j, n)
                    if what == "normalise":
                        part_of_sums(j)
                    if what == "turn outputs":
                        gated(j)

            for g in range(NT // 2):
                for par in range(2):
                    act.wait_ge(var_ready, 2 * NT + 2 * g + par + 1)
                    act.activation(std[:, par:par + 1], var[:, par:par + 1], ACT.Sqrt).then_inc(std_ready, 1)
                for par in range(2):
                    t = 2 * g + par
                    act.wait_ge(turned, 2 * NT + t + 1)
                    act.activation(xT_hi[:, :, t:t + 1, 0:T], turned_view(par), ACT.Copy, scale=SX).then_inc(hi_ready, 1)
            act.wait_ge(b1_ready, 1)
            for n, (first, tiles, f) in enumerate(hidden()):
                act.wait_ge(hs_ready, n + 1)
                if n >= 2:
                    act.wait_ge(h_lo2_ready, n - 1)
                product = ps[:, 4 + n % 4, 0:tiles * T]
                act.activation(h32[:, n % 2, 0:tiles * T], product, ACT.Relu, bias=b1c[:, f:f + 1],
                               scale=SQ / (SX * SW))
                act.activation(hT_hi[:, f, first:first + tiles, 0:T], product.rearrange("p (a b) -> p a b", a=tiles),
                               ACT.Relu, bias=b1c[:, f:f + 1], scale=SQ / (SX * SW)).then_inc(h_hi2_ready, 1)
            for t in range(NT):
                act.wait_ge(var_ready, 3 * NT + t + 1)
                act.activation(std[:, t % 2:t % 2 + 1], var[:, t % 2:t % 2 + 1], ACT.Sqrt).then_inc(std_ready, 1)

        @block.tensor
        def _(pe):
            pe.wait_ge(const_in, 32)
            pe.wait_ge(spans_ready, 1)
            n_rows = NCH // CPR
            for a in range(2):
                for j in range(CPR):
                    last = pe.matmul(ps[0:NT, 6 + a, j * n_rows:(j + 1) * n_rows],
                                     spans[:, a, j:j + 1].to_broadcast([n_rows, NT]),
                                     gconst[0:n_rows, C_ID10:C_ID10 + n_rows], start=True, stop=True)
            last.then_inc(spans_spread, 1)
            pe.wait_ge(walk_ready, 1)
            pe.matmul(ps[0:1, 5, 0:NT], walk[:, 2:3], gconst[0:NT, C_ID10:C_ID10 + NT], start=True, stop=True)
            pe.matmul(ps[0:1, 5, NT:2 * NT], walk[:, 6:7], gconst[0:NT, C_ID10:C_ID10 + NT], start=True, stop=True)
            pe.matmul(ps[0:1, 5, 2 * NT:3 * NT], walk[:, 6:7], gconst[0:NT, C_UPPER:C_UPPER + NT],
                      start=True, stop=True).then_inc(walk_turned, 1)

            with pe.Fori(0, NT // 2) as g:
                for par in range(2):
                    t = 2 * g + par
                    pe.wait_ge(xn_ready, t + 1)
                    pe.wait_ge(lo_ready, 2 * g)
                    for k in range(KD):
                        last = pe.transpose(ps[:, 2 * par + k // 4, (k % 4) * PITCH:(k % 4) * PITCH + T],
                                            xb[:, par, k * 128:(k + 1) * 128], ident[0:T, 0:T])
                    last.then_inc(turned, 1)

            pe.wait_ge(lo_ready, NT)
            pe.wait_ge(plan_ready, 1)

            def count(s, par, start, stop):
                for first, n in GROUPS:
                    last = pe.matmul(ps[:, 3 * par + first // 4, 0:n * T], hot_dst[s],
                                     hot_src[s][:, first * T:(first + n) * T], start=start, stop=stop,
                                     skip_group_check=True)
                last.then_inc(hot_used[s], 1)
                return last

            with pe.Fori(0, NT // 2) as g:
                for par in range(2):
                    b = 2 * g + par
                    rounds = pe.value_load(plan[0:1, ds(NT + b, 1)], min_val=2, max_val=NCH // 4 + 1)
                    before = pe.value_load(plan[0:1, ds(2 * NT + b, 1)], min_val=0, max_val=NT * (NCH // 4 + 1))
                    pe.wait_ge(a_lo_ready, 2 * g)
                    for s in range(4):
                        pe.wait_ge(hot_ready, 4 * before + s + 1)
                        count(s, par, s == 0, False)
                    with pe.Fori(1, rounds) as i:
                        for s in range(4):
                            pe.wait_ge(hot_ready, 4 * before + 4 * i + s + 1)
                            count(s, par, False, s == 3)

            pe.wait_ge(a_lo_ready, NT)
            pe.wait_ge(pads_ready, 5)
            for t in range(NT):
                for b in range(NT):
                    pe.matmul(ps[:, 6, t:t + 1], aT_hi[:, b, t, :], ones16[:, 0:1], start=(b == 0), stop=False)
                    last = pe.matmul(ps[:, 6, t:t + 1], aT_lo[:, b, t, :], ones16[:, 0:1], start=False,
                                     stop=(b == NT - 1))
            last.then_inc(deg_ready, 1)

            pe.wait_ge(wg_split, 1)
            with pe.Fori(0, NT // 2) as g:
                for par in range(2):
                    t = 2 * g + par
                    pe.wait_ge(hb_ready, 2 * g)
                    for k in range(KD):
                        for x_part, w_parts in ((xT_hi, (wg_hi, wg_lo)), (xT_lo, (wg_hi,))):
                            for w_part in w_parts:
                                for j in range(2):
                                    last = pe.matmul(ps[:, 2 * par + j, :], x_part[:, k, ds(t, 1), :].rearrange("p a b -> p (a b)"),
                                                     w_part[:, k, j * HALF:(j + 1) * HALF],
                                                     start=(k == 0 and x_part is xT_hi and w_part is wg_hi),
                                                     stop=(k == KD - 1 and x_part is xT_lo))
                    last.then_inc(h_ready, 1)

            pe.wait_ge(h_lo_ready, NT)
            with pe.Fori(0, NT // 2) as g:
                for par in range(2):
                    t = 2 * g + par
                    pe.wait_ge(x1_ready, 2 * g)
                    for b in range(NT):
                        for a_part, h_parts in ((aT_hi, (h_hi, h_lo)), (aT_lo, (h_hi,))):
                            for h_part in h_parts:
                                for j in range(2):
                                    last = pe.matmul(ps[:, 2 * par + j, :],
                                                     a_part[:, b, ds(t, 1), :].rearrange("p a b -> p (a b)"),
                                                     h_part[:, b, j * HALF:(j + 1) * HALF],
                                                     start=(b == 0 and a_part is aT_hi and h_part is h_hi),
                                                     stop=(b == NT - 1 and a_part is aT_lo))
                    last.then_inc(agg_ready, 1)
                for par in range(2):
                    t = 2 * g + par
                    pe.wait_ge(xn_ready, NT + t + 1)
                    pe.wait_ge(lo_ready, NT + 2 * g)
                    for k in range(KD):
                        last = pe.transpose(ps[:, 4 + 2 * par + k // 4, (k % 4) * PITCH:(k % 4) * PITCH + T],
                                            xn[:, par, k * 128:(k + 1) * 128], ident[0:T, 0:T])
                    last.then_inc(turned, 1)


            pe.wait_ge(sel_split, SPLIT * KD)
            pe.wait_ge(lo_ready, 2 * NT)
            with pe.Fori(0, NT // 2) as g:
                for par in range(2):
                    t = 2 * g + par
                    pe.wait_ge(exp_ready, 2 * g)
                    for k in range(KD):
                        for x_part, w_parts in ((xT_hi, (wsel_hi, wsel_lo)), (xT_lo, (wsel_hi,))):
                            for w_part in w_parts:
                                last = pe.matmul(ps[:, par, 0:2 * H * EX], flat(x_part[:, k, ds(t, 1), :]), w_part[:, k, :],
                                                 start=(k == 0 and x_part is xT_hi and w_part is wsel_hi),
                                                 stop=(k == KD - 1 and x_part is xT_lo))
                    last.then_inc(logits_ready, 1)
            pe.wait_ge(gates_ready, 1)
            for t in range(NT):
                pe.transpose(ps[:, 4 + t // 4, (t % 4) * T:(t % 4 + 1) * T], sig[:, t, H * EX:2 * H * EX], ident[0:T, 0:T])\
                    .then_inc(go_turned, 1)

            n_chunks = KD + PAIRS

            def output(h, j, n):
                if j == 0 and n == 0:
                    pe.wait_ge(v32_ready, NT * (h + 1))
                    pe.wait_ge(w_split, SPLIT * n_chunks * (h + 1))
                half, a = n % 2, n // 2
                pe.wait_ge(og_pair_ready, NCK * h + (j + 2) % NCK + 1)
                pe.wait_ge(acc_added, PER_HEAD * h + max(output_count(0, j, n) - 1, 0))
                for k in range(PAIRS):
                    for o_part_, w_parts in ((og_hi, (wo_hi, wo_lo)), (og_lo, (wo_hi,))):
                        for w_part in w_parts:
                            last = pe.matmul(ps[:, 6 + half, :], o_part_[:, j % 2, k, a, :],
                                             w_part[:, k, half * HALF:(half + 1) * HALF],
                                             start=(k == 0 and o_part_ is og_hi and w_part is wo_hi),
                                             stop=(k == PAIRS - 1 and o_part_ is og_lo))
                last.then_inc(o_ready, 1)

            pe.wait_ge(att_pads, 12)
            pe.wait_ge(goT_ready, 1)
            with pe.Fori(0, H) as h:
                def project(i):
                    if i >= 2:
                        pe.wait_ge(qk_pass, NT * h + i - 1)
                    for k in range(KD):
                        for x_part, w_parts in ((xT_hi, (wqkv_hi, wqkv_lo)), (xT_lo, (wqkv_hi,))):
                            for w_part in w_parts:
                                last = pe.matmul(ps[:, 2 + i % 2, 0:2 * P], x_part[:, k, i, :], w_part[:, k, 0:2 * P],
                                                 start=(k == 0 and x_part is xT_hi and w_part is wqkv_hi),
                                                 stop=(k == KD - 1 and x_part is xT_lo))
                    last.then_inc(proj_ready, 1)

                def values(i):
                    if i >= 2:
                        pe.wait_ge(v32_ready, NT * h + i - 1)
                    if i >= LATE_VALUES:
                        pe.wait_ge(acc_added, PER_HEAD * h + LATE - (1 if i == LATE_VALUES else 0))
                    for k in range(KD):
                        for x_part, w_parts in ((xT_hi, (wqkv_hi, wqkv_lo)), (xT_lo, (wqkv_hi,))):
                            for w_part in w_parts:
                                last = pe.matmul(ps[:, values_bank(i), :], x_part[:, k, i, :], w_part[:, k, 2 * P:WQKV],
                                                 start=(k == 0 and x_part is xT_hi and w_part is wqkv_hi),
                                                 stop=(k == KD - 1 and x_part is xT_lo))
                    last.then_inc(values_ready, 1)

                def turn(i):
                    bank = 4 + i % 2
                    pe.wait_ge(tok_ready, NT * h + i + 1)
                    if i == 1:
                        pe.wait_ge(og_ready, NCK * h)
                    if i >= 2:
                        pe.wait_ge(qkT_ready, NT * h + i - 1)
                        pe.wait_ge(kb_ready, NT * h + i - 1)
                    pe.transpose(ps16[:, bank, 0:T], tok[:, i, Q_LO:Q_LO + 2 * P], ident16[0:T, 0:T])
                    pe.transpose(ps16[:, bank, PITCH:PITCH + T], tok[:, i, K_HI:K_HI + 2 * P], ident16[0:T, 0:T])
                    pe.transpose(ps16[0:P, bank, 2 * PITCH:2 * PITCH + T], tok[:, i, K_LO:K_LO + P], ident16[0:T, 0:T])\
                        .then_inc(tr_ready, 1)

                def rough_scores(i):
                    pe.wait_ge(max_ready, NT * h + i)
                    if i == 0:
                        pe.wait_ge(v32_ready, NT * h + LATE_VALUES)
                        pe.wait_ge(qk_pass, NT * (h + 1))
                        pe.wait_ge(qkT_ready, NT * (h + 1))
                        pe.wait_ge(kb_ready, NT * (h + 1))
                    for first, n in GROUPS:
                        last = pe.matmul(ps[:, first // 4, 0:n * T], qkT[:, 0, i, :], qkT[:, 1, first:first + n, 0:T],
                                         start=True, stop=True)
                    last.then_inc(smax_ready, 1)

                def turn_maxima(j):
                    pe.wait_ge(max_ready, NT * h + CH * (j + 1))
                    pe.wait_ge(qb_ready, NCK * h + j)
                    for a in range(CH):
                        last = pe.transpose(ps16[0:P + 1, 2, QM + PITCH * a:QM + PITCH * a + T],
                                            tok[:, CH * j + a, Q_HI:MAXC + 1], ident16[0:T, 0:T])
                    last.then_inc(qm_turned, 1)

                def scores(j, u):
                    n = KU * j + u
                    pe.wait_ge(qb_ready, NCK * h + j + 1)
                    pe.wait_ge(exp_done, KU * NCK * h + max(n - 1, 0))
                    for a in range(2):
                        into = ps[:, 3 + n % 2, a * CHN:(a + 1) * CHN]
                        pe.matmul(into, qkT[:, 1, 2 * u + a, :], qkT[:, 0, CH * j:CH * (j + 1), 0:T], start=True, stop=False)
                        last = pe.matmul(into, kb[:, 2 * u + a, :], qb[:, CH * j:CH * (j + 1), 0:T], start=False, stop=True)
                    last.then_inc(st_ready, 1)

                def weigh(j, a):
                    pe.wait_ge(plo_ready, KU * NCK * h + KU * (j + 1))
                    pe.wait_ge(og_ready, NCK * h + j)
                    if j == 0:
                        pe.wait_ge(vt_ready, NT * (h + 1))
                    base = a * (2 * P + 1)
                    for t in range(NT):
                        both = [(pT_hi, 0), (pT_lo, P)]
                        for part, first in both if t < NT - 1 else both[::-1]:
                            last = pe.matmul(ps[:, AV, base + first:base + 2 * P + 1], part[:, j % 2, t, a, :],
                                             vt[:, t, first:2 * P + 1], start=(t == 0 and part is pT_hi),
                                             stop=(t == NT - 1 and part is pT_hi))
                    if a == CH - 1:
                        last.then_inc(av_ready, 1)

                def turn_outputs(j):
                    pe.wait_ge(o32_ready, NCK * h + j + 1)
                    for a in range(CH):
                        last = pe.transpose(ps[:, AV, OT + a * T:OT + (a + 1) * T], flat(o32[:, a, :, :]), ident[0:T, 0:T])
                    last.then_inc(ot_ready, 1)

                pe.wait_ge(w_split, SPLIT * n_chunks * h + SPLIT * KD)
                for what, j, n in head_order():
                    if what == "project" and n < NT:
                        project(n)
                    if what == "values":
                        values(n)
                    if what == "turn":
                        turn(n)
                    if what == "rough":
                        rough_scores(n)
                    if what == "turn maxima":
                        turn_maxima(j)
                    if what == "scores":
                        scores(j, n)
                    if what == "weigh":
                        weigh(j, n)
                    if what == "turn outputs":
                        turn_outputs(j)
                    if what == "output":
                        output(h, j, n)

            for j in (3, 4):
                for n in range(2 * CH):
                    output(H, j, n)

            for g in range(NT // 2):
                for par in range(2):
                    t = 2 * g + par
                    pe.wait_ge(y_ready, t + 1)
                    if g:
                        pe.wait_ge(lo_ready, 2 * NT + 2 * g)
                    for k in range(KD):
                        last = pe.transpose(ps[:, 2 * par + k // 4, (k % 4) * PITCH:(k % 4) * PITCH + T],
                                            acc[:, t, k * 128:(k + 1) * 128], ident[0:T, 0:T])
                    last.then_inc(turned, 1)
            pe.wait_ge(mlp_split, SPLIT * KD)
            for n, (first, tiles, f) in enumerate(hidden()):
                pe.wait_ge(lo_ready, 2 * NT + first + tiles)
                if n >= 4:
                    pe.wait_ge(h_hi2_ready, n - 3)
                for k in range(KD):
                    for w_part, x_parts in ((w1_hi, (xT_hi, xT_lo)), (w1_lo, (xT_hi,))):
                        for x_part in x_parts:
                            last = pe.matmul(ps[:, 4 + n % 4, 0:tiles * T], w_part[:, k, f * 128:(f + 1) * 128],
                                             x_part[:, k, first:first + tiles, 0:T],
                                             start=(k == 0 and w_part is w1_hi and x_part is xT_hi),
                                             stop=(k == KD - 1 and w_part is w1_lo))
                last.then_inc(hs_ready, 1)
            pe.wait_ge(att_pads, 14)
            pe.wait_ge(mlp_split, SPLIT * (KD + F // 128))
            pe.wait_ge(h_lo2_ready, len(hidden()))
            for t in range(NT):
                if t >= 2:
                    pe.wait_ge(var_ready, 3 * NT + t - 1)
                for k in range(F // 128):
                    for h_part, w_parts in ((hT_hi, (w2_hi, w2_lo)), (hT_lo, (w2_hi,))):
                        for w_part in w_parts:
                            for half in range(2):
                                last = pe.matmul(ps[:, 4 + 2 * (t % 2) + half, :], h_part[:, k, t, :],
                                                 w_part[:, k, half * HALF:(half + 1) * HALF],
                                                 start=(k == 0 and h_part is hT_hi and w_part is w2_hi),
                                                 stop=(k == F // 128 - 1 and h_part is hT_lo))
                last.then_inc(z_ready, 1)


def constants():
    import numpy as np

    kept = np.zeros((128, C_KEPT), np.float32)
    kept[:, C_ID:C_ID + 128] = np.eye(128)
    kept[:, C_REV:C_REV + EX] = np.arange(EX, 0, -1)
    kept[:, C_LNP] = np.log(SP_)
    c = np.zeros((128, CCOLS), np.float32)
    c[:, C_IOTA:C_IOTA + NT * PITCH] = np.arange(NT * PITCH)
    c[:, C_CHUNK:C_CHUNK + NCH] = np.arange(NCH).reshape(NCH // CPR, CPR).T.reshape(-1)
    c[:, C_SELF:C_SELF + NT] = np.arange(128)[:, None] + T * np.arange(NT)
    c[:, C_LOW] = T * np.arange(128)
    c[:, C_UPPER:C_UPPER + NT] = np.arange(128)[:, None] < np.arange(NT)
    c[:, C_ID10:] = np.eye(128)[:, 0:NCH // CPR]
    half = NROT // 2
    inv = np.float32(10000.0) ** (-np.arange(half, dtype=np.float32) / np.float32(half))
    angle = np.arange(N, dtype=np.float32)[:, None] * inv[None, :].astype(np.float32)
    cos, sin = np.cos(angle), np.sin(angle)
    rope = np.concatenate([cos, cos, -sin, sin], -1).astype(np.float32)
    return kept, c, rope.reshape(NT, T, 2 * NROT).transpose(1, 0, 2)


def kernel(**inputs):
    import numpy as np
    import concourse.bacc as bacc
    from concourse.bass_utils import run_bass_kernel_spmd

    def slabs(w):
        return np.ascontiguousarray(w.reshape(-1, 128, w.shape[-1]).transpose(1, 0, 2))

    nc = bacc.Bacc("TRN2", target_bir_lowering=False, num_devices=1)
    arrays, args = {}, []

    def give(name, a):
        a = np.ascontiguousarray(a)
        arrays[name] = a
        args.append(nc.dram_tensor(name, a.shape, mybir.dt.from_np(a.dtype), kind="ExternalInput").ap())

    give("x", inputs["x"])
    give("src", inputs["src"].reshape(NCH, T).T)
    give("dst", inputs["dst"].reshape(NCH, T).T)
    give("dst_rows", inputs["dst"].reshape(NCH // CPR, CPR, T))
    give("wg", slabs(inputs["L0_gnn_W"].T))
    give("bg", inputs["L0_gnn_b"])
    sel = np.concatenate([inputs["L0_ffn_Wsel_v"].reshape(H * EX, D), inputs["L0_ffn_Wsel_o"].reshape(H * EX, D)])
    give("wsel", slabs(sel.T))
    wv = inputs["L0_ffn_Wv"].transpose(0, 2, 1, 3).reshape(H, D, EX * P)
    qkv = np.concatenate([inputs["L0_ffn_Wq"], inputs["L0_ffn_Wk"], wv], -1)
    give("wqkv", qkv.reshape(H, KD, 128, WQKV).transpose(0, 2, 1, 3))
    give("wo", inputs["L0_ffn_Wo"].reshape(H, PAIRS, 128, D).transpose(0, 2, 1, 3))
    give("w1", slabs(inputs["L0_ffn_W1"]))
    give("b1", inputs["L0_ffn_b1"].reshape(F // 128, 128).T)
    give("w2", slabs(inputs["L0_ffn_W2"]))
    give("rowvecs", np.stack([inputs["L0_ffn_ln1_g"], inputs["L0_ffn_ln1_b"], inputs["L0_ffn_b2"],
                              inputs["L0_ffn_ln2_g"], inputs["L0_ffn_ln2_b"]]))
    kept, graph, rope = constants()
    give("ctab", kept)
    give("gtab", graph)
    give("rtab", rope)
    args.append(nc.dram_tensor("out", [N, D], F32, kind="ExternalOutput").ap())
    build(nc, *args)
    r = run_bass_kernel_spmd(nc, [arrays], core_ids=[0])
    return r.results[0]["out"]
```

```python
from contextlib import ExitStack

import concourse.bass as bass
from concourse import mybir

ALU = mybir.AluOpType
ACT = mybir.ActivationFunctionType
AX_X = mybir.AxisListType.X
F32 = mybir.dt.float32
F16 = mybir.dt.float16
I32 = mybir.dt.int32
ds = bass.ds

N = 1250
D = 1024
E_EDGES = 40000
H, P, EX, F = 16, 64, 8, 512
NROT = 32
EPS = 1e-5

T = 125
NT = N // T
PITCH = 128
KD = D // 128
NCH = E_EDGES // T
CPR = 4
SELF = NCH + 8
ECOLS = SELF + NT
HALF = D // 2
GROUPS = ((0, 4), (4, 4), (8, 2))

SX = 64.0
SW = 256.0

SQ = 16.0
SP_ = 1024.0
SM = 512.0
WQKV = (2 + EX) * P
PAIRS = EX // 2
CH = 2
NCK = NT // CH
KU = NT // 2
SPLIT = 3
ONE = 1
CHN = CH * T

Q_LO, Q_HI, MAXC, K_LO, K_HI, K_HI2, TOKW = 0, 64, 128, 132, 196, 260, 328

C_ID = 0
C_REV = 128
C_LNP = C_REV + EX
C_KEPT = C_LNP + 1
C_IOTA = 0
C_CHUNK = C_IOTA + NT * PITCH
C_SELF = C_CHUNK + NCH
C_LOW = C_SELF + NT
C_UPPER = C_LOW + 1
C_ID10 = C_UPPER + NT
CCOLS = C_ID10 + NCH // CPR


class Chain:

    def __init__(self, engine, sem):
        self.engine, self.sem, self.base, self.n = engine, sem, 0, 0

    def done(self, instruction):
        instruction.then_inc(self.sem, 1)
        self.n += 1

    def wait(self):
        self.engine.wait_ge(self.sem, self.base + self.n)

    def step(self, instruction):
        self.done(instruction)
        self.wait()

    def enter(self, i, per_round):
        self.saved, self.per_round = (self.base, self.n), per_round
        self.base, self.n = self.base + self.n + i * per_round, 0

    def leave(self, rounds):
        assert self.n == self.per_round, (self.n, self.per_round)
        base, n = self.saved
        self.base, self.n = base, n + rounds * self.per_round


def build(nc, x, src, dst, dst_rows, wg, bg, wsel, wqkv, wo, w1, b1, w2, rowvecs, ctab, gtab, rtab, out):
    ctx = ExitStack()

    def sb(name, shape, dt, where=None):
        return (where or ctx).enter_context(nc.sbuf_tensor(name, shape, dt))

    def sem(name):
        return ctx.enter_context(nc.semaphore(name))

    with ctx:
        ps = ctx.enter_context(nc.psum_tensor("ps", [128, 8, 512], F32))
        goT_dram = nc.dram_tensor("goT_dram", [H * EX, N], F32, kind="Internal").ap()
        x1_dram = nc.dram_tensor("x1_dram", [N, D], F32, kind="Internal").ap()

        consts = sb("consts", [128, C_KEPT], F32)
        xT_hi = sb("xT_hi", [128, KD, NT, PITCH], F16)
        xT_lo = sb("xT_lo", [128, KD, NT, PITCH], F16)
        arena = sb("arena", [128, NT * D], F32)
        stats = sb("stats", [T, 2, 2, 6], F32)
        mv = sb("mv", [T, 2, 2], F32)
        var = sb("var", [T, 2], F32)
        std = sb("std", [T, 2], F32)
        rstd = sb("rstd", [T, 2], F32)
        b1c = sb("b1c", [128, F // 128], F32)
        ident = consts[:, C_ID:C_ID + 128]
        ident16 = sb("ident16", [128, 128], F16)
        acc = arena[0:T, :].rearrange("p (t d) -> p t d", t=NT)
        wg_hi = arena[:, 0:KD * D // 2].bitcast(F16).rearrange("p (k d) -> p k d", k=KD)
        wg_lo = arena[:, KD * D // 2:KD * D].bitcast(F16).rearrange("p (k d) -> p k d", k=KD)
        w_stage = arena[:, KD * D:NT * D].rearrange("p (s d) -> p s d", s=2)

        gv = sb("gv", [T, NT, H * EX], F32)
        w_pair = arena[:, KD * D:NT * D]

        front = ExitStack()
        gconst = sb("gconst", [128, CCOLS], F32, front)
        bias_g = sb("bias_g", [T, D], F32, front)
        edges = sb("edges", [T, 2, ECOLS], F32, front)
        front.close()
        gates = ExitStack()
        wsel_hi = sb("wsel_hi", [128, KD, 2 * H * EX], F16, gates)
        wsel_lo = sb("wsel_lo", [128, KD, 2 * H * EX], F16, gates)
        sig = sb("sig", [T, 2, 2 * H * EX], F32, gates)
        pick_a = sb("pick_a", [T, 2 * H * EX], F32, gates)
        pick_b = sb("pick_b", [T, 2 * H * EX], F32, gates)
        best = sb("best", [T, 2, 2 * H], F32, gates)
        gates_rest = sb("gates_rest", [T, 320], F32, gates)
        sel_stage = w_pair.rearrange("p (k n) -> p k n", k=KD)
        go_keep = w_pair[0:T, 0:NT * H * EX].rearrange("p (t n) -> p t n", t=NT)

        gnn = ExitStack()
        aT_hi = sb("aT_hi", [T, NT, NT, PITCH], F16, gnn)
        aT_lo = sb("aT_lo", [T, NT, NT, PITCH], F16, gnn)
        h_hi = sb("h_hi", [T, NT, D], F16, gnn)
        h_lo = sb("h_lo", [T, NT, D], F16, gnn)
        xn = sb("xn", [T, 2, D], F32, gnn)
        spans = sb("spans", [NCH // CPR, 2, CPR], F32, gnn)
        walk = sb("walk", [NT, 8], F32, gnn)
        walk_i = sb("walk_i", [NT, 1], I32, gnn)
        plan = sb("plan", [1, 3 * NT], I32, gnn)
        deg = sb("deg", [T, NT], F32, gnn)
        dis = sb("dis", [T, 3, NT], F32, gnn)
        ones16 = sb("ones16", [T, 2], F16, gnn)
        many = sb("many", [T, NT], F16, gnn)
        blocks_f = sb("blocks_f", [1, 2], F32, gnn)
        blocks_i = sb("blocks_i", [1, 2], I32, gnn)
        xb = sb("xb", [T, 2, D], F32, gnn)
        edges_i = xn[:, 0, 0:2 * NCH].bitcast(I32).rearrange("p (a c) -> p a c", a=2)
        near = xn[0:NT, 0, 0:2 * NCH].rearrange("p (a c) -> p a c", a=2)
        rows_i = xn[0:NCH // CPR, 1, 0:CPR * T].bitcast(I32).rearrange("p (a c) -> p a c", a=CPR)
        rows = xn[0:NCH // CPR, 1, HALF:HALF + CPR * T].rearrange("p (a c) -> p a c", a=CPR)
        iota16 = h_hi[:, 0:2, :].rearrange("p a b -> p (a b)")[:, 0:NT * PITCH]
        hot_src = [h_hi[:, 2 + 2 * s:4 + 2 * s, :].rearrange("p a b -> p (a b)")[:, 0:N] for s in range(4)]
        hot_dst = [h_lo[:, s, 0:PITCH] for s in range(4)]
        gnn.close()
        gates.close()

        att = ExitStack()
        rope = sb("rope", [T, NT, 2 * NROT], F32, att)
        tok = sb("tok", [T, NT, TOKW], F16, att)
        vt = sb("vt", [T, NT, 2 * P + 2], F16, att)
        qk32 = sb("qk32", [T, 2, 2, P], F32, att)
        rot = sb("rot", [T, 2, 2, NROT], F32, att)
        vprod = sb("vprod", [T, EX, P], F32, att)
        v32 = sb("v32", [T, 2, P], F32, att)
        wqkv_hi = sb("wqkv_hi", [128, KD, WQKV], F16, att)
        wqkv_lo = sb("wqkv_lo", [128, KD, WQKV], F16, att)
        wo_hi = sb("wo_hi", [128, PAIRS, D], F16, att)
        wo_lo = sb("wo_lo", [128, PAIRS, D], F16, att)
        stage = sb("stage", [128, 2, D], F32, att)
        qkT = sb("qkT", [128, 2, NT, PITCH], F16, att)
        qb = sb("qb", [P + 1, NT, PITCH], F16, att)
        kb = sb("kb", [P + 1, NT, PITCH], F16, att)
        mx = sb("mx", [T, 2], F32, att)
        og_hi = sb("og_hi", [128, 2, PAIRS, CH, PITCH], F16, att)
        og_lo = sb("og_lo", [128, 2, PAIRS, CH, PITCH], F16, att)
        pT = sb("pT", [T, 2 * 2 * NT * CH * PITCH], F16, att)
        pT_hi, pT_lo = (pT[:, part * 2 * NT * CH * PITCH:(part + 1) * 2 * NT * CH * PITCH]
                        .rearrange("p (j t s c) -> p j t s c", j=2, t=NT, s=CH) for part in range(2))
        behind = ExitStack()
        p32 = sb("p32", [T, 2, 2 * CHN], F32, behind)
        go_b = sb("go_b", [128, 2, PAIRS, CHN], F32, behind)
        og32 = sb("og32", [128, PAIRS, CHN], F32, behind)
        rsum = sb("rsum", [T, CH], F32, behind)
        o_low = sb("o_low", [T, CH, P], F32, behind)
        o_sum = sb("o_sum", [T, CH, P], F32, behind)
        o32 = sb("o32", [T, CH, 2, P], F32, behind)
        goT = sb("goT", [128, NT, T], F32, behind)
        behind.close()
        hidden_stack = ExitStack()
        hT_hi = sb("hT_hi", [128, F // 128, NT, PITCH], F16, hidden_stack)
        hT_lo = sb("hT_lo", [128, F // 128, NT, PITCH], F16, hidden_stack)
        h32 = sb("h32", [128, 2, 4 * T], F32, hidden_stack)
        hidden_stack.close()
        att.close()

        w1_hi, w1_lo = (w[:, :, 0:F] for w in (wqkv_hi, wqkv_lo))
        w2_hi, w2_lo = wo_hi, wo_lo
        vecs = pT[:, 0:2 * 5 * D].bitcast(F32).rearrange("p (a d) -> p a d", a=5)
        x1b = [og[0:T].rearrange("p a b c d -> p (a b c d)").bitcast(F32) for og in (og_hi, og_lo)]
        low = ExitStack()
        fin = sb("fin", [T, 3, D], F32, low)
        low.close()

        const_in = sem("const_in")
        edges_in = sem("edges_in")
        bias_in = sem("bias_in")
        x_in = [sem("x_in0"), sem("x_in1")]
        wg_in = [sem("wg_in0"), sem("wg_in1")]
        wg_split = sem("wg_split")
        pool_chain = sem("pool_chain")
        dve_chain = sem("dve_chain")
        pads_ready = sem("pads_ready")
        spans_ready = sem("spans_ready")
        spans_spread = sem("spans_spread")
        walk_ready = sem("walk_ready")
        walk_turned = sem("walk_turned")
        plan_ready = sem("plan_ready")
        var_ready = sem("var_ready")
        std_ready = sem("std_ready")
        xn_ready = sem("xn_ready")
        turned = sem("turned")
        hi_ready = sem("hi_ready")
        lo_ready = sem("lo_ready")
        hot_ready = sem("hot_ready")
        rstd_ready = sem("rstd_ready")
        hot_used = [sem(f"hot_used{s}") for s in range(4)]
        a_hi_ready = sem("a_hi_ready")
        a_lo_ready = sem("a_lo_ready")
        deg_ready = sem("deg_ready")
        deg_root = sem("deg_root")
        dis_ready = sem("dis_ready")
        h_ready = sem("h_ready")
        hb_ready = sem("hb_ready")
        h_hi_ready = sem("h_hi_ready")
        h_lo_ready = sem("h_lo_ready")
        agg_ready = sem("agg_ready")
        x1_ready = sem("x1_ready")
        acc_ready = sem("acc_ready")
        x1_out = [sem("x1_out0"), sem("x1_out1")]

        sel_split = sem("sel_split")
        rope_in = sem("rope_in")
        logits_ready = sem("logits_ready")
        exp_ready = sem("exp_ready")
        gates_ready = sem("gates_ready")
        sel_in = sem("sel_in")
        go_turned = sem("go_turned")
        goT_ready = sem("goT_ready")
        goT_out = sem("goT_out")
        w_in0 = sem("w_in0")
        w_in1 = sem("w_in1")
        w_split = sem("w_split")
        split_gate = sem("split_gate")
        att_pads = sem("att_pads")
        proj_ready = sem("proj_ready")
        values_ready = sem("values_ready")
        qk_pass = sem("qk_pass")
        rope_ready = sem("rope_ready")
        v32_ready = sem("v32_ready")
        tok_hi = sem("tok_hi")
        vt_hi = sem("vt_hi")
        tok_ready = sem("tok_ready")
        vt_ready = sem("vt_ready")
        tr_ready = sem("tr_ready")
        qkT_ready = sem("qkT_ready")
        kb_ready = sem("kb_ready")
        smax_ready = sem("smax_ready")
        max_ready = sem("max_ready")
        qm_turned = sem("qm_turned")
        qb_ready = sem("qb_ready")
        st_ready = sem("st_ready")
        exp_done = sem("exp_done")
        plo_ready = sem("plo_ready")
        av_ready = sem("av_ready")
        o32_ready = sem("o32_ready")
        ot_ready = sem("ot_ready")
        og_ready = sem("og_ready")
        og_hi_ready = sem("og_hi_ready")
        og_pair_ready = sem("og_pair_ready")
        go_in0 = sem("go_in0")
        go_in1 = sem("go_in1")
        o_ready = sem("o_ready")
        acc_added = sem("acc_added")
        mlp_in0 = sem("mlp_in0")
        mlp_in1 = sem("mlp_in1")
        mlp_split = sem("mlp_split")
        vecs_in = sem("vecs_in")
        b1_in = sem("b1_in")
        b1_ready = sem("b1_ready")
        y_ready = sem("y_ready")
        hs_ready = sem("hs_ready")
        h_hi2_ready = sem("h_hi2_ready")
        h_lo2_ready = sem("h_lo2_ready")
        z_ready = sem("z_ready")
        yb_ready = sem("yb_ready")
        x1b_ready = sem("x1b_ready")
        x1_in0 = sem("x1_in0")
        x1_in1 = sem("x1_in1")
        fin_ready = sem("fin_ready")
        fin_out0 = sem("fin_out0")
        fin_out1 = sem("fin_out1")
        fin_out2 = sem("fin_out2")
        many_found = sem("many_found")
        many_marked = sem("many_marked")
        many_summed = sem("many_summed")
        low_blocks_ready = sem("low_blocks_ready")
        w_in, go_in = (w_in0, w_in1), (go_in0, go_in1)
        mlp_in, x1_in, fin_out = (mlp_in0, mlp_in1), (x1_in0, x1_in1), (fin_out0, fin_out1, fin_out2)

        ps16 = ps[:, :, :].rearrange("p a b -> p (a b)").bitcast(F16).rearrange("p (a b) -> p a b", a=8)
        PER_HEAD = 2 * NT
        LATE = 2 * 2 * CH
        LATE_VALUES = 6
        AV, OT = 5, CH * (2 * P + 1)
        QM = 512

        def head_of(w, h):
            return w[ds(h, 1)].rearrange("o p k n -> (o p) k n") if not isinstance(h, int) else w[h]

        def columns(row, a, b, n):
            step = b - a
            return row[:, a:a + 2 * step].rearrange("p (x c) -> p x c", x=2)[:, :, 0:n]

        def p_block(j, u):
            return p32[:, (KU * j + u) % 2, :].rearrange("p (t s c) -> p t s c", t=2, s=CH)

        def head_order():
            def sc(j, *pairs):
                return [(what, j, u) for u in pairs for what in ("scores", "weights")]

            def out_(j, *numbers):
                return [("output", j, n) for n in numbers]

            def values(*tiles):
                return [("values", 0, t) for t in tiles]

            def rough(t):
                return [("rough", 0, t)]

            def weigh(j):
                return [("weigh", j, a) for a in range(CH)] + [("normalise", j, 0)]

            def max_(j):
                return [("turn maxima", j, 0)]

            def turn_out(j):
                return [("turn outputs", j, 0)]

            order = []
            for t in range(NT + 1):
                order.append(("project", 0, t))
                if t % 2 == 0 and t < NT:
                    order += values(t // 2)
                if 2 <= t < NT:
                    order.append(("turn", 0, t - 2))
            order += values(5) + [("turn", 0, NT - 2)] + out_(3, 0) + [("turn", 0, NT - 1)] + out_(3, 1)
            order += rough(0) + out_(3, 2) + rough(1) + out_(3, 3) + max_(0) + out_(4, 0)
            order += sc(0, 0, 1) + rough(2) + out_(4, 1) + sc(0, 2, 3) + out_(4, 2) + rough(3) + sc(0, 4) + out_(4, 3)
            order += max_(1) + values(6)
            order += sc(1, 0, 1) + rough(4) + values(7) + sc(1, 2, 3) + rough(5) + values(8) + max_(2) + sc(1, 4)
            order += values(9) + [("scores", 2, 0), ("scores", 2, 1)] + rough(6) + weigh(0)
            order += [("weights", 2, 0)]
            order += turn_out(0) + [("weights", 2, 1)] + rough(7) + sc(2, 2) + weigh(1) + sc(2, 3) + out_(0, 0) + sc(2, 4)
            order += out_(0, 1) + max_(3) + turn_out(1) + out_(0, 2) + out_(0, 3)
            order += sc(3, 0, 1) + out_(1, 0) + rough(8) + sc(3, 2, 3) + weigh(2) + out_(1, 1) + rough(9) + sc(3, 4)
            order += out_(1, 2) + max_(4) + turn_out(2) + out_(1, 3)
            order += sc(4, 0, 1) + out_(2, 0) + sc(4, 2, 3) + weigh(3) + sc(4, 4) + out_(2, 1) + turn_out(3) + out_(2, 2)
            order += weigh(4) + out_(2, 3) + turn_out(4)
            return order

        def output_count(h, j, n):
            return PER_HEAD * h + 2 * CH * ((j + 2) % NCK) + n

        def tail_order():
            order = [("output", 0), ("statistics", 0), ("output", 1), ("scaled", 0), ("output", 2), ("statistics", 1),
                     ("output", 3), ("turn", 0), ("scaled", 1), ("output", 4), ("statistics", 2), ("halves", 0),
                     ("output", 5), ("turn", 1), ("scaled", 2), ("output", 6), ("statistics", 3), ("halves", 1),
                     ("output", 7), ("turn", 2), ("scaled", 3), ("turn", 3), ("halves", 2), ("statistics", 4),
                     ("halves", 3), ("scaled", 4)]
            for t in range(5, NT):
                order += [("hidden", t - 5), ("turn", t - 1), ("statistics", t), ("halves", t - 1), ("scaled", t)]
            order += [("hidden", 5), ("turn", NT - 1), ("halves", NT - 1)]
            return order + [("hidden", n) for n in range(6, len(hidden()))]

        def hidden():
            return [(first, tiles, f) for first, tiles in GROUPS for f in range(F // 128)]

        def values_bank(i):
            return i % 2 if i < LATE_VALUES else 6 + i % 2

        def flat(ap):
            return ap.rearrange("p a b -> p (a b)")

        block = ctx.enter_context(nc.Block())

        def tile_rows(dram, t):
            return dram[ds(t * T, T), :]

        def turned_view(par, bank=0):
            both = ps[:, bank + 2 * par:bank + 2 * par + 2, :].rearrange("p a (b c) -> p a b c", b=4)
            return both[:, :, :, 0:T].rearrange("p a b (o c) -> p (a b) o c", o=1)

        def plan_of(engine, b):
            return [engine.value_load(plan[0:1, row * NT + b:row * NT + b + 1], min_val=least, max_val=most)
                    for row, least, most in ((0, 0, NCH - 1), (1, 2, NCH // 4 + 1), (2, 0, NT * (NCH // 4 + 1)))]

        @block.sync
        def _(sp):
            sp.dma_start(gconst[:, :], gtab).then_inc(const_in, 16)
            sp.dma_start(consts[:, :], ctab).then_inc(const_in, 16)
            sp.dma_start(b1c[:, :], b1).then_inc(b1_in, 16)
            sp.dma_start(rows_i[:, :, :], dst_rows).then_inc(edges_in, 16)
            sp.dma_start(edges_i[:, 0, :], src).then_inc(edges_in, 16)
            sp.dma_start(edges_i[:, 1, :], dst).then_inc(edges_in, 16)
            for t in range(2):
                sp.dma_start(xb[:, t, :], tile_rows(x, t)).then_inc(x_in[t], 16)
            sp.dma_start(bias_g[:, :], bg.partition_broadcast(T)).then_inc(bias_in, 16)
            with sp.Fori(1, NT // 2) as g:
                for par in range(2):
                    sp.wait_ge(turned, 2 * g + par - 1)
                    sp.dma_start(xb[:, par, :], tile_rows(x, 2 * g + par)).then_inc(x_in[par], 16)
            sp.wait_ge(h_lo_ready, ONE + NT)
            for t in range(2):
                sp.dma_start(xb[:, t, :], tile_rows(x, t)).then_inc(x_in[t], 16)
            for t in range(NT):
                sp.wait_ge(x1_ready, t + 1)
                sp.dma_start(x1_dram[t * T:(t + 1) * T, :], xb[:, t % 2, :]).then_inc(x1_out[t % 2], 16)
                if t + 2 < NT:
                    sp.wait_ge(x1_out[t % 2], 16 * (t // 2) + 16)
                    sp.wait_ge(xn_ready, NT + t + 1)
                    sp.dma_start(xb[:, t % 2, :], x[(t + 2) * T:(t + 3) * T, :]).then_inc(x_in[t % 2], 16)
            n_chunks = KD + PAIRS

            def load_chunk(h, c):
                if c < KD:
                    sp.dma_start(stage[:, c % 2, 0:WQKV], head_of(wqkv, h)[:, c, :]).then_inc(w_in[c % 2], 16)
                else:
                    sp.dma_start(stage[:, c % 2, :], head_of(wo, h)[:, c - KD, :]).then_inc(w_in[c % 2], 16)

            sp.wait_ge(agg_ready, NT)
            load_chunk(0, 0)
            load_chunk(0, 1)
            with sp.Fori(0, H - 1) as h:
                for c in range(n_chunks):
                    sp.wait_ge(w_split, SPLIT * n_chunks * h + SPLIT * (c + 1))
                    load_chunk(h + (c + 2) // n_chunks, (c + 2) % n_chunks)
            for c in range(n_chunks - 2):
                sp.wait_ge(w_split, SPLIT * n_chunks * (H - 1) + SPLIT * (c + 1))
                load_chunk(H - 1, c + 2)


            chunks = [(w1, k, F) for k in range(KD)] + [(w2, k, D) for k in range(F // 128)]

            def load_mlp(c):
                if c >= 2:
                    sp.wait_ge(mlp_split, SPLIT * (c - 1))
                w, k, width = chunks[c]
                sp.dma_start(stage[:, c % 2, 0:width], w[:, k, :]).then_inc(mlp_in[c % 2], 16)

            sp.wait_ge(w_split, SPLIT * n_chunks * H)
            for c in range(KD + 2):
                load_mlp(c)
            sp.wait_ge(av_ready, ONE + NCK * H)
            sp.dma_start(vecs, rowvecs.partition_broadcast(T)).then_inc(vecs_in, 16)
            for c in range(KD + 2, len(chunks)):
                load_mlp(c)
            sp.wait_ge(o_ready, PER_HEAD * H + LATE)
            for t in range(NT):
                if t >= 2:
                    sp.wait_ge(fin_ready, t - 1)
                sp.dma_start(x1b[t % 2], x1_dram[t * T:(t + 1) * T, :]).then_inc(x1_in[t % 2], 16)
                if t >= 1:
                    sp.wait_ge(fin_ready, t)
                    sp.dma_start(out[(t - 1) * T:t * T, :], fin[:, (t - 1) % 3, :]).then_inc(fin_out[(t - 1) % 3], 16)
            sp.wait_ge(fin_ready, NT)
            sp.dma_start(out[(NT - 1) * T:NT * T, :], fin[:, (NT - 1) % 3, :]).then_inc(fin_out[(NT - 1) % 3], 16)
            for part in range(3):
                sp.wait_ge(fin_out[part], 16 * len(range(part, NT, 3)))

        @block.gpsimd
        def _(pool):
            def split(hi, lo, staged, steps_done, n, gate=None):
                if gate is not None:
                    pool.sem_inc(gate, 1)
                pool.tensor_scalar(hi, staged, SW, 0.0, ALU.mult, ALU.add).then_inc(steps_done, 1)
                pool.wait_ge(steps_done, n + 1)
                if gate is not None:
                    pool.sem_inc(gate, 1)
                pool.tensor_scalar(staged, staged, SW, 0.0, ALU.mult, ALU.add).then_inc(steps_done, 1)
                pool.wait_ge(steps_done, n + 2)
                pool.tensor_tensor(lo, staged, hi, ALU.subtract).then_inc(steps_done, 1)

            for buf in (xT_hi, xT_lo):
                pool.memset(buf[:, :, :, T:PITCH], 0.0).then_inc(pads_ready, 1)
            for buf in (aT_hi, aT_lo):
                pool.memset(buf[:, :, :, T:PITCH], 0.0).then_inc(pads_ready, 1)
            pool.memset(ones16[:, :], 1.0).then_inc(pads_ready, 1)
            for k in range(2):
                pool.dma_start(w_stage[:, k, :], wg[:, k, :]).then_inc(wg_in[k], 16)
            for b in range(NT):
                pool.wait_ge(rstd_ready, b + 1)
                pool.tensor_scalar(xb[:, b % 2, :], xb[:, b % 2, :], mv[:, b % 2, 0:1], rstd[:, b % 2:b % 2 + 1],
                                   ALU.subtract, ALU.mult).then_inc(xn_ready, 1)
                if b < KD:
                    pool.wait_ge(wg_in[b % 2], 16 * (b // 2 + 1))
                    split(wg_hi[:, b, :], wg_lo[:, b, :], w_stage[:, b % 2, :], pool_chain, SPLIT * b)
                    if b + 2 < KD:
                        pool.wait_ge(pool_chain, SPLIT * (b + 1))
                        pool.dma_start(w_stage[:, b % 2, :], wg[:, b + 2, :]).then_inc(wg_in[b % 2], 16)
            pool.wait_ge(pool_chain, SPLIT * KD)
            pool.sem_inc(wg_split, 1)

            pool.wait_ge(h_lo_ready, ONE + NT)
            pool.dma_start(sel_stage, wsel).then_inc(sel_in, 16)
            pool.wait_ge(sel_in, 16)
            split(wsel_hi[:, :, :], wsel_lo[:, :, :], sel_stage, sel_split, 0)
            for t in range(NT - 2):
                pool.wait_ge(xn_ready, NT + t + 1)
                pool.tensor_scalar(acc[:, t, :], xn[:, t % 2, :], 1.0, 0.0, ALU.mult, ALU.add).then_inc(acc_ready, 1)

            n_chunks = KD + PAIRS

            def split_projections(h):
                for c in range(KD):
                    pool.wait_ge(w_in[c % 2], 16 * (n_chunks // 2 * h + c // 2 + 1))
                    split(wqkv_hi[:, c, :], wqkv_lo[:, c, :], stage[:, c % 2, 0:WQKV], w_split,
                          SPLIT * n_chunks * h + SPLIT * c, split_gate)

            def split_outputs(h):
                pool.wait_ge(o_ready, PER_HEAD * h + LATE)
                for c in range(KD, n_chunks):
                    pool.wait_ge(w_in[c % 2], 16 * (n_chunks // 2 * h + c // 2 + 1))
                    split(wo_hi[:, c - KD, :], wo_lo[:, c - KD, :], stage[:, c % 2, :], w_split,
                          SPLIT * n_chunks * h + SPLIT * c, split_gate)

            pool.wait_ge(agg_ready, NT)
            for buf in (qkT[:, :, :, T:PITCH], qb[:, :, T:PITCH], kb[:, :, T:PITCH], pT_hi[:, :, :, :, T:PITCH],
                        pT_lo[:, :, :, :, T:PITCH]):
                pool.memset(buf, 0.0).then_inc(att_pads, 1)
            pool.wait_ge(att_pads, 5)
            pool.memset(kb[P:P + 1, :, 0:T], SM).then_inc(att_pads, 1)
            pool.wait_ge(att_pads, 6)
            split_projections(0)
            pool.wait_ge(gates_ready, NT)
            pool.memset(vt[:, :, 2 * P:2 * P + 2], 1.0).then_inc(att_pads, 1)
            pool.memset(tok[:, :, MAXC + 1:K_LO], 0.0).then_inc(att_pads, 1)
            for buf in (flat(wo_hi[:, :, :]), flat(wo_lo[:, :, :]), og_hi[:, :, :, :, :].rearrange("p a b c d -> p (a b c d)"),
                        og_lo[:, :, :, :, :].rearrange("p a b c d -> p (a b c d)")):
                pool.memset(buf.bitcast(F32), 0.0).then_inc(att_pads, 1)
            pool.wait_ge(go_turned, NT)
            for t in range(NT - 2, NT):
                pool.wait_ge(xn_ready, NT + t + 1)
                pool.tensor_scalar(acc[:, t, :], xn[:, t % 2, :], 1.0, 0.0, ALU.mult, ALU.add).then_inc(acc_ready, 1)

            with pool.Fori(0, H - 1) as h:
                split_outputs(h)
                pool.wait_ge(values_ready, NT * (h + 1))
                split_projections(h + 1)
            split_outputs(H - 1)

            pool.wait_ge(values_ready, NT * H)
            for c in range(KD):
                pool.wait_ge(mlp_in[c % 2], 16 * (c // 2 + 1))
                split(w1_hi[:, c, :], w1_lo[:, c, :], stage[:, c % 2, 0:F], mlp_split, SPLIT * c)
            pool.wait_ge(o_ready, PER_HEAD * H + LATE)
            for buf in (hT_hi, hT_lo):
                pool.memset(buf[:, :, :, T:PITCH], 0.0).then_inc(att_pads, 1)
            for c in range(KD, KD + F // 128):
                pool.wait_ge(mlp_in[c % 2], 16 * (c // 2 + 1))
                split(w2_hi[:, c - KD, :], w2_lo[:, c - KD, :], stage[:, c % 2, :], mlp_split, SPLIT * c)
            for t in range(NT):
                pool.wait_ge(turned, 2 * NT + t + 1)
                pool.wait_ge(vecs_in, 16)
                pool.tensor_tensor(acc[:, t, :], acc[:, t, :], vecs[:, 2, :], ALU.add).then_inc(yb_ready, 1)
            for t in range(NT):
                pool.wait_ge(x1_in[t % 2], 16 * (t // 2 + 1))
                pool.tensor_tensor(x1b[t % 2], x1b[t % 2], vecs[:, 4, :], ALU.add).then_inc(x1b_ready, 1)

        def stats_of(dve, chain, par, tile, sems):
            for j in range(2):
                chain.done(dve.bn_stats(stats[:, par, j, :], tile[:, j * HALF:(j + 1) * HALF]))
            chain.wait()
            chain.step(dve.bn_aggr(mv[:, par, :], stats[:, par, :, :]))
            dve.tensor_scalar(var[:, par:par + 1], mv[:, par, 1:2], EPS, None, ALU.add).then_inc(sems, 1)

        @block.vector
        def _(dve):
            for signal in (max_ready, og_ready, plo_ready, tok_ready, acc_added, h_lo_ready):
                dve.sem_inc(signal, ONE)
            chain = Chain(dve, dve_chain)
            dve.wait_ge(const_in, 32)
            dve.wait_ge(edges_in, 48)
            dve.tensor_copy(ident16[:, :], ident)
            dve.tensor_copy(iota16, gconst[0:T, C_IOTA:C_IOTA + NT * PITCH])
            dve.memset(edges[:, :, NCH:SELF], -1.0)
            for a in range(2):
                dve.tensor_copy(edges[:, a, 0:NCH], edges_i[:, a, :])
                dve.tensor_copy(edges[:, a, SELF:ECOLS], gconst[0:T, C_SELF:C_SELF + NT])
            chain.step(dve.tensor_copy(rows[:, :, :], rows_i[:, :, :]))
            dve.tensor_reduce(spans[:, 0, :], rows[:, :, :], AX_X, ALU.min)
            dve.tensor_reduce(spans[:, 1, :], rows[:, :, :], AX_X, ALU.max).then_inc(spans_ready, 1)
            dve.wait_ge(spans_spread, 1)
            least = ps[0:NT, 6, 0:NCH]
            greatest = ps[0:NT, 7, 0:NCH]
            low = gconst[0:NT, C_LOW:C_LOW + 1]
            chain.step(dve.tensor_scalar(walk[:, 0:1], low, float(T - 1), None, ALU.add))
            chain.step(dve.tensor_scalar(near[:, 0, :], least, walk[:, 0:1], None, ALU.is_le))
            chain.step(dve.scalar_tensor_tensor(near[:, 0, :], greatest, low, near[:, 0, :], ALU.is_ge, ALU.mult))
            number = gconst[0:NT, C_CHUNK:C_CHUNK + NCH]
            chain.step(dve.scalar_tensor_tensor(near[:, 1, :], near[:, 0, :], -1000.0, number, ALU.mult, ALU.add))
            chain.step(dve.tensor_reduce(walk[:, 1:2], near[:, 1, :], AX_X, ALU.min))
            chain.step(dve.tensor_scalar(walk[:, 2:3], walk[:, 1:2], 1000.0, float(NCH - 1), ALU.add, ALU.min))
            chain.step(dve.scalar_tensor_tensor(near[:, 1, :], number, 1.0, near[:, 0, :], ALU.add, ALU.mult))
            chain.step(dve.tensor_reduce(walk[:, 3:4], near[:, 1, :], AX_X, ALU.max))
            chain.step(dve.scalar_tensor_tensor(walk[:, 4:5], walk[:, 3:4], 4.0, walk[:, 2:3], ALU.add, ALU.subtract))
            chain.step(dve.tensor_scalar(walk[:, 5:6], walk[:, 4:5], 8.0, None, ALU.max))
            chain.step(dve.tensor_copy(walk_i[:, :], walk[:, 5:6]))
            chain.step(dve.tensor_scalar(walk_i[:, :], walk_i[:, :], 2, None, ALU.logical_shift_right))
            dve.tensor_copy(walk[:, 6:7], walk_i[:, :]).then_inc(walk_ready, 1)
            dve.wait_ge(walk_turned, 1)
            dve.tensor_copy(plan[:, :], ps[0:1, 5, 0:3 * NT]).then_inc(plan_ready, 1)

            def layer_norm_stats(t, x_tile, loaded):
                dve.wait_ge(x_in[t % 2], loaded)
                stats_of(dve, chain, t % 2, x_tile, var_ready)

            def low_of_turned(t, count, bank):
                dve.wait_ge(hi_ready, count + t + 1)
                dve.scalar_tensor_tensor(xT_lo[:, :, t:t + 1, 0:T], turned_view(0, bank), SX,
                                         xT_hi[:, :, t:t + 1, 0:T], ALU.mult, ALU.subtract).then_inc(lo_ready, 1)

            def one_hot(s, column, b):
                dve.tensor_scalar(hot_src[s], iota16[:, 0:N], edges[:, 0, ds(column, 1)], None, ALU.is_equal)
                dve.tensor_scalar(hot_dst[s], iota16[:, b * T:b * T + PITCH], edges[:, 1, ds(column, 1)], None,
                                  ALU.is_equal).then_inc(hot_ready, 1)

            def a_low(b):
                dve.wait_ge(a_hi_ready, b + 1)
                for first, n in GROUPS:
                    sums = ps[0:T, 3 * (b % 2) + first // 4, 0:n * T].rearrange("p (b c) -> p b c", b=n)
                    last = dve.tensor_tensor(aT_lo[:, b, first:first + n, 0:T], sums,
                                             aT_hi[:, b, first:first + n, 0:T], ALU.subtract)
                last.then_inc(a_lo_ready, 1)

            dve.wait_ge(plan_ready, 1)
            layer_norm_stats(0, xb[:, 0, :], 16)
            following = plan_of(dve, 0)
            for b in range(NT):
                par = b % 2
                first, rounds, before = following
                for s in range(4):
                    if b:
                        dve.wait_ge(hot_used[s], before)
                    one_hot(s, first + (s - 1) if s else SELF + b, b)
                if b >= 1:
                    a_low(b - 1)
                dve.wait_ge(std_ready, b + 1)
                dve.reciprocal(rstd[:, par:par + 1], std[:, par:par + 1]).then_inc(rstd_ready, 1)
                if b + 1 < NT:
                    following = plan_of(dve, b + 1)
                with dve.Fori(1, rounds) as i:
                    for s in range(4):
                        column = nc.s_assert_within(
                            first + 4 * i + (s - 1), 0, SELF - 1,
                            skip_runtime_bounds_check_because="rounds ends at most 3 chunks after the last")
                        dve.wait_ge(hot_used[s], before + i)
                        one_hot(s, column, b)
                if b >= 1:
                    low_of_turned(b - 1, 0, 6)
                if b + 1 < NT:
                    layer_norm_stats(b + 1, xb[:, 1 - par, :], 16 * ((b + 1) // 2) + 16)
            a_low(NT - 1)
            low_of_turned(NT - 1, 0, 6)

            dve.wait_ge(deg_ready, 1)
            dve.tensor_scalar(many[:, :], ps[0:T, 5, 0:NT], 2048.0, None, ALU.is_gt).then_inc(many_marked, 1)
            dve.wait_ge(many_marked, 1)
            dve.tensor_reduce(many[:, 0:1], many[:, :], AX_X, ALU.max).then_inc(many_found, 1)

            dve.wait_ge(deg_root, 1)
            chain.step(dve.reciprocal(dis[:, 0, :], deg[:, :]))
            dve.tensor_scalar(dis[:, 1, :], dis[:, 0, :], SX, None, ALU.mult)
            chain.step(dve.tensor_scalar(dis[:, 2, :], dis[:, 0, :], 1.0 / SX, None, ALU.mult))
            dve.sem_inc(dis_ready, 1)

            dve.wait_ge(bias_in, 16)
            with dve.Fori(0, NT // 2) as g:
                for par in range(2):
                    t = 2 * g + par
                    dve.wait_ge(h_ready, t + 1)
                    dve.wait_ge(h_lo_ready, ONE + 2 * g)
                    dve.scalar_tensor_tensor(xb[:, par, :], ps[0:T, 2 * par:2 * par + 2, :].rearrange("p a b -> p (a b)"),
                                             1.0 / (SX * SW), bias_g[:, :], ALU.mult, ALU.add).then_inc(hb_ready, 1)
                for par in range(2):
                    t = 2 * g + par
                    dve.wait_ge(h_hi_ready, t + 1)
                    dve.scalar_tensor_tensor(h_lo[:, ds(t, 1), :].rearrange("p a b -> p (a b)"), xb[:, par, :],
                                             dis[:, 1, ds(t, 1)], h_hi[:, ds(t, 1), :].rearrange("p a b -> p (a b)"),
                                             ALU.mult, ALU.subtract).then_inc(h_lo_ready, 1)

            dve.wait_ge(many_summed, 1)
            chain.step(dve.tensor_scalar(blocks_f[:, 0:1], ps[0:1, 7, 0:1], 1.0, float(NT - 1), ALU.min, ALU.mult))
            chain.step(dve.tensor_scalar(blocks_f[:, 1:2], blocks_f[:, 0:1], 1.0, None, ALU.add))
            dve.tensor_copy(blocks_i[:, 0:1], blocks_f[:, 1:2]).then_inc(low_blocks_ready, 1)

            groups = 2 * H
            a8, b8 = (buf[:, :].rearrange("p (g e) -> p g e", e=EX) for buf in (pick_a, pick_b))
            rev8 = consts[0:T, C_REV:C_REV + EX].unsqueeze(1).to_broadcast([T, groups, EX])

            def spread(j):
                return best[:, j, :].unsqueeze(2).to_broadcast([T, groups, EX])

            def first_best(values, into):
                chain.step(dve.tensor_reduce(best[:, 0, :], values, AX_X, ALU.max))
                chain.step(dve.tensor_tensor(b8, values, spread(0), ALU.is_equal))
                chain.step(dve.tensor_tensor(b8, b8, rev8, ALU.mult))
                chain.step(dve.tensor_reduce(best[:, 1, :], b8, AX_X, ALU.max))
                chain.step(dve.tensor_tensor(into, b8, spread(1), ALU.is_equal))

            def choose(t):
                s8 = sig[:, t % 2, :].rearrange("p (g e) -> p g e", e=EX)
                dve.wait_ge(exp_ready, t + 1)
                chain.step(dve.tensor_scalar(s8, s8, 1.0, None, ALU.add))
                chain.step(dve.reciprocal(s8, s8))
                first_best(s8, a8)
                chain.step(dve.scalar_tensor_tensor(b8, a8, -4.0, s8, ALU.mult, ALU.add))
                first_best(b8, b8)
                chain.step(dve.tensor_tensor(a8, a8, b8, ALU.add))
                dve.tensor_tensor(gv[:, t, :], sig[:, t % 2, 0:H * EX], pick_a[:, 0:H * EX], ALU.mult)
                dve.tensor_tensor(go_keep[:, t, :], sig[:, t % 2, H * EX:2 * H * EX], pick_a[:, H * EX:2 * H * EX],
                                  ALU.mult).then_inc(gates_ready, 1)

            for t in range(NT + 1):
                par = t % 2
                if t >= 1:
                    low_of_turned(t - 1, NT, 4)
                if t < NT:
                    dve.wait_ge(x_in[par], 16 * (NT // 2) + 16 * (t // 2) + 16)
                    dve.wait_ge(agg_ready, t + 1)
                    dve.scalar_tensor_tensor(xb[:, par, :], flat(ps[0:T, 2 * par:2 * par + 2, :]),
                                             dis[:, 2, t:t + 1], xb[:, par, :], ALU.mult, ALU.add).then_inc(x1_ready, 1)
                    dve.wait_ge(x1_ready, t + 1)
                    stats_of(dve, chain, par, xb[:, par, :], var_ready)
                    dve.wait_ge(std_ready, NT + t + 1)
                    chain.step(dve.reciprocal(rstd[:, par:par + 1], std[:, par:par + 1]))
                    if t >= 2:
                        dve.wait_ge(turned, NT + t - 1)
                        dve.wait_ge(acc_ready, t - 1)
                    dve.tensor_scalar(xn[:, par, :], xb[:, par, :], mv[:, par, 0:1], rstd[:, par:par + 1],
                                      ALU.subtract, ALU.mult).then_inc(xn_ready, 1)
                if t >= 1:
                    choose(t - 1)
            for par in range(2):
                dve.wait_ge(x1_out[par], 16 * (NT // 2))
            for first, n in GROUPS:
                dve.wait_ge(go_turned, NT)
                last = dve.tensor_copy(goT[:, first:first + n, :],
                                       ps[:, 5 + first // 4, 0:n * T].rearrange("p (a b) -> p a b", a=n))
            last.then_inc(goT_ready, 1)

            dve.wait_ge(rope_in, 16)
            dve.wait_ge(goT_out, 16)
            dve.wait_ge(att_pads, 12)
            dve.sem_inc(og_pair_ready, 2 * CH)
            with dve.Fori(0, H) as h:
                def rotate(i):
                    par = i % 2
                    qk = qk32[:, par, :, :]
                    half = NROT // 2

                    def table(first, n):
                        return rope[:, i:i + 1, first:first + n].to_broadcast([T, 2, n])

                    dve.wait_ge(qk_pass, NT * h + i + 1)
                    if i:
                        dve.wait_ge(rope_ready, NT * h + i)
                    dve.tensor_tensor(rot[:, 0, :, :], qk[:, :, 0:NROT], table(0, NROT), ALU.mult)
                    dve.tensor_tensor(rot[:, 1, :, 0:half], qk[:, :, half:NROT], table(NROT, half), ALU.mult)
                    chain.step(dve.tensor_tensor(rot[:, 1, :, half:NROT], qk[:, :, 0:half], table(NROT + half, half),
                                                 ALU.mult))
                    dve.tensor_tensor(qk32[:, par, :, 0:NROT], rot[:, 0, :, :], rot[:, 1, :, :], ALU.add)\
                        .then_inc(rope_ready, 1)

                def values(i):
                    par = i % 2
                    dve.wait_ge(values_ready, NT * h + i + 1)
                    gate = gv[:, i:i + 1, ds(EX * h, EX)].rearrange("p o e -> p (o e)").unsqueeze(2)
                    chain.step(dve.tensor_tensor(vprod[:, :, :], ps[0:T, values_bank(i), :].rearrange("p (e c) -> p e c", e=EX),
                                                 gate.to_broadcast([T, EX, P]), ALU.mult))
                    dve.tensor_reduce(v32[:, par, :], vprod[:, :, :].rearrange("p e c -> p c e"), AX_X, ALU.add)\
                        .then_inc(v32_ready, 1)

                def low_qk(i):
                    par = i % 2
                    dve.wait_ge(tok_hi, NT * h + i + 1)
                    dve.tensor_tensor(columns(tok[:, i, :], Q_LO, K_LO, P), qk32[:, par, :, :],
                                      columns(tok[:, i, :], Q_HI, K_HI, P), ALU.subtract).then_inc(tok_ready, 1)

                def low_values(i):
                    dve.wait_ge(vt_hi, NT * h + i + 1)
                    dve.scalar_tensor_tensor(vt[:, i, 0:P], v32[:, i % 2, :], SQ / (SX * SW), vt[:, i, P:2 * P],
                                             ALU.mult, ALU.subtract).then_inc(vt_ready, 1)

                def take_kb(i):
                    dve.wait_ge(qkT_ready, NT * h + i + 1)
                    dve.tensor_copy(kb[0:P, i, 0:T], ps16[0:P, 4 + i % 2, 2 * PITCH:2 * PITCH + T]).then_inc(kb_ready, 1)

                def row_max(i):
                    dve.wait_ge(smax_ready, NT * h + i + 1)
                    chain.done(dve.tensor_reduce(mx[:, 0:1], ps[0:T, 0:2, 0:4 * T], mybir.AxisListType.XY, ALU.max))
                    chain.step(dve.tensor_reduce(mx[:, 1:2], ps[0:T, 2, 0:2 * T], AX_X, ALU.max))
                    dve.tensor_scalar(tok[:, i, MAXC:MAXC + 1], mx[:, 0:1], mx[:, 1:2], -1.0 / SM, ALU.max, ALU.mult)\
                        .then_inc(max_ready, 1)

                def p_low(j, u):
                    dve.wait_ge(exp_done, ONE + KU * NCK * h + KU * j + u + 1)
                    dve.tensor_tensor(pT_lo[:, j % 2, 2 * u:2 * u + 2, :, 0:T], p_block(j, u),
                                      pT_hi[:, j % 2, 2 * u:2 * u + 2, :, 0:T], ALU.subtract).then_inc(plo_ready, 1)

                def add_out(j, n):
                    dve.wait_ge(o_ready, output_count(h, j, n) + 1)
                    into = acc[:, CH * j + n // 2, (n % 2) * HALF:(n % 2 + 1) * HALF]
                    dve.scalar_tensor_tensor(into, ps[0:T, 6 + n % 2, :], 1.0 / (SQ * SW), into, ALU.mult, ALU.add)\
                        .then_inc(acc_added, 1)

                def normalise(j):
                    values = ps[0:T, AV, 0:OT].rearrange("p (s c) -> p s c", s=CH)
                    dve.wait_ge(av_ready, ONE + NCK * h + j + 1)
                    chain.done(dve.reciprocal(rsum[:, :], values[:, :, 2 * P:2 * P + 1].rearrange("p s o -> p (s o)")))
                    chain.step(dve.tensor_copy(o_low[:, :, :], values[:, :, 0:P]))
                    chain.step(dve.tensor_tensor(o_sum[:, :, :], o_low[:, :, :], values[:, :, P:2 * P], ALU.add))
                    dve.tensor_tensor(o32[:, :, :, :], o_sum[:, :, :].unsqueeze(2).to_broadcast([T, CH, 2, P]),
                                      rsum[:, :].unsqueeze(2).unsqueeze(3).to_broadcast([T, CH, 2, P]), ALU.mult)\
                        .then_inc(o32_ready, 1)

                def gated(j):
                    dve.wait_ge(ot_ready, NCK * h + j + 1)
                    dve.wait_ge(go_in[j % 2], 32 * (((NCK + 1 - j % 2) // 2) * h + j // 2 + 1))
                    for a in range(CH):
                        oT = ps[:, AV, OT + a * T:OT + (a + 1) * T].unsqueeze(1).to_broadcast([128, PAIRS, T])
                        dve.tensor_tensor(og32[:, :, a * T:(a + 1) * T], go_b[:, j % 2, :, a * T:(a + 1) * T], oT,
                                          ALU.mult).then_inc(og_ready, 1)
                    for a in range(CH):
                        dve.wait_ge(og_hi_ready, CH * (NCK * h + j) + a + 1)
                        dve.tensor_tensor(og_lo[:, j % 2, :, a, 0:T], og32[:, :, a * T:(a + 1) * T],
                                          og_hi[:, j % 2, :, a, 0:T], ALU.subtract).then_inc(og_pair_ready, 1)

                chain.enter(h, NT * 2 + NT * 2 + NCK * 3)
                for what, j, n in head_order():
                    if what == "project":
                        if n < NT:
                            rotate(n)
                        if n >= 1:
                            low_qk(n - 1)
                    if what == "values":
                        values(n)
                        if n >= 1:
                            low_values(n - 1)
                        if n == NT - 1:
                            low_values(n)
                    if what == "turn":
                        take_kb(n)
                    if what == "rough":
                        row_max(n)
                    if what == "weights":
                        p_low(j, n)
                    if what == "normalise":
                        normalise(j)
                    if what == "turn outputs":
                        gated(j)
                    if what == "output":
                        add_out(j, n)
            chain.leave(H)
            dve.wait_ge(b1_in, 16)
            dve.tensor_scalar(b1c[:, :], b1c[:, :], SQ, None, ALU.mult).then_inc(b1_ready, 1)

            def scaled(t, tile, count, gain, into_shift):
                par = t % 2
                dve.wait_ge(std_ready, count + t + 1)
                chain.done(dve.reciprocal(rstd[:, par:par + 1], std[:, par:par + 1]))
                chain.step(dve.scalar_tensor_tensor(tile, tile, mv[:, par, 0:1], vecs[:, gain, :], ALU.subtract, ALU.mult))
                return dve.scalar_tensor_tensor(tile, tile, rstd[:, par:par + 1], into_shift, ALU.mult, ALU.add)

            for what, n in tail_order():
                if what == "output":
                    j = 3 + n // (2 * CH)
                    dve.wait_ge(o_ready, PER_HEAD * H + n + 1)
                    t, half = CH * j + n % (2 * CH) // 2, n % 2
                    into = acc[:, t, half * HALF:(half + 1) * HALF]
                    dve.scalar_tensor_tensor(into, ps[0:T, 6 + half, :], 1.0 / (SQ * SW), into, ALU.mult, ALU.add)\
                        .then_inc(acc_added, 1)
                if what == "statistics":
                    dve.wait_ge(acc_added, ONE + PER_HEAD * H + min(max(2 * (n - 5), 0), LATE))
                    stats_of(dve, chain, n % 2, acc[:, n, :], var_ready)
                if what == "scaled":
                    dve.wait_ge(vecs_in, 16)
                    scaled(n, acc[:, n, :], 2 * NT, 0, vecs[:, 1, :]).then_inc(y_ready, 1)
                if what == "halves":
                    low_of_turned(n, 2 * NT, 2 * (n % 2))
                if what == "hidden":
                    first, tiles, f = hidden()[n]
                    dve.wait_ge(h_hi2_ready, n + 1)
                    dve.tensor_tensor(hT_lo[:, f, first:first + tiles, 0:T],
                                      h32[:, n % 2, 0:tiles * T].rearrange("p (a b) -> p a b", a=tiles),
                                      hT_hi[:, f, first:first + tiles, 0:T], ALU.subtract).then_inc(h_lo2_ready, 1)
            for t in range(NT + 1):
                if t < NT:
                    par = t % 2
                    dve.wait_ge(z_ready, t + 1)
                    dve.wait_ge(yb_ready, t + 1)
                    if t >= 3:
                        dve.wait_ge(fin_out[t % 3], 16 * (t // 3))
                    chain.step(dve.scalar_tensor_tensor(fin[:, t % 3, :], flat(ps[0:T, 2 * par:2 + 2 * par, :]),
                                                        1.0 / (SQ * SW), acc[:, t, :], ALU.mult, ALU.add))
                    stats_of(dve, chain, par, fin[:, t % 3, :], var_ready)
                if t >= 1:
                    dve.wait_ge(x1b_ready, t)
                    scaled(t - 1, fin[:, (t - 1) % 3, :], 3 * NT, 3, x1b[(t - 1) % 2]).then_inc(fin_ready, 1)

        @block.scalar
        def _(act):
            for signal in (exp_done, qb_ready):
                act.sem_inc(signal, ONE)
            def root(t, count):
                act.wait_ge(var_ready, count + t + 1)
                act.activation(std[:, t % 2:t % 2 + 1], var[:, t % 2:t % 2 + 1], ACT.Sqrt).then_inc(std_ready, 1)

            def high_of_turned(t, count, bank):
                act.wait_ge(turned, count + t + 1)
                act.activation(xT_hi[:, :, t:t + 1, 0:T], turned_view(0, bank), ACT.Copy, scale=SX)\
                    .then_inc(hi_ready, 1)

            act.wait_ge(plan_ready, 1)
            root(0, 0)
            for b in range(NT):
                if b >= 1:
                    high_of_turned(b - 1, 0, 6)
                rounds = act.value_load(plan[0:1, NT + b:NT + b + 1], min_val=2, max_val=NCH // 4 + 1)
                before = act.value_load(plan[0:1, 2 * NT + b:2 * NT + b + 1], min_val=0,
                                        max_val=NT * (NCH // 4 + 1))
                act.wait_ge(hot_used[3], before + rounds)
                for first, n in GROUPS:
                    sums = ps[0:T, 3 * (b % 2) + first // 4, 0:n * T].rearrange("p (b c) -> p b c", b=n)
                    last = act.activation(aT_hi[:, b, first:first + n, 0:T], sums, ACT.Copy)
                last.then_inc(a_hi_ready, 1)
                if b + 1 < NT:
                    root(b + 1, 0)
            high_of_turned(NT - 1, 0, 6)
            act.wait_ge(many_marked, 1)
            act.activation(deg[:, :], ps[0:T, 5, 0:NT], ACT.Sqrt).then_inc(deg_root, 1)
            act.wait_ge(dis_ready, 1)
            with act.Fori(0, NT // 2) as g:
                for par in range(2):
                    t = 2 * g + par
                    act.wait_ge(hb_ready, t + 1)
                    act.activation(h_hi[:, ds(t, 1), :].rearrange("p a b -> p (a b)"), xb[:, par, :], ACT.Copy,
                                   scale=dis[:, 1, ds(t, 1)]).then_inc(h_hi_ready, 1)
            for t in range(NT + 1):
                if t >= 1:
                    high_of_turned(t - 1, NT, 4)
                if t < NT:
                    root(t, NT)
                if t >= 1:
                    act.wait_ge(logits_ready, t)
                    if t >= 3:
                        act.wait_ge(gates_ready, t - 2)
                    act.activation(sig[:, (t - 1) % 2, :], ps[0:T, 6, 0:2 * H * EX], ACT.Exp, scale=-1.0 / (SX * SW))\
                        .then_inc(exp_ready, 1)

            act.wait_ge(goT_ready, 1)
            for par in range(2):
                act.wait_ge(x1_out[par], 16 * (NT // 2))
            act.dma_start(goT_dram, flat(goT[:, :, :])).then_inc(goT_out, 16)
            act.dma_start(rope[:, :, :], rtab).then_inc(rope_in, 16)
            act.wait_ge(acc_ready, NT)
            act.wait_ge(goT_out, 16)

            with act.Fori(0, H) as h:
                def load_gates(j):
                    for e in range(2):
                        rows = goT_dram[ds(EX * h, EX), CHN * j:CHN * (j + 1)].rearrange("(k e) n -> e k n", e=2)[e]
                        act.dma_start(go_b[P * e:P * (e + 1), j % 2, :, :], rows.partition_broadcast(P))\
                            .then_inc(go_in[j % 2], 16)

                act.wait_ge(og_ready, ONE + CH * NCK * h)
                load_gates(0)
                load_gates(1)

                def take_qk(i):
                    par = i % 2
                    qk = ps[0:T, 2 + par, 0:2 * P].rearrange("p (a c) -> p a c", a=2)
                    act.wait_ge(proj_ready, NT * h + i + 1)
                    act.wait_ge(tok_ready, ONE + NT * h + max(i - 1, 0))
                    act.activation(qk32[:, par, :, :], qk, ACT.Copy, scale=SQ / (SX * SW))\
                        .then_inc(qk_pass, 1)

                def high_halves(i):
                    par = i % 2
                    act.wait_ge(rope_ready, NT * h + i + 1)
                    act.wait_ge(qm_turned, ONE + NCK * h)
                    act.activation(columns(tok[:, i, :], Q_HI, K_HI, P), qk32[:, par, :, :], ACT.Copy)
                    act.activation(tok[:, i, K_HI2:K_HI2 + P], qk32[:, par, 1, :], ACT.Copy).then_inc(tok_hi, 1)

                def high_values(i):
                    act.wait_ge(v32_ready, NT * h + i + 1)
                    act.wait_ge(av_ready, ONE + NCK * h)
                    act.activation(vt[:, i, P:2 * P], v32[:, i % 2, :], ACT.Copy, scale=SQ / (SX * SW)).then_inc(vt_hi, 1)

                def take_qkT(i):
                    act.wait_ge(tr_ready, NT * h + i + 1)
                    act.activation(qkT[:, :, i, 0:T], ps16[:, 4 + i % 2, 0:2 * PITCH]
                                   .rearrange("p (a c) -> p a c", a=2)[:, :, 0:T], ACT.Copy).then_inc(qkT_ready, 1)

                def exps(j, u):
                    n = KU * j + u
                    act.wait_ge(st_ready, KU * NCK * h + n + 1)
                    act.wait_ge(plo_ready, ONE + KU * NCK * h + max(n - 1, 0))
                    if u == 0:
                        act.wait_ge(av_ready, ONE + NCK * h + max(j - 1, 0))
                    scores = ps[0:T, 3 + n % 2, 0:2 * CHN]
                    act.activation(p32[:, n % 2, :], scores, ACT.Exp, bias=consts[0:T, C_LNP:C_LNP + 1],
                                   scale=1.0 / (SQ * SQ * P ** 0.5))
                    act.activation(pT_hi[:, j % 2, 2 * u:2 * u + 2, :, 0:T],
                                   scores.rearrange("p (t s c) -> p t s c", t=2, s=CH), ACT.Exp,
                                   bias=consts[0:T, C_LNP:C_LNP + 1], scale=1.0 / (SQ * SQ * P ** 0.5))\
                        .then_inc(exp_done, 1)

                def take_maxima(j):
                    act.wait_ge(qm_turned, ONE + NCK * h + j + 1)
                    act.activation(qb[:, CH * j:CH * (j + 1), 0:T], ps16[0:P + 1, 2, QM:QM + CH * PITCH]
                                   .rearrange("p (a c) -> p a c", a=CH)[:, :, 0:T], ACT.Copy).then_inc(qb_ready, 1)

                def gated(j):
                    act.wait_ge(o_ready, output_count(h, j - 2, 0) + 2 * CH if j >= 2 else PER_HEAD * h + LATE)
                    for a in range(CH):
                        act.wait_ge(og_ready, ONE + CH * (NCK * h + j) + a + 1)
                        act.activation(og_hi[:, j % 2, :, a, 0:T], og32[:, :, a * T:(a + 1) * T], ACT.Copy)\
                            .then_inc(og_hi_ready, 1)
                    if j + 2 < NCK:
                        load_gates(j + 2)

                for what, j, n in head_order():
                    if what == "project":
                        if n < NT:
                            take_qk(n)
                        if n >= 1:
                            high_halves(n - 1)
                    if what == "values":
                        high_values(n)
                    if what == "turn":
                        take_qkT(n)
                    if what == "turn maxima":
                        take_maxima(j)
                    if what == "weights":
                        exps(j, n)
                    if what == "turn outputs":
                        gated(j)

            act.wait_ge(b1_ready, 1)
            for what, n in tail_order():
                if what == "statistics":
                    root(n, 2 * NT)
                if what == "halves":
                    high_of_turned(n, 2 * NT, 2 * (n % 2))
                if what == "hidden":
                    first, tiles, f = hidden()[n]
                    act.wait_ge(hs_ready, n + 1)
                    if n >= 2:
                        act.wait_ge(h_lo2_ready, n - 1)
                    product = ps[:, 4 + n % 4, 0:tiles * T]
                    act.activation(h32[:, n % 2, 0:tiles * T], product, ACT.Relu, bias=b1c[:, f:f + 1],
                                   scale=SQ / (SX * SW))
                    act.activation(hT_hi[:, f, first:first + tiles, 0:T],
                                   product.rearrange("p (a b) -> p a b", a=tiles), ACT.Relu, bias=b1c[:, f:f + 1],
                                   scale=SQ / (SX * SW)).then_inc(h_hi2_ready, 1)
            for t in range(NT):
                root(t, 3 * NT)

        @block.tensor
        def _(pe):
            for signal in (av_ready, qm_turned):
                pe.sem_inc(signal, ONE)
            pe.wait_ge(const_in, 32)
            pe.wait_ge(spans_ready, 1)
            n_rows = NCH // CPR
            for a in range(2):
                for j in range(CPR):
                    last = pe.matmul(ps[0:NT, 6 + a, j * n_rows:(j + 1) * n_rows],
                                     spans[:, a, j:j + 1].to_broadcast([n_rows, NT]),
                                     gconst[0:n_rows, C_ID10:C_ID10 + n_rows], start=True, stop=True)
            last.then_inc(spans_spread, 1)
            pe.wait_ge(walk_ready, 1)
            pe.matmul(ps[0:1, 5, 0:NT], walk[:, 2:3], gconst[0:NT, C_ID10:C_ID10 + NT], start=True, stop=True)
            pe.matmul(ps[0:1, 5, NT:2 * NT], walk[:, 6:7], gconst[0:NT, C_ID10:C_ID10 + NT], start=True, stop=True)
            pe.matmul(ps[0:1, 5, 2 * NT:3 * NT], walk[:, 6:7], gconst[0:NT, C_UPPER:C_UPPER + NT],
                      start=True, stop=True).then_inc(walk_turned, 1)

            def turn_tile(t, count, source, bank):
                pe.wait_ge(xn_ready, count + t + 1)
                pe.wait_ge(lo_ready, count + t)
                for k in range(KD):
                    last = pe.transpose(ps[:, bank + k // 4, (k % 4) * PITCH:(k % 4) * PITCH + T],
                                        source[:, k * 128:(k + 1) * 128], ident[0:T, 0:T])
                last.then_inc(turned, 1)

            pe.wait_ge(plan_ready, 1)

            def count(s, par, start, stop):
                for first, n in GROUPS:
                    last = pe.matmul(ps[:, 3 * par + first // 4, 0:n * T], hot_dst[s],
                                     hot_src[s][:, first * T:(first + n) * T], start=start, stop=stop,
                                     skip_group_check=True)
                last.then_inc(hot_used[s], 1)

            following = plan_of(pe, 0)
            for b in range(NT):
                par = b % 2
                rounds, before = following[1:]
                if b >= 2:
                    pe.wait_ge(a_lo_ready, b - 1)
                for s in range(4):
                    pe.wait_ge(hot_ready, 4 * before + s + 1)
                    count(s, par, s == 0, False)
                if b >= 1:
                    turn_tile(b - 1, 0, xb[:, 1 - par, :], 6)
                if b + 1 < NT:
                    following = plan_of(pe, b + 1)
                with pe.Fori(1, rounds) as i:
                    for s in range(4):
                        pe.wait_ge(hot_ready, 4 * before + 4 * i + s + 1)
                        count(s, par, False, s == 3)
            turn_tile(NT - 1, 0, xb[:, 1, :], 6)

            pe.wait_ge(a_lo_ready, NT)
            pe.wait_ge(pads_ready, 5)
            for t in range(NT):
                for b in range(NT):
                    pe.matmul(ps[:, 5, t:t + 1], aT_hi[:, b, t, :], ones16[:, 0:1], start=(b == 0), stop=False)
                    last = pe.matmul(ps[:, 5, t:t + 1], aT_lo[:, b, t, :], ones16[:, 0:1], start=False,
                                     stop=(b == NT - 1))
            last.then_inc(deg_ready, 1)

            pe.wait_ge(wg_split, 1)
            pe.wait_ge(lo_ready, NT)

            def transform(t, par):
                for k in range(KD):
                    for x_part, w_parts in ((xT_hi, (wg_hi, wg_lo)), (xT_lo, (wg_hi,))):
                        for w_part in w_parts:
                            for j in range(2):
                                last = pe.matmul(ps[:, 2 * par + j, :], flat(x_part[:, k, ds(t, 1), :]),
                                                 w_part[:, k, j * HALF:(j + 1) * HALF],
                                                 start=(k == 0 and x_part is xT_hi and w_part is wg_hi),
                                                 stop=(k == KD - 1 and x_part is xT_lo))
                last.then_inc(h_ready, 1)

            for t in range(2):
                transform(t, t)
            pe.wait_ge(many_found, 1)
            pe.matmul(ps[0:1, 7, 0:1], many[:, 0:1], ones16[:, 0:1], start=True, stop=True).then_inc(many_summed, 1)
            with pe.Fori(1, NT // 2) as g:
                for par in range(2):
                    pe.wait_ge(hb_ready, 2 * g + par - 1)
                    transform(2 * g + par, par)

            pe.wait_ge(low_blocks_ready, 1)
            low_blocks = pe.value_load(blocks_i[0:1, 0:1], min_val=1, max_val=NT)

            def aggregate(t, par, blocks, last_part):
                for b in blocks:
                    if isinstance(t, int) and t == 0:
                        pe.wait_ge(h_lo_ready, ONE + b + 1)
                    for h_part in (h_hi, h_lo):
                        for j in range(2):
                            last = pe.matmul(ps[:, 2 * par + j, :], flat(aT_hi[:, b, ds(t, 1), :]),
                                             h_part[:, b, j * HALF:(j + 1) * HALF],
                                             start=(b == 0 and h_part is h_hi),
                                             stop=(b == NT - 1 and h_part is h_lo), skip_group_check=True)
                if last_part:
                    last.then_inc(agg_ready, 1)

            def aggregate_low(t, par):
                with pe.Fori(0, low_blocks) as b:
                    for j in range(2):
                        pe.matmul(ps[:, 2 * par + j, :],
                                  aT_lo[:, ds(b, 1), ds(t, 1), :].rearrange("p a b c -> p (a b c)"),
                                  flat(h_hi[:, ds(b, 1), j * HALF:(j + 1) * HALF]), start=False, stop=False,
                                  skip_group_check=True)

            def logits(t):
                pe.wait_ge(sel_split, SPLIT)
                pe.wait_ge(lo_ready, NT + t + 1)
                pe.wait_ge(exp_ready, t)
                for k in range(KD):
                    for x_part, w_parts in ((xT_hi, (wsel_hi, wsel_lo)), (xT_lo, (wsel_hi,))):
                        for w_part in w_parts:
                            last = pe.matmul(ps[:, 6, 0:2 * H * EX], flat(x_part[:, k, ds(t, 1), :]), w_part[:, k, :],
                                             start=(k == 0 and x_part is xT_hi and w_part is wsel_hi),
                                             stop=(k == KD - 1 and x_part is xT_lo))
                last.then_inc(logits_ready, 1)

            first_half, second_half = range(NT // 2), range(NT // 2, NT)
            aggregate(0, 0, first_half, False)
            pe.wait_ge(h_lo_ready, ONE + NT)
            aggregate_low(0, 0)
            aggregate(0, 0, second_half, True)

            def aggregate_and_turn(t, par):
                aggregate(t, par, first_half, False)
                turn_tile(t - 1, NT, xn[:, 1 - par, :], 4)
                aggregate_low(t, par)
                aggregate(t, par, second_half, True)
                logits(t - 1)

            aggregate_and_turn(1, 1)
            with pe.Fori(1, NT // 2) as g:
                for par in range(2):
                    t = 2 * g + par
                    pe.wait_ge(x1_ready, t - 1)
                    aggregate_and_turn(t, par)
            turn_tile(NT - 1, NT, xn[:, 1, :], 4)
            logits(NT - 1)
            pe.wait_ge(gates_ready, NT)
            for t in range(NT):
                pe.transpose(ps[:, 5 + t // 4, (t % 4) * T:(t % 4 + 1) * T], go_keep[:, t, :], ident[0:T, 0:T])\
                    .then_inc(go_turned, 1)

            n_chunks = KD + PAIRS

            def output(h, j, n):
                if j == 0 and n == 0:
                    pe.wait_ge(v32_ready, NT * (h + 1))
                    pe.wait_ge(w_split, SPLIT * n_chunks * (h + 1))
                half, a = n % 2, n // 2
                pe.wait_ge(att_pads, 12)
                pe.wait_ge(og_pair_ready, CH * (NCK * h + (j + 2) % NCK) + n // 2 + 1)
                pe.wait_ge(acc_added, ONE + PER_HEAD * h + max(output_count(0, j, n) - 1, 0))
                for k in range(PAIRS):
                    for o_part_, w_parts in ((og_hi, (wo_hi, wo_lo)), (og_lo, (wo_hi,))):
                        for w_part in w_parts:
                            last = pe.matmul(ps[:, 6 + half, :], o_part_[:, j % 2, k, a, :],
                                             w_part[:, k, half * HALF:(half + 1) * HALF],
                                             start=(k == 0 and o_part_ is og_hi and w_part is wo_hi),
                                             stop=(k == PAIRS - 1 and o_part_ is og_lo))
                last.then_inc(o_ready, 1)

            pe.wait_ge(att_pads, 8)
            pe.wait_ge(goT_ready, 1)
            with pe.Fori(0, H) as h:
                def project(i):
                    if i >= 2:
                        pe.wait_ge(qk_pass, NT * h + i - 1)
                    for k in range(KD):
                        for x_part, w_parts in ((xT_hi, (wqkv_hi, wqkv_lo)), (xT_lo, (wqkv_hi,))):
                            for w_part in w_parts:
                                last = pe.matmul(ps[:, 2 + i % 2, 0:2 * P], x_part[:, k, i, :], w_part[:, k, 0:2 * P],
                                                 start=(k == 0 and x_part is xT_hi and w_part is wqkv_hi),
                                                 stop=(k == KD - 1 and x_part is xT_lo))
                    last.then_inc(proj_ready, 1)

                def values(i):
                    if i >= 2:
                        pe.wait_ge(v32_ready, NT * h + i - 1)
                    if i >= LATE_VALUES:
                        pe.wait_ge(acc_added, ONE + (PER_HEAD * h + LATE - (1 if i == LATE_VALUES else 0)))
                    for k in range(KD):
                        for x_part, w_parts in ((xT_hi, (wqkv_hi, wqkv_lo)), (xT_lo, (wqkv_hi,))):
                            for w_part in w_parts:
                                last = pe.matmul(ps[:, values_bank(i), :], x_part[:, k, i, :], w_part[:, k, 2 * P:WQKV],
                                                 start=(k == 0 and x_part is xT_hi and w_part is wqkv_hi),
                                                 stop=(k == KD - 1 and x_part is xT_lo))
                    last.then_inc(values_ready, 1)

                def turn(i):
                    bank = 4 + i % 2
                    pe.wait_ge(tok_ready, ONE + NT * h + i + 1)
                    if i == 1:
                        pe.wait_ge(og_ready, ONE + CH * NCK * h)
                    if i >= 2:
                        pe.wait_ge(qkT_ready, NT * h + i - 1)
                        pe.wait_ge(kb_ready, NT * h + i - 1)
                    pe.transpose(ps16[:, bank, 0:T], tok[:, i, Q_LO:Q_LO + 2 * P], ident16[0:T, 0:T])
                    pe.transpose(ps16[:, bank, PITCH:PITCH + T], tok[:, i, K_HI:K_HI + 2 * P], ident16[0:T, 0:T])
                    pe.transpose(ps16[0:P, bank, 2 * PITCH:2 * PITCH + T], tok[:, i, K_LO:K_LO + P], ident16[0:T, 0:T])\
                        .then_inc(tr_ready, 1)

                def rough_scores(i):
                    pe.wait_ge(max_ready, ONE + NT * h + i)
                    if i == 0:
                        pe.wait_ge(v32_ready, NT * h + LATE_VALUES)
                        pe.wait_ge(qk_pass, NT * (h + 1))
                        pe.wait_ge(qkT_ready, NT * (h + 1))
                        pe.wait_ge(kb_ready, NT * (h + 1))
                    for first, n in GROUPS:
                        last = pe.matmul(ps[:, first // 4, 0:n * T], qkT[:, 0, i, :], qkT[:, 1, first:first + n, 0:T],
                                         start=True, stop=True)
                    last.then_inc(smax_ready, 1)

                def turn_maxima(j):
                    pe.wait_ge(max_ready, ONE + NT * h + CH * (j + 1))
                    pe.wait_ge(qb_ready, ONE + NCK * h + j)
                    for a in range(CH):
                        last = pe.transpose(ps16[0:P + 1, 2, QM + PITCH * a:QM + PITCH * a + T],
                                            tok[:, CH * j + a, Q_HI:MAXC + 1], ident16[0:T, 0:T])
                    last.then_inc(qm_turned, 1)

                def scores(j, u):
                    n = KU * j + u
                    pe.wait_ge(qb_ready, ONE + NCK * h + j + 1)
                    pe.wait_ge(exp_done, ONE + KU * NCK * h + max(n - 1, 0))
                    for a in range(2):
                        into = ps[:, 3 + n % 2, a * CHN:(a + 1) * CHN]
                        pe.matmul(into, qkT[:, 1, 2 * u + a, :], qkT[:, 0, CH * j:CH * (j + 1), 0:T], start=True, stop=False)
                        last = pe.matmul(into, kb[:, 2 * u + a, :], qb[:, CH * j:CH * (j + 1), 0:T], start=False, stop=True)
                    last.then_inc(st_ready, 1)

                def weigh(j, a):
                    pe.wait_ge(plo_ready, ONE + KU * NCK * h + KU * (j + 1))
                    pe.wait_ge(og_ready, ONE + CH * (NCK * h + j))
                    if j == 0:
                        pe.wait_ge(vt_ready, NT * (h + 1))
                    base = a * (2 * P + 1)
                    for t in range(NT):
                        both = [(pT_hi, 0), (pT_lo, P)]
                        for part, first in both if t < NT - 1 else both[::-1]:
                            last = pe.matmul(ps[:, AV, base + first:base + 2 * P + 1], part[:, j % 2, t, a, :],
                                             vt[:, t, first:2 * P + 1], start=(t == 0 and part is pT_hi),
                                             stop=(t == NT - 1 and part is pT_hi))
                    if a == CH - 1:
                        last.then_inc(av_ready, 1)

                def turn_outputs(j):
                    pe.wait_ge(o32_ready, NCK * h + j + 1)
                    for a in range(CH):
                        last = pe.transpose(ps[:, AV, OT + a * T:OT + (a + 1) * T], flat(o32[:, a, :, :]), ident[0:T, 0:T])
                    last.then_inc(ot_ready, 1)

                pe.wait_ge(w_split, SPLIT * n_chunks * h + SPLIT * KD)
                for what, j, n in head_order():
                    if what == "project" and n < NT:
                        project(n)
                    if what == "values":
                        values(n)
                    if what == "turn":
                        turn(n)
                    if what == "rough":
                        rough_scores(n)
                    if what == "turn maxima":
                        turn_maxima(j)
                    if what == "scores":
                        scores(j, n)
                    if what == "weigh":
                        weigh(j, n)
                    if what == "turn outputs":
                        turn_outputs(j)
                    if what == "output":
                        output(h, j, n)

            for what, n in tail_order():
                if what == "output":
                    output(H, 3 + n // (2 * CH), n % (2 * CH))
                if what == "turn":
                    pe.wait_ge(y_ready, n + 1)
                    if n >= 2:
                        pe.wait_ge(lo_ready, 2 * NT + n - 1)
                    for k in range(KD):
                        last = pe.transpose(ps[:, 2 * (n % 2) + k // 4, (k % 4) * PITCH:(k % 4) * PITCH + T],
                                            acc[:, n, k * 128:(k + 1) * 128], ident[0:T, 0:T])
                    last.then_inc(turned, 1)
                if what == "hidden":
                    first, tiles, f = hidden()[n]
                    pe.wait_ge(mlp_split, SPLIT * KD)
                    pe.wait_ge(acc_added, ONE + PER_HEAD * H + LATE)
                    pe.wait_ge(lo_ready, 2 * NT + first + tiles)
                    if n >= 4:
                        pe.wait_ge(h_hi2_ready, n - 3)
                    for k in range(KD):
                        for w_part, x_parts in ((w1_hi, (xT_hi, xT_lo)), (w1_lo, (xT_hi,))):
                            for x_part in x_parts:
                                last = pe.matmul(ps[:, 4 + n % 4, 0:tiles * T], w_part[:, k, f * 128:(f + 1) * 128],
                                                 x_part[:, k, first:first + tiles, 0:T],
                                                 start=(k == 0 and w_part is w1_hi and x_part is xT_hi),
                                                 stop=(k == KD - 1 and w_part is w1_lo))
                    last.then_inc(hs_ready, 1)
            pe.wait_ge(att_pads, 14)
            pe.wait_ge(mlp_split, SPLIT * (KD + F // 128))
            for t in range(NT):
                pe.wait_ge(h_lo2_ready, min(4 * (t // 4) + 4, len(hidden())))
                if t >= 2:
                    pe.wait_ge(var_ready, 3 * NT + t - 1)
                for k in range(F // 128):
                    for h_part, w_parts in ((hT_hi, (w2_hi, w2_lo)), (hT_lo, (w2_hi,))):
                        for w_part in w_parts:
                            for half in range(2):
                                last = pe.matmul(ps[:, 2 * (t % 2) + half, :], h_part[:, k, t, :],
                                                 w_part[:, k, half * HALF:(half + 1) * HALF],
                                                 start=(k == 0 and h_part is hT_hi and w_part is w2_hi),
                                                 stop=(k == F // 128 - 1 and h_part is hT_lo))
                last.then_inc(z_ready, 1)


def constants():
    import numpy as np

    kept = np.zeros((128, C_KEPT), np.float32)
    kept[:, C_ID:C_ID + 128] = np.eye(128)
    kept[:, C_REV:C_REV + EX] = np.arange(EX, 0, -1)
    kept[:, C_LNP] = np.log(SP_)
    c = np.zeros((128, CCOLS), np.float32)
    c[:, C_IOTA:C_IOTA + NT * PITCH] = np.arange(NT * PITCH)
    c[:, C_CHUNK:C_CHUNK + NCH] = np.arange(NCH).reshape(NCH // CPR, CPR).T.reshape(-1)
    c[:, C_SELF:C_SELF + NT] = np.arange(128)[:, None] + T * np.arange(NT)
    c[:, C_LOW] = T * np.arange(128)
    c[:, C_UPPER:C_UPPER + NT] = np.arange(128)[:, None] < np.arange(NT)
    c[:, C_ID10:] = np.eye(128)[:, 0:NCH // CPR]
    half = NROT // 2
    inv = np.float32(10000.0) ** (-np.arange(half, dtype=np.float32) / np.float32(half))
    angle = np.arange(N, dtype=np.float32)[:, None] * inv[None, :].astype(np.float32)
    cos, sin = np.cos(angle), np.sin(angle)
    rope = np.concatenate([cos, cos, -sin, sin], -1).astype(np.float32)
    return kept, c, rope.reshape(NT, T, 2 * NROT).transpose(1, 0, 2)


def kernel(**inputs):
    import numpy as np
    import concourse.bacc as bacc
    from concourse.bass_utils import run_bass_kernel_spmd

    def slabs(w):
        return np.ascontiguousarray(w.reshape(-1, 128, w.shape[-1]).transpose(1, 0, 2))

    nc = bacc.Bacc("TRN2", target_bir_lowering=False, num_devices=1)
    arrays, args = {}, []

    def give(name, a):
        a = np.ascontiguousarray(a)
        arrays[name] = a
        args.append(nc.dram_tensor(name, a.shape, mybir.dt.from_np(a.dtype), kind="ExternalInput").ap())

    give("x", inputs["x"])
    give("src", inputs["src"].reshape(NCH, T).T)
    give("dst", inputs["dst"].reshape(NCH, T).T)
    give("dst_rows", inputs["dst"].reshape(NCH // CPR, CPR, T))
    give("wg", slabs(inputs["L0_gnn_W"].T))
    give("bg", inputs["L0_gnn_b"])
    sel = np.concatenate([inputs["L0_ffn_Wsel_v"].reshape(H * EX, D), inputs["L0_ffn_Wsel_o"].reshape(H * EX, D)])
    give("wsel", slabs(sel.T))
    wv = inputs["L0_ffn_Wv"].transpose(0, 2, 1, 3).reshape(H, D, EX * P)
    qkv = np.concatenate([inputs["L0_ffn_Wq"], inputs["L0_ffn_Wk"], wv], -1)
    give("wqkv", qkv.reshape(H, KD, 128, WQKV).transpose(0, 2, 1, 3))
    give("wo", inputs["L0_ffn_Wo"].reshape(H, PAIRS, 128, D).transpose(0, 2, 1, 3))
    give("w1", slabs(inputs["L0_ffn_W1"]))
    give("b1", inputs["L0_ffn_b1"].reshape(F // 128, 128).T)
    give("w2", slabs(inputs["L0_ffn_W2"]))
    give("rowvecs", np.stack([inputs["L0_ffn_ln1_g"], inputs["L0_ffn_ln1_b"], inputs["L0_ffn_b2"],
                              inputs["L0_ffn_ln2_g"], inputs["L0_ffn_ln2_b"]]))
    kept, graph, rope = constants()
    give("ctab", kept)
    give("gtab", graph)
    give("rtab", rope)
    args.append(nc.dram_tensor("out", [N, D], F32, kind="ExternalOutput").ap())
    build(nc, *args)
    r = run_bass_kernel_spmd(nc, [arrays], core_ids=[0])
    return r.results[0]["out"]
```
